# Optimizing a Trainium2 kernel written in Bass

```python
import numpy as np
import jax
import jax.numpy as jnp

def _softmax(x, axis=-1):
    return jax.nn.softmax(x, axis=axis)

def _gelu(x):
    return jax.nn.gelu(x, approximate=True)

def _silu(x):
    return jax.nn.silu(x)

def _sigmoid(x):
    return jax.nn.sigmoid(x)

def _layernorm(x, axis=-1, eps=1e-05):
    m = jnp.mean(x, axis=axis, keepdims=True)
    v = jnp.var(x, axis=axis, keepdims=True)
    return (x - m) / jnp.sqrt(v + eps)

def _scatter_add(tgt, idx, src, axis=0):
    return tgt.at[idx].add(src)

def _segment_sum(src, seg, n):
    return jax.ops.segment_sum(src, seg, n)
kernel_name = 'mk_decoder_preln_d2_seqx_r8_7bdd04'

def setup_inputs(seed: int=0):
    np.random.seed(seed)
    _w = jnp.asarray

    def _rec_inputs():
        import jax
        import jax.numpy as jnp
        _rk = jax.random.key(seed)
        x = 7.22e-05 + 1 * jax.random.normal(jax.random.fold_in(_rk, 1), (2, 512, 128), jnp.float32)
        _lenS = 512 - jax.random.randint(jax.random.fold_in(_rk, 7), (2,), 0, max(1, 512 // 4) + 1, jnp.int32)
        _lenS2 = 154 - jax.random.randint(jax.random.fold_in(_rk, 8), (2,), 0, max(1, 154 // 4) + 1, jnp.int32)
        _ctx_1024P = jax.random.normal(jax.random.fold_in(_rk, 11), (2, 16, 128), jnp.float32)
        _ctx_1024c = jax.random.dirichlet(jax.random.fold_in(_rk, 511), 0.3 * jnp.ones((16,), jnp.float32), (2, 154))
        _ctx_1024t = jnp.einsum('bsk,bkd->bsd', _ctx_1024c, _ctx_1024P)
        _ctx_1024t = _ctx_1024t * jax.lax.rsqrt(jnp.mean(jnp.square(_ctx_1024t)) + 1e-12) * 0.953939
        ctx_1024 = 2.81802e-05 + 1.00001 * (_ctx_1024t + 0.3 * jax.random.normal(jax.random.fold_in(_rk, 611), (2, 154, 128), jnp.float32))
        return (x, ctx_1024)
    x, ctx_1024 = _rec_inputs()

    def _L0_attn_setup():
        import math
        import jax, jax.numpy as jnp
        import numpy as np
        EPS = 1e-06
        NEG = -1000000000.0

        def rms_norm(x):
            return x * jax.lax.rsqrt(jnp.mean(x * x, axis=-1, keepdims=True) + EPS)

        def apply_rope(x, cos, sin):
            d2 = x.shape[-1] // 2
            x1, x2 = (x[..., :d2], x[..., d2:])
            c = cos[None, None, :, :]
            s = sin[None, None, :, :]
            return jnp.concatenate([x1 * c - x2 * s, x2 * c + x1 * s], axis=-1)
        key = jax.random.key(seed)
        k1, k2, k3 = jax.random.split(key, 3)
        B, T, C = (2, 256, 128)
        H, D = (16, 64)
        dim_inner = H * D
        x = jax.random.normal(k1, (B, T, C), dtype=jnp.float32)
        w_qkv = jax.random.normal(k2, (3 * dim_inner, C), dtype=jnp.float32) * (1.0 / math.sqrt(C))
        w_out = jax.random.normal(k3, (C, dim_inner), dtype=jnp.float32) * (1.0 / math.sqrt(dim_inner))
        return {'x': x, 'w_qkv': w_qkv, 'w_out': w_out}
    _L0_attn_all = _L0_attn_setup()
    _L0_attn_in = {k: v for k, v in _L0_attn_all.items() if k in ('w_qkv', 'w_out')}
    del _L0_attn_all

    def _L0_xattn_setup():
        import jax, jax.numpy as jnp
        import numpy as np
        B, T, S, D = (4, 256, 512, 128)
        TOP_K = 32

        def _read(query, mem_state, top_k, Wq, bq, Wk, bk, Wv, bv, Wo, bo):
            b, t, d = query.shape
            s = mem_state.shape[1]
            scale = 1.0 / np.sqrt(d)
            q = query @ Wq.T + bq
            k = mem_state @ Wk.T + bk
            v = mem_state @ Wv.T + bv
            scores = jnp.einsum('btd,bsd->bts', q, k) * scale
            if top_k < s:
                vals, idx = jax.lax.top_k(scores, top_k)
                b_ix = jnp.arange(b)[:, None, None]
                t_ix = jnp.arange(t)[None, :, None]
                masked = jnp.full_like(scores, -jnp.inf)
                scores = masked.at[b_ix, t_ix, idx].set(vals)
            attn = jax.nn.softmax(scores, axis=-1)
            ctx = jnp.einsum('bts,bsd->btd', attn, v)
            return ctx @ Wo.T + bo
        key = jax.random.key(seed)
        ks = jax.random.split(key, 12)
        std = 0.02
        inp = {'query': jax.random.normal(ks[0], (B, T, D), dtype=jnp.float32), 'mem_state': jax.random.normal(ks[1], (B, S, D), dtype=jnp.float32), 'top_k': TOP_K, 'Wq': jax.random.normal(ks[2], (D, D), dtype=jnp.float32) * std, 'bq': jnp.zeros((D,), dtype=jnp.float32), 'Wk': jax.random.normal(ks[3], (D, D), dtype=jnp.float32) * std, 'bk': jnp.zeros((D,), dtype=jnp.float32), 'Wv': jax.random.normal(ks[4], (D, D), dtype=jnp.float32) * std, 'bv': jnp.zeros((D,), dtype=jnp.float32), 'Wo': jax.random.normal(ks[5], (D, D), dtype=jnp.float32) * std, 'bo': jnp.zeros((D,), dtype=jnp.float32)}
        return inp
    _L0_xattn_all = _L0_xattn_setup()
    _L0_xattn_in = {k: v for k, v in _L0_xattn_all.items() if k in ('Wq', 'bq', 'Wk', 'bk', 'Wv', 'bv', 'Wo', 'bo')}
    del _L0_xattn_all

    def _L0_ffn_setup():
        import jax, jax.numpy as jnp
        import numpy as np
        BLOCK = 16
        _GRID = jnp.array([0.0, 0.5, 1.0, 1.5, 2.0, 3.0, 4.0, 6.0], dtype=jnp.float32)
        _MID = jnp.array([0.25, 0.75, 1.25, 1.75, 2.5, 3.5, 5.0], dtype=jnp.float32)

        def fp4_quant_dequant(x):
            shape = x.shape
            xb = x.reshape(shape[:-1] + (shape[-1] // BLOCK, BLOCK))
            scale = jnp.max(jnp.abs(xb), axis=-1, keepdims=True) / 6.0
            scale = jnp.maximum(scale, jnp.float32(1e-12))
            xn = xb / scale
            idx = jnp.searchsorted(_MID, jnp.abs(xn))
            q = _GRID[idx] * jnp.sign(xn) * scale
            return q.reshape(shape)

        def fp4_linear(x, w):
            xq = fp4_quant_dequant(x)
            wq = fp4_quant_dequant(w)
            return jnp.einsum('bsk,nk->bsn', xq, wq)
        key = jax.random.key(seed)
        k1, k2, k3, k4 = jax.random.split(key, 4)
        H, I = (128, 352)
        x = jax.random.normal(k1, (4, 512, H), dtype=jnp.float32)
        w_gate = jax.random.normal(k2, (I, H), dtype=jnp.float32) * 0.02
        w_up = jax.random.normal(k3, (I, H), dtype=jnp.float32) * 0.02
        w_down = jax.random.normal(k4, (H, I), dtype=jnp.float32) * 0.02
        return {'x': x, 'w_gate': w_gate, 'w_up': w_up, 'w_down': w_down}
    _L0_ffn_all = _L0_ffn_setup()
    _L0_ffn_in = {k: v for k, v in _L0_ffn_all.items() if k in ('w_gate', 'w_up', 'w_down')}
    del _L0_ffn_all

    def _L1_attn_setup():
        import jax, jax.numpy as jnp
        import numpy as np
        N_LAYER, N_HEAD, D_MODEL, D_FF = (6, 16, 128, 512)
        D_HEAD = D_MODEL // N_HEAD
        M_FEAT = 2 * D_MODEL // N_HEAD
        CHUNK = 128
        LN_EPS = 1e-05
        ATT_EPS = 1e-06
        B, S = (4, 256)

        def _layer_norm(x, g, b):
            mu = x.mean(-1, keepdims=True)
            var = ((x - mu) ** 2).mean(-1, keepdims=True)
            return (x - mu) * jax.lax.rsqrt(var + LN_EPS) * g + b

        def _favor_phi(x, omega):
            x = x * D_HEAD ** (-0.25)
            u = jnp.einsum('bhsd,dm->bhsm', x, omega)
            nrm = 0.5 * jnp.sum(x * x, axis=-1, keepdims=True)
            phi = jnp.concatenate([jnp.exp(u - nrm), jnp.exp(-u - nrm)], axis=-1)
            return phi * M_FEAT ** (-0.5)

        def _causal_linear_attention(Qp, Kp, V):
            b, h, s, m = Qp.shape
            d = V.shape[-1]
            c = s // CHUNK
            Qc = Qp.reshape(b, h, c, CHUNK, m)
            Kc = Kp.reshape(b, h, c, CHUNK, m)
            Vc = V.reshape(b, h, c, CHUNK, d)
            kv = jnp.einsum('bhclm,bhcld->bhcmd', Kc, Vc)
            ksum = Kc.sum(axis=3)
            kv_pre = jnp.cumsum(kv, axis=2) - kv
            ks_pre = jnp.cumsum(ksum, axis=2) - ksum
            scores = jnp.einsum('bhcim,bhcjm->bhcij', Qc, Kc)
            mask = jnp.tril(jnp.ones((CHUNK, CHUNK), bool))
            scores = jnp.where(mask, scores, 0.0)
            num = jnp.einsum('bhcij,bhcjd->bhcid', scores, Vc) + jnp.einsum('bhcim,bhcmd->bhcid', Qc, kv_pre)
            den = scores.sum(-1) + jnp.einsum('bhcim,bhcm->bhci', Qc, ks_pre)
            out = num / (den[..., None] + ATT_EPS)
            return out.reshape(b, h, s, d)

        def _forward(x, Wq, bq, Wk, bk, Wv, bv, Wo, bo, omega, g1, be1, W1, bf1, W2, bf2, g2, be2):
            bsz, slen, _ = x.shape
            out = x
            for l in range(N_LAYER):

                def proj(W, bvec):
                    y = jnp.einsum('bsd,de->bse', out, W) + bvec
                    return y.reshape(bsz, slen, N_HEAD, D_HEAD).transpose(0, 2, 1, 3)
                q = proj(Wq[l], bq[l])
                k = proj(Wk[l], bk[l])
                v = proj(Wv[l], bv[l])
                Qp = _favor_phi(q, omega[l])
                Kp = _favor_phi(k, omega[l])
                a = _causal_linear_attention(Qp, Kp, v)
                a = a.transpose(0, 2, 1, 3).reshape(bsz, slen, D_MODEL)
                a = jnp.einsum('bsd,de->bse', a, Wo[l]) + bo[l]
                h1 = _layer_norm(out + a, g1[l], be1[l])
                y = jax.nn.relu(jnp.einsum('bsd,df->bsf', h1, W1[l]) + bf1[l])
                y = jnp.einsum('bsf,fd->bsd', y, W2[l]) + bf2[l]
                out = _layer_norm(h1 + y, g2[l], be2[l])
            return out
        key = jax.random.key(seed)
        ks = jax.random.split(key, 12)
        s = D_MODEL ** (-0.5)
        f32 = jnp.float32
        return {'x': jax.random.normal(ks[0], (B, S, D_MODEL), f32), 'Wq': jax.random.normal(ks[1], (N_LAYER, D_MODEL, D_MODEL), f32) * s, 'bq': jnp.zeros((N_LAYER, D_MODEL), f32), 'Wk': jax.random.normal(ks[2], (N_LAYER, D_MODEL, D_MODEL), f32) * s, 'bk': jnp.zeros((N_LAYER, D_MODEL), f32), 'Wv': jax.random.normal(ks[3], (N_LAYER, D_MODEL, D_MODEL), f32) * s, 'bv': jnp.zeros((N_LAYER, D_MODEL), f32), 'Wo': jax.random.normal(ks[4], (N_LAYER, D_MODEL, D_MODEL), f32) * s, 'bo': jnp.zeros((N_LAYER, D_MODEL), f32), 'omega': jax.random.normal(ks[5], (N_LAYER, D_HEAD, M_FEAT // 2), f32), 'g1': jnp.ones((N_LAYER, D_MODEL), f32), 'be1': jnp.zeros((N_LAYER, D_MODEL), f32), 'W1': jax.random.normal(ks[6], (N_LAYER, D_MODEL, D_FF), f32) * s, 'bf1': jnp.zeros((N_LAYER, D_FF), f32), 'W2': jax.random.normal(ks[7], (N_LAYER, D_FF, D_MODEL), f32) * D_FF ** (-0.5), 'bf2': jnp.zeros((N_LAYER, D_MODEL), f32), 'g2': jnp.ones((N_LAYER, D_MODEL), f32), 'be2': jnp.zeros((N_LAYER, D_MODEL), f32)}
    _L1_attn_all = _L1_attn_setup()
    _L1_attn_in = {k: v for k, v in _L1_attn_all.items() if k in ('Wq', 'bq', 'Wk', 'bk', 'Wv', 'bv', 'Wo', 'bo', 'omega', 'g1', 'be1', 'W1', 'bf1', 'W2', 'bf2', 'g2', 'be2')}
    del _L1_attn_all

    def _L1_xattn_setup():
        import jax, jax.numpy as jnp
        import numpy as np
        B, L, D, H = (4, 256, 128, 16)
        DH = D // H
        SCALE = 1.0 / float(np.sqrt(DH))

        def _split_heads(x):
            b, l, _ = x.shape
            return x.reshape(b, l, H, DH).transpose(0, 2, 1, 3)
        key = jax.random.key(seed)
        ks = jax.random.split(key, 11)
        s = 0.02
        return {'q': jax.random.normal(ks[0], (B, L, D), jnp.float32), 'k': jax.random.normal(ks[1], (B, L, D), jnp.float32), 'v': jax.random.normal(ks[2], (B, L, D), jnp.float32), 'Wq': jax.random.normal(ks[3], (D, D), jnp.float32) * s, 'bq': jnp.zeros((D,), jnp.float32), 'Wk': jax.random.normal(ks[4], (D, D), jnp.float32) * s, 'bk': jnp.zeros((D,), jnp.float32), 'Wv': jax.random.normal(ks[5], (D, D), jnp.float32) * s, 'bv': jnp.zeros((D,), jnp.float32), 'Wo': jax.random.normal(ks[6], (D, D), jnp.float32) * s, 'bo': jnp.zeros((D,), jnp.float32)}
    _L1_xattn_all = _L1_xattn_setup()
    _L1_xattn_in = {k: v for k, v in _L1_xattn_all.items() if k in ('Wq', 'bq', 'Wk', 'bk', 'Wv', 'bv', 'Wo', 'bo')}
    del _L1_xattn_all

    def _L1_ffn_setup():
        import jax, jax.numpy as jnp
        import numpy as np
        DIM = 128
        DEPTH = 6
        HEADS = 16
        DIM_HEAD = 64
        WINDOW = 32
        INNER = HEADS * DIM_HEAD
        DIM_INNER = int(DIM * 4 * 2 / 3)
        QK_SCALE = 8.0

        def shift_tokens(t):
            a, s = jnp.split(t, 2, -1)
            s = jnp.pad(s, ((0, 0), (1, 0), (0, 0)))[:, :-1]
            return jnp.concatenate([a, s], -1)

        def l2norm(t):
            return t / jnp.maximum(jnp.linalg.norm(t, axis=-1, keepdims=True), 1e-12)

        def rotate_half(x):
            x1, x2 = jnp.split(x, 2, -1)
            return jnp.concatenate([-x2, x1], -1)

        def rotary_tables(n):
            half = jnp.arange(0, DIM_HEAD, 2, dtype=jnp.float32)
            inv_freq = 1.0 / 10000.0 ** (half / DIM_HEAD)
            t = jnp.arange(n, dtype=jnp.float32)
            freqs = t[:, None] * inv_freq[None, :]
            freqs = jnp.concatenate([freqs, freqs], -1)
            base_scale = (half + 0.4 * DIM_HEAD) / (1.4 * DIM_HEAD)
            power = (t - n // 2) / (WINDOW // 2)
            scale = base_scale[None, :] ** power[:, None]
            scale = jnp.concatenate([scale, scale], -1)
            return (freqs, scale)

        def local_attention(q, k, v):
            b, h, n, d = q.shape
            w = WINDOW
            nw = n // w
            bq = q.reshape(b, h, nw, w, d)
            bk = k.reshape(b, h, nw, w, d)
            bv = v.reshape(b, h, nw, w, d)

            def look(t):
                p = jnp.pad(t, ((0, 0), (0, 0), (1, 0), (0, 0), (0, 0)))
                return jnp.concatenate([p[:, :, :nw], p[:, :, 1:]], axis=3)
            bk2, bv2 = (look(bk), look(bv))
            seq = jnp.arange(n).reshape(nw, w)
            seq_p = jnp.pad(seq, ((1, 0), (0, 0)), constant_values=-1)
            jt = jnp.concatenate([seq_p[:nw], seq_p[1:]], axis=1)
            it = seq[:, :, None]
            jb = jt[:, None, :]
            mask = (it < jb) | (it > jb + w) | (jb == -1)
            sim = jnp.einsum('bhwie,bhwje->bhwij', bq, bk2) * QK_SCALE
            sim = jnp.where(mask, -jnp.finfo(sim.dtype).max, sim)
            attn = jax.nn.softmax(sim, -1)
            out = jnp.einsum('bhwij,bhwje->bhwie', attn, bv2)
            return out.reshape(b, h, n, d)

        def attn_layer(x, Wqkv, qs, ksc, Wo):
            b, n, _ = x.shape
            qkv = x @ Wqkv
            q, k, v = jnp.split(qkv, 3, -1)
            sh = lambda t: t.reshape(b, n, HEADS, DIM_HEAD).transpose(0, 2, 1, 3)
            q, k, v = (sh(q), sh(k), sh(v))
            q = l2norm(q) * qs
            k = l2norm(k) * ksc
            freqs, scale = rotary_tables(n)
            cos, sin = (jnp.cos(freqs), jnp.sin(freqs))
            q = q * cos * scale + rotate_half(q) * sin * scale
            inv = 1.0 / scale
            k = k * cos * inv + rotate_half(k) * sin * inv
            out = local_attention(q, k, v)
            out = out.transpose(0, 2, 1, 3).reshape(b, n, INNER)
            return out @ Wo

        def ffn_layer(x, g, bln, W1, b1, W2, b2):
            mu = x.mean(-1, keepdims=True)
            var = ((x - mu) ** 2).mean(-1, keepdims=True)
            xn = (x - mu) / jnp.sqrt(var + 1e-05) * g + bln
            hg = xn @ W1 + b1
            a, gate = jnp.split(hg, 2, -1)
            return a * jax.nn.gelu(gate, approximate=False) @ W2 + b2
        key = jax.random.key(seed)
        ks = jax.random.split(key, 8)
        B, N = (2, 256)
        init = lambda k, shape: jax.random.normal(k, shape, jnp.float32) * 0.02
        return {'x': jax.random.normal(ks[0], (B, N, DIM), jnp.float32), 'Wqkv': init(ks[1], (DEPTH, DIM, 3 * INNER)), 'q_scale': jnp.ones((DEPTH, DIM_HEAD), jnp.float32), 'k_scale': jnp.ones((DEPTH, DIM_HEAD), jnp.float32), 'Wo': init(ks[2], (DEPTH, INNER, DIM)), 'ln_g': jnp.ones((DEPTH, DIM), jnp.float32), 'ln_b': jnp.zeros((DEPTH, DIM), jnp.float32), 'W1': init(ks[3], (DEPTH, DIM, 2 * DIM_INNER)), 'b1': jnp.zeros((DEPTH, 2 * DIM_INNER), jnp.float32), 'W2': init(ks[4], (DEPTH, DIM_INNER, DIM)), 'b2': jnp.zeros((DEPTH, DIM), jnp.float32)}
    _L1_ffn_all = _L1_ffn_setup()
    _L1_ffn_in = {k: v for k, v in _L1_ffn_all.items() if k in ('Wqkv', 'q_scale', 'k_scale', 'Wo', 'ln_g', 'ln_b', 'W1', 'b1', 'W2', 'b2')}
    del _L1_ffn_all
    return {'x': x, 'ctx_1024': ctx_1024, 'L0_attn_w_qkv': _L0_attn_in['w_qkv'], 'L0_attn_w_out': _L0_attn_in['w_out'], 'L0_xattn_Wq': _L0_xattn_in['Wq'], 'L0_xattn_bq': _L0_xattn_in['bq'], 'L0_xattn_Wk': _L0_xattn_in['Wk'], 'L0_xattn_bk': _L0_xattn_in['bk'], 'L0_xattn_Wv': _L0_xattn_in['Wv'], 'L0_xattn_bv': _L0_xattn_in['bv'], 'L0_xattn_Wo': _L0_xattn_in['Wo'], 'L0_xattn_bo': _L0_xattn_in['bo'], 'L0_ffn_w_gate': _L0_ffn_in['w_gate'], 'L0_ffn_w_up': _L0_ffn_in['w_up'], 'L0_ffn_w_down': _L0_ffn_in['w_down'], 'L1_attn_Wq': _L1_attn_in['Wq'], 'L1_attn_bq': _L1_attn_in['bq'], 'L1_attn_Wk': _L1_attn_in['Wk'], 'L1_attn_bk': _L1_attn_in['bk'], 'L1_attn_Wv': _L1_attn_in['Wv'], 'L1_attn_bv': _L1_attn_in['bv'], 'L1_attn_Wo': _L1_attn_in['Wo'], 'L1_attn_bo': _L1_attn_in['bo'], 'L1_attn_omega': _L1_attn_in['omega'], 'L1_attn_g1': _L1_attn_in['g1'], 'L1_attn_be1': _L1_attn_in['be1'], 'L1_attn_W1': _L1_attn_in['W1'], 'L1_attn_bf1': _L1_attn_in['bf1'], 'L1_attn_W2': _L1_attn_in['W2'], 'L1_attn_bf2': _L1_attn_in['bf2'], 'L1_attn_g2': _L1_attn_in['g2'], 'L1_attn_be2': _L1_attn_in['be2'], 'L1_xattn_Wq': _L1_xattn_in['Wq'], 'L1_xattn_bq': _L1_xattn_in['bq'], 'L1_xattn_Wk': _L1_xattn_in['Wk'], 'L1_xattn_bk': _L1_xattn_in['bk'], 'L1_xattn_Wv': _L1_xattn_in['Wv'], 'L1_xattn_bv': _L1_xattn_in['bv'], 'L1_xattn_Wo': _L1_xattn_in['Wo'], 'L1_xattn_bo': _L1_xattn_in['bo'], 'L1_ffn_Wqkv': _L1_ffn_in['Wqkv'], 'L1_ffn_q_scale': _L1_ffn_in['q_scale'], 'L1_ffn_k_scale': _L1_ffn_in['k_scale'], 'L1_ffn_Wo': _L1_ffn_in['Wo'], 'L1_ffn_ln_g': _L1_ffn_in['ln_g'], 'L1_ffn_ln_b': _L1_ffn_in['ln_b'], 'L1_ffn_W1': _L1_ffn_in['W1'], 'L1_ffn_b1': _L1_ffn_in['b1'], 'L1_ffn_W2': _L1_ffn_in['W2'], 'L1_ffn_b2': _L1_ffn_in['b2']}

def reference(x, ctx_1024, L0_attn_w_qkv, L0_attn_w_out, L0_xattn_Wq, L0_xattn_bq, L0_xattn_Wk, L0_xattn_bk, L0_xattn_Wv, L0_xattn_bv, L0_xattn_Wo, L0_xattn_bo, L0_ffn_w_gate, L0_ffn_w_up, L0_ffn_w_down, L1_attn_Wq, L1_attn_bq, L1_attn_Wk, L1_attn_bk, L1_attn_Wv, L1_attn_bv, L1_attn_Wo, L1_attn_bo, L1_attn_omega, L1_attn_g1, L1_attn_be1, L1_attn_W1, L1_attn_bf1, L1_attn_W2, L1_attn_bf2, L1_attn_g2, L1_attn_be2, L1_xattn_Wq, L1_xattn_bq, L1_xattn_Wk, L1_xattn_bk, L1_xattn_Wv, L1_xattn_bv, L1_xattn_Wo, L1_xattn_bo, L1_ffn_Wqkv, L1_ffn_q_scale, L1_ffn_k_scale, L1_ffn_Wo, L1_ffn_ln_g, L1_ffn_ln_b, L1_ffn_W1, L1_ffn_b1, L1_ffn_W2, L1_ffn_b2):
    import jax
    import jax.numpy as jnp

    def _L0_attn_ref(x, w_qkv, w_out):
        import math
        import jax, jax.numpy as jnp
        import numpy as np
        EPS = 1e-06
        NEG = -1000000000.0

        def rms_norm(x):
            return x * jax.lax.rsqrt(jnp.mean(x * x, axis=-1, keepdims=True) + EPS)

        def apply_rope(x, cos, sin):
            d2 = x.shape[-1] // 2
            x1, x2 = (x[..., :d2], x[..., d2:])
            c = cos[None, None, :, :]
            s = sin[None, None, :, :]
            return jnp.concatenate([x1 * c - x2 * s, x2 * c + x1 * s], axis=-1)
        H, D, window_size = (16, 64, 32)
        B, T, C = x.shape
        xn = rms_norm(x)
        qkv = xn @ w_qkv.T
        q, k, v = jnp.split(qkv, 3, axis=-1)
        q = q.reshape(B, T, H, D).transpose(0, 2, 1, 3)
        k = k.reshape(B, T, H, D).transpose(0, 2, 1, 3)
        v = v.reshape(B, T, H, D).transpose(0, 2, 1, 3)
        inv_freq = 1.0 / 10000.0 ** (jnp.arange(0, D, 2, dtype=jnp.float32) / D)
        freqs = jnp.outer(jnp.arange(T, dtype=jnp.float32), inv_freq)
        cos, sin = (jnp.cos(freqs), jnp.sin(freqs))
        q = apply_rope(q, cos, sin)
        k = apply_rope(k, cos, sin)
        scale = 1.0 / math.sqrt(D)
        attn = jnp.einsum('bhqd,bhkd->bhqk', q, k) * scale
        q_pos = jnp.arange(T)[:, None]
        k_pos = jnp.arange(T)[None, :]
        mask = (q_pos >= k_pos) & (q_pos - k_pos <= window_size)
        attn = jnp.where(mask[None, None], attn, NEG)
        attn = jax.nn.softmax(attn.astype(jnp.float32), axis=-1).astype(q.dtype)
        out = jnp.einsum('bhqk,bhkd->bhqd', attn, v)
        out = out.transpose(0, 2, 1, 3).reshape(B, T, H * D)
        return out @ w_out.T

    def _L0_xattn_ref(query, mem_state, top_k, Wq, bq, Wk, bk, Wv, bv, Wo, bo):
        import jax, jax.numpy as jnp
        import numpy as np
        B, T, S, D = (4, 256, 512, 128)
        TOP_K = 32

        def _read(query, mem_state, top_k, Wq, bq, Wk, bk, Wv, bv, Wo, bo):
            b, t, d = query.shape
            s = mem_state.shape[1]
            scale = 1.0 / np.sqrt(d)
            q = query @ Wq.T + bq
            k = mem_state @ Wk.T + bk
            v = mem_state @ Wv.T + bv
            scores = jnp.einsum('btd,bsd->bts', q, k) * scale
            if top_k < s:
                vals, idx = jax.lax.top_k(scores, top_k)
                b_ix = jnp.arange(b)[:, None, None]
                t_ix = jnp.arange(t)[None, :, None]
                masked = jnp.full_like(scores, -jnp.inf)
                scores = masked.at[b_ix, t_ix, idx].set(vals)
            attn = jax.nn.softmax(scores, axis=-1)
            ctx = jnp.einsum('bts,bsd->btd', attn, v)
            return ctx @ Wo.T + bo
        return _read(query, mem_state, top_k, Wq, bq, Wk, bk, Wv, bv, Wo, bo)

    def _L0_ffn_ref(x, w_gate, w_up, w_down):
        import jax, jax.numpy as jnp
        import numpy as np
        BLOCK = 16
        _GRID = jnp.array([0.0, 0.5, 1.0, 1.5, 2.0, 3.0, 4.0, 6.0], dtype=jnp.float32)
        _MID = jnp.array([0.25, 0.75, 1.25, 1.75, 2.5, 3.5, 5.0], dtype=jnp.float32)

        def fp4_quant_dequant(x):
            shape = x.shape
            xb = x.reshape(shape[:-1] + (shape[-1] // BLOCK, BLOCK))
            scale = jnp.max(jnp.abs(xb), axis=-1, keepdims=True) / 6.0
            scale = jnp.maximum(scale, jnp.float32(1e-12))
            xn = xb / scale
            idx = jnp.searchsorted(_MID, jnp.abs(xn))
            q = _GRID[idx] * jnp.sign(xn) * scale
            return q.reshape(shape)

        def fp4_linear(x, w):
            xq = fp4_quant_dequant(x)
            wq = fp4_quant_dequant(w)
            return jnp.einsum('bsk,nk->bsn', xq, wq)
        gate = fp4_linear(x, w_gate)
        y = fp4_linear(x, w_up)
        h = jax.nn.silu(gate) * y
        return fp4_linear(h, w_down)

    def _L1_attn_ref(x, Wq, bq, Wk, bk, Wv, bv, Wo, bo, omega, g1, be1, W1, bf1, W2, bf2, g2, be2):
        import jax, jax.numpy as jnp
        import numpy as np
        N_LAYER, N_HEAD, D_MODEL, D_FF = (6, 16, 128, 512)
        D_HEAD = D_MODEL // N_HEAD
        M_FEAT = 2 * D_MODEL // N_HEAD
        CHUNK = 128
        LN_EPS = 1e-05
        ATT_EPS = 1e-06
        B, S = (4, 256)

        def _layer_norm(x, g, b):
            mu = x.mean(-1, keepdims=True)
            var = ((x - mu) ** 2).mean(-1, keepdims=True)
            return (x - mu) * jax.lax.rsqrt(var + LN_EPS) * g + b

        def _favor_phi(x, omega):
            x = x * D_HEAD ** (-0.25)
            u = jnp.einsum('bhsd,dm->bhsm', x, omega)
            nrm = 0.5 * jnp.sum(x * x, axis=-1, keepdims=True)
            phi = jnp.concatenate([jnp.exp(u - nrm), jnp.exp(-u - nrm)], axis=-1)
            return phi * M_FEAT ** (-0.5)

        def _causal_linear_attention(Qp, Kp, V):
            b, h, s, m = Qp.shape
            d = V.shape[-1]
            c = s // CHUNK
            Qc = Qp.reshape(b, h, c, CHUNK, m)
            Kc = Kp.reshape(b, h, c, CHUNK, m)
            Vc = V.reshape(b, h, c, CHUNK, d)
            kv = jnp.einsum('bhclm,bhcld->bhcmd', Kc, Vc)
            ksum = Kc.sum(axis=3)
            kv_pre = jnp.cumsum(kv, axis=2) - kv
            ks_pre = jnp.cumsum(ksum, axis=2) - ksum
            scores = jnp.einsum('bhcim,bhcjm->bhcij', Qc, Kc)
            mask = jnp.tril(jnp.ones((CHUNK, CHUNK), bool))
            scores = jnp.where(mask, scores, 0.0)
            num = jnp.einsum('bhcij,bhcjd->bhcid', scores, Vc) + jnp.einsum('bhcim,bhcmd->bhcid', Qc, kv_pre)
            den = scores.sum(-1) + jnp.einsum('bhcim,bhcm->bhci', Qc, ks_pre)
            out = num / (den[..., None] + ATT_EPS)
            return out.reshape(b, h, s, d)

        def _forward(x, Wq, bq, Wk, bk, Wv, bv, Wo, bo, omega, g1, be1, W1, bf1, W2, bf2, g2, be2):
            bsz, slen, _ = x.shape
            out = x
            for l in range(N_LAYER):

                def proj(W, bvec):
                    y = jnp.einsum('bsd,de->bse', out, W) + bvec
                    return y.reshape(bsz, slen, N_HEAD, D_HEAD).transpose(0, 2, 1, 3)
                q = proj(Wq[l], bq[l])
                k = proj(Wk[l], bk[l])
                v = proj(Wv[l], bv[l])
                Qp = _favor_phi(q, omega[l])
                Kp = _favor_phi(k, omega[l])
                a = _causal_linear_attention(Qp, Kp, v)
                a = a.transpose(0, 2, 1, 3).reshape(bsz, slen, D_MODEL)
                a = jnp.einsum('bsd,de->bse', a, Wo[l]) + bo[l]
                h1 = _layer_norm(out + a, g1[l], be1[l])
                y = jax.nn.relu(jnp.einsum('bsd,df->bsf', h1, W1[l]) + bf1[l])
                y = jnp.einsum('bsf,fd->bsd', y, W2[l]) + bf2[l]
                out = _layer_norm(h1 + y, g2[l], be2[l])
            return out
        return _forward(x, Wq, bq, Wk, bk, Wv, bv, Wo, bo, omega, g1, be1, W1, bf1, W2, bf2, g2, be2)

    def _L1_xattn_ref(q, k, v, Wq, bq, Wk, bk, Wv, bv, Wo, bo):
        import jax, jax.numpy as jnp
        import numpy as np
        B, L, D, H = (4, 256, 128, 16)
        DH = D // H
        SCALE = 1.0 / float(np.sqrt(DH))

        def _split_heads(x):
            b, l, _ = x.shape
            return x.reshape(b, l, H, DH).transpose(0, 2, 1, 3)
        qh = _split_heads(q @ Wq.T + bq)
        kh = _split_heads(k @ Wk.T + bk)
        vh = _split_heads(v @ Wv.T + bv)
        scores = jnp.einsum('bhqd,bhkd->bhqk', qh, kh) * SCALE
        attn = jax.nn.softmax(scores, axis=-1)
        out = jnp.einsum('bhqk,bhkd->bhqd', attn, vh)
        out = out.transpose(0, 2, 1, 3).reshape(q.shape[0], q.shape[1], D)
        return out @ Wo.T + bo

    def _L1_ffn_ref(x, Wqkv, q_scale, k_scale, Wo, ln_g, ln_b, W1, b1, W2, b2):
        import jax, jax.numpy as jnp
        import numpy as np
        DIM = 128
        DEPTH = 6
        HEADS = 16
        DIM_HEAD = 64
        WINDOW = 32
        INNER = HEADS * DIM_HEAD
        DIM_INNER = int(DIM * 4 * 2 / 3)
        QK_SCALE = 8.0

        def shift_tokens(t):
            a, s = jnp.split(t, 2, -1)
            s = jnp.pad(s, ((0, 0), (1, 0), (0, 0)))[:, :-1]
            return jnp.concatenate([a, s], -1)

        def l2norm(t):
            return t / jnp.maximum(jnp.linalg.norm(t, axis=-1, keepdims=True), 1e-12)

        def rotate_half(x):
            x1, x2 = jnp.split(x, 2, -1)
            return jnp.concatenate([-x2, x1], -1)

        def rotary_tables(n):
            half = jnp.arange(0, DIM_HEAD, 2, dtype=jnp.float32)
            inv_freq = 1.0 / 10000.0 ** (half / DIM_HEAD)
            t = jnp.arange(n, dtype=jnp.float32)
            freqs = t[:, None] * inv_freq[None, :]
            freqs = jnp.concatenate([freqs, freqs], -1)
            base_scale = (half + 0.4 * DIM_HEAD) / (1.4 * DIM_HEAD)
            power = (t - n // 2) / (WINDOW // 2)
            scale = base_scale[None, :] ** power[:, None]
            scale = jnp.concatenate([scale, scale], -1)
            return (freqs, scale)

        def local_attention(q, k, v):
            b, h, n, d = q.shape
            w = WINDOW
            nw = n // w
            bq = q.reshape(b, h, nw, w, d)
            bk = k.reshape(b, h, nw, w, d)
            bv = v.reshape(b, h, nw, w, d)

            def look(t):
                p = jnp.pad(t, ((0, 0), (0, 0), (1, 0), (0, 0), (0, 0)))
                return jnp.concatenate([p[:, :, :nw], p[:, :, 1:]], axis=3)
            bk2, bv2 = (look(bk), look(bv))
            seq = jnp.arange(n).reshape(nw, w)
            seq_p = jnp.pad(seq, ((1, 0), (0, 0)), constant_values=-1)
            jt = jnp.concatenate([seq_p[:nw], seq_p[1:]], axis=1)
            it = seq[:, :, None]
            jb = jt[:, None, :]
            mask = (it < jb) | (it > jb + w) | (jb == -1)
            sim = jnp.einsum('bhwie,bhwje->bhwij', bq, bk2) * QK_SCALE
            sim = jnp.where(mask, -jnp.finfo(sim.dtype).max, sim)
            attn = jax.nn.softmax(sim, -1)
            out = jnp.einsum('bhwij,bhwje->bhwie', attn, bv2)
            return out.reshape(b, h, n, d)

        def attn_layer(x, Wqkv, qs, ksc, Wo):
            b, n, _ = x.shape
            qkv = x @ Wqkv
            q, k, v = jnp.split(qkv, 3, -1)
            sh = lambda t: t.reshape(b, n, HEADS, DIM_HEAD).transpose(0, 2, 1, 3)
            q, k, v = (sh(q), sh(k), sh(v))
            q = l2norm(q) * qs
            k = l2norm(k) * ksc
            freqs, scale = rotary_tables(n)
            cos, sin = (jnp.cos(freqs), jnp.sin(freqs))
            q = q * cos * scale + rotate_half(q) * sin * scale
            inv = 1.0 / scale
            k = k * cos * inv + rotate_half(k) * sin * inv
            out = local_attention(q, k, v)
            out = out.transpose(0, 2, 1, 3).reshape(b, n, INNER)
            return out @ Wo

        def ffn_layer(x, g, bln, W1, b1, W2, b2):
            mu = x.mean(-1, keepdims=True)
            var = ((x - mu) ** 2).mean(-1, keepdims=True)
            xn = (x - mu) / jnp.sqrt(var + 1e-05) * g + bln
            hg = xn @ W1 + b1
            a, gate = jnp.split(hg, 2, -1)
            return a * jax.nn.gelu(gate, approximate=False) @ W2 + b2
        for i in range(DEPTH):
            x = attn_layer(shift_tokens(x), Wqkv[i], q_scale[i], k_scale[i], Wo[i]) + x
            x = ffn_layer(shift_tokens(x), ln_g[i], ln_b[i], W1[i], b1[i], W2[i], b2[i]) + x
        return x
    x = x + _L0_attn_ref(_layernorm(x, axis=-1), L0_attn_w_qkv, L0_attn_w_out)
    x = x + _L0_xattn_ref(_layernorm(x, axis=-1), ctx_1024, 32, L0_xattn_Wq, L0_xattn_bq, L0_xattn_Wk, L0_xattn_bk, L0_xattn_Wv, L0_xattn_bv, L0_xattn_Wo, L0_xattn_bo)
    x = x + _L0_ffn_ref(_layernorm(x, axis=-1), L0_ffn_w_gate, L0_ffn_w_up, L0_ffn_w_down)
    x = x + _L1_attn_ref(_layernorm(x, axis=-1), L1_attn_Wq, L1_attn_bq, L1_attn_Wk, L1_attn_bk, L1_attn_Wv, L1_attn_bv, L1_attn_Wo, L1_attn_bo, L1_attn_omega, L1_attn_g1, L1_attn_be1, L1_attn_W1, L1_attn_bf1, L1_attn_W2, L1_attn_bf2, L1_attn_g2, L1_attn_be2)
    x = x + _L1_xattn_ref(_layernorm(x, axis=-1), ctx_1024, ctx_1024, L1_xattn_Wq, L1_xattn_bq, L1_xattn_Wk, L1_xattn_bk, L1_xattn_Wv, L1_xattn_bv, L1_xattn_Wo, L1_xattn_bo)
    x = x + _L1_ffn_ref(_layernorm(x, axis=-1), L1_ffn_Wqkv, L1_ffn_q_scale, L1_ffn_k_scale, L1_ffn_Wo, L1_ffn_ln_g, L1_ffn_ln_b, L1_ffn_W1, L1_ffn_b1, L1_ffn_W2, L1_ffn_b2)
    return x

_drawn_inputs = setup_inputs


def setup_inputs(seed=0):
    import zlib

    import numpy as np

    out = dict(_drawn_inputs(seed))
    spreads = {'L0_xattn_bq': (0.0, 0.715),
     'L0_xattn_bk': (0.0, 0.8),
     'L0_xattn_bv': (0.0, 0.1),
     'L0_xattn_bo': (0.0, 0.1),
     'L1_attn_bq': (0.0, 0.369),
     'L1_attn_bk': (0.0, 0.404),
     'L1_attn_bv': (0.0, 0.1),
     'L1_attn_bo': (0.0, 0.1),
     'L1_attn_g1': (1.0, 0.2),
     'L1_attn_be1': (0.0, 0.1),
     'L1_attn_bf1': (0.0, 0.1),
     'L1_attn_bf2': (0.0, 0.1),
     'L1_attn_g2': (1.0, 0.2),
     'L1_attn_be2': (0.0, 0.1),
     'L1_xattn_bq': (0.0, 0.8),
     'L1_xattn_bk': (0.0, 0.8),
     'L1_xattn_bv': (0.0, 0.667),
     'L1_xattn_bo': (0.0, 0.1),
     'L1_ffn_q_scale': (1.0, 0.6),
     'L1_ffn_k_scale': (1.0, 0.6),
     'L1_ffn_ln_g': (1.0, 0.6),
     'L1_ffn_ln_b': (0.0, 0.8),
     'L1_ffn_b1': (0.0, 0.8),
     'L1_ffn_b2': (0.0, 0.1)}
    factors = {'L0_xattn_Wq': 3.813,
     'L0_xattn_Wk': 3.624,
     'L0_ffn_w_gate': 6.425,
     'L0_ffn_w_up': 5.884,
     'L0_ffn_w_down': 5.987,
     'L1_xattn_Wq': 8.0,
     'L1_xattn_Wk': 8.0,
     'L1_xattn_Wv': 3.119,
     'L1_xattn_Wo': 2.719,
     'L1_ffn_W1': 4.584,
     'L1_ffn_W2': 4.687}
    for name, (base, spread) in spreads.items():
        noise = np.random.default_rng([zlib.crc32(name.encode()), seed]).standard_normal(out[name].shape)
        drawn = base * np.exp(spread * noise) if base else spread * noise
        out[name] = jnp.asarray(drawn.astype(out[name].dtype))
    for name, factor in factors.items():
        out[name] = (out[name] * factor).astype(out[name].dtype)
    return out
```

```python
import math
from contextlib import ExitStack, contextmanager

import concourse.bass as bass
from concourse import mybir

F32 = mybir.dt.float32
BF16 = mybir.dt.bfloat16
ALU = mybir.AluOpType
ACT = mybir.ActivationFunctionType
AX = mybir.AxisListType.X

B, T, C = 2, 512, 128
N = B * T
NT = T // 128
S = 154
SH = S // 2
H, D = 16, 64
NP = H // 2
WIN = 32
INNER = H * D
TOPK = 32
I0 = 352
FB = 16
HS, DS = 16, 8
DFF = 512
LAYERS = 6
DI = int(128 * 4 * 2 / 3)
DIC = [(0, 128), (128, 128), (256, DI - 256)]
NEG = -1e30
STAGE = 6
LAST = 'ABCDEF'[STAGE - 1]


class Signal:
    every = []

    def __init__(self, book, name, sem):
        self.book = book.setdefault(name, {"key": {}, "per": {}})
        self.sem, self.name, self.n = sem, name, 0
        self.loop = None
        Signal.every.append(self)

    def mark(self, key=None):
        self.n += 1
        if key is not None:
            self.book["key"][key] = (Loop.now, self.n)
        return self.sem, 1

    def value(self, loop, n):
        if loop is None:
            return n
        per = self.book["per"].get(loop, 0)
        if Loop.now == loop:
            return Loop.reg * per + n if per else n
        return n + (LAYERS - 1) * per

    def at(self, key):
        loop, n = self.book["key"].get(key, (None, 1))
        return self.sem, self.value(loop, n)


class Loop:
    now, reg = None, None


@contextmanager
def layers(eng, name, trips=LAYERS):
    before = {s: s.n for s in Signal.every}
    with eng.Fori(0, trips) as reg:
        Loop.now, Loop.reg = name, reg
        yield reg
    for s, n in before.items():
        if s.n != n:
            s.book["per"][name] = s.n - n
            s.n = n + trips * (s.n - n)
    Loop.now = None


def build(nc, A, out, book, stage=99):
    Signal.every = []
    with ExitStack() as c:
        def sb(name, shape, dt=F32):
            return c.enter_context(nc.sbuf_tensor(name, shape, dt))

        def sg(name):
            return Signal(book, name, c.enter_context(nc.semaphore(name)))

        def raw(name):
            return c.enter_context(nc.semaphore(name))

        ps = c.enter_context(nc.psum_tensor("ps", [128, 8, 512], F32))

        x = sb("x", [128, N])
        mean_m = sb("mean_m", [128, 128])
        ident = sb("ident", [128, 128])
        identb = sb("identb", [128, 128], BF16)
        band = sb("band", [128, 160], BF16)
        ones = sb("ones", [1, 128])
        eps5 = sb("eps5", [128, 4])
        xc = sb("xc", [128, B, T])
        sq = sb("sq", [128, B, T])
        rs = sb("rs", [128, B, T])
        xn = sb("xn", [128, B, T])
        big = sb("big", [128, 38000])

        class Area:
            def __init__(self):
                self.at = 0

            def __call__(self, *dims):
                n = math.prod(dims)
                v = big[:, self.at:self.at + n]
                self.at += n
                assert self.at <= 38000, self.at
                if len(dims) == 2:
                    return v.rearrange("p (a b) -> p a b", a=dims[0])
                if len(dims) == 3:
                    return v.rearrange("p (a b c) -> p a b c", a=dims[0], b=dims[1])
                return v

        loaded = {}
        full = [sg(f"full{k}") for k in range(8)]
        free = [sg(f"free{k}") for k in range(8)]
        taken = [Signal(book, f"taken{k}", None) for k in range(8)]
        dve_step, act_step, pool_step = sg("dve_step"), sg("act_step"), sg("pool_step")
        const_in, stored = raw("const_in"), raw("stored")
        centred, squared, rooted, normed = sg("centred"), sg("squared"), sg("rooted"), sg("normed")
        x_new = sg("x_new")
        S_ = {}

        def take(pe, *banks):
            for k in banks:
                t = taken[k]
                per = t.book["per"].get(Loop.now, 0) if Loop.now else 0
                v = (Loop.reg * per + t.n) if per else t.n
                if t.n > 0:
                    pe.wait_ge(free[k].sem, v)
                t.mark()

        def step(eng, sgn, ins, extra=None):
            ins.then_inc(*sgn.mark(("step", sgn.n)))
            eng.wait_ge(*sgn.at(("step", sgn.n - 1)))

        def norm_pe(pe, key, b, bank, src, wait=(), center=True):
            for w in wait:
                pe.wait_ge(*w)
            if center:
                take(pe, bank)
                pe.matmul(ps[:, bank, :], mean_m[:, :], src, start=True, stop=True).then_inc(*full[bank].mark((key, b, "mean")))
            pe.wait_ge(*squared.at((key, b)))
            take(pe, bank)
            pe.matmul(ps[:, bank, :], mean_m[:, :], sq[:, b, :], start=True, stop=True).then_inc(*full[bank].mark((key, b, "var")))

        def norm_dve(dve, key, b, bank, src, center=True, out_=None):
            if center:
                dve.wait_ge(*full[bank].at((key, b, "mean")))
                dve.tensor_tensor(xc[:, b, :], src, ps[:, bank, :], ALU.subtract).then_inc(*centred.mark((key, b)))
                dve.wait_ge(*centred.at((key, b)))
            dve.wait_ge(*rooted.at((key, b)))
            dve.tensor_tensor(xn[:, b, :] if out_ is None else out_, xc[:, b, :] if center else src, rs[:, b, :],
                              ALU.mult).then_inc(*normed.mark((key, b)))

        def norm_act(act, key, b, bank, src, eps, center=True, wait=()):
            if center:
                act.wait_ge(*centred.at((key, b)))
                act.sem_inc(free[bank].mark()[0], 1)
                act.activation(sq[:, b, :], xc[:, b, :], ACT.Square).then_inc(*squared.mark((key, b)))
            else:
                for w in wait:
                    act.wait_ge(*w)
                act.activation(sq[:, b, :], src, ACT.Square).then_inc(*squared.mark((key, b)))
            act.wait_ge(*full[bank].at((key, b, "var")))
            step(act, act_step, act.activation(rs[:, b, :], ps[:, bank, :], ACT.Ln, bias=eps5[:, eps:eps + 1]))
            act.sem_inc(free[bank].mark()[0], 1)
            act.activation(rs[:, b, :], rs[:, b, :], ACT.Exp, scale=-0.5).then_inc(*rooted.mark((key, b)))

        ar = Area()
        Wqkv = ar(5, INNER)
        Wo = ar(NP, C)
        QT = ar(NP, T)
        KT = ar(NP, T)
        V = ar(NT, INNER)
        OT = ar(NP, T)
        tab0 = ar(4, T)
        tab = ar(4, T)
        P = ar(2, 2, 256)
        PT = ar(2, 2, 256)
        tmp = ar(4, T)
        sqh = ar(4, T)
        rk = ar(T)
        rq = ar(NT, H)
        seg = ar(NP, H)
        spread = ar(NP, 128)
        scl = ar(4)
        W1 = ar(2 * DI)
        W2 = ar(3, C)
        b1 = ar(6)
        fg = QT[:, 0:3, :]
        fh = QT[:, 3:6, :]
        lng = ar(3)
        nm = sb("nm", [128, 2, 8])
        QKV = ("q", "r", "k", "s")
        wsel = {"q": 0, "k": 1, "v": 2, "r": 3, "s": 4}
        roped, raised, v_ready, k_sq, q_sq = sg("roped"), sg("raised"), sg("v_ready"), sg("k_sq"), sg("q_sq")
        part1, part2 = sg("part1"), sg("part2")
        k_norm, q_norm, k_raised = sg("k_norm"), sg("q_norm"), sg("k_raised")
        topped, exped, scaled, turned, merged = sg("topped"), sg("exped"), sg("scaled"), sg("turned"), sg("merged")
        tabs_ready, gated, shifted = sg("tabs_ready"), sg("gated"), sg("shifted")
        attn_loaded, ffn_loaded = raw("attn_loaded"), raw("ffn_loaded")

        def attn_pe(pe, key, src, l2):
            for b in range(B):
                src_ready(pe, key, b)
                for p in range(NP):
                    for j, w in enumerate(QKV):
                        take(pe, j)
                        pe.matmul(ps[:, j, :], Wqkv[:, wsel[w], 128 * p:128 * p + 128], src(b), start=True, stop=True)\
                            .then_inc(*full[j].mark((key, b, p)))
                    if l2 and p > 0:
                        l2_pe(pe, key, b, p - 1)
                if l2:
                    l2_pe(pe, key, b, NP - 1)
                for t in range(NT):
                    for hf in range(2):
                        take(pe, 4 + hf)
                        pe.matmul(ps[:, 4 + hf, :], src(b)[:, 128 * t:128 * t + 128], Wqkv[:, 2, 512 * hf:512 * hf + 512],
                                  start=True, stop=True).then_inc(*full[4 + hf].mark((key, b, "v", t)))
                if l2:
                    pe.wait_ge(*k_norm.at((key, b)))
                    for p in range(NP):
                        k = p % 4
                        take(pe, k)
                        pe.matmul(ps[:, k, :], spread[0:16, p, :], rk[0:16, :], start=True, stop=True)\
                            .then_inc(*full[k].mark((key, b, "kn", p)))
                units = [(p, t) for p in range(NP) for t in range(NT)]
                for u in range(len(units) + 2):
                    if u < len(units):
                        p, t = units[u]
                        sl = 2 * (u % 2)
                        k0 = WIN if t == 0 else 0
                        pe.wait_ge(*(k_raised if l2 else roped).at((key, b, p) if l2 else (key, b, p, "k")))
                        pe.wait_ge(*roped.at((key, b, p, "q")))
                        take(pe, sl, sl + 1)
                        for h in range(2):
                            pe.matmul(ps[:, sl + h, k0:160], identb[:, :], band[:, k0:160], start=True, stop=False)
                            last = pe.matmul(ps[:, sl + h, k0:160], QT[64 * h:64 * h + 64, p, 128 * t:128 * t + 128],
                                             KT[64 * h:64 * h + 64, p, 128 * t - WIN + k0:128 * t + 128],
                                             start=False, stop=True)
                            last.then_inc(*full[sl + h].mark((key, b, p, t)))
                    if 1 <= u <= len(units):
                        p, t = units[u - 1]
                        pb, tb = (u - 1) % 2, 4 + (u - 1) % 2
                        pe.wait_ge(*scaled.at((key, b, p, t)))
                        take(pe, tb)
                        for h in range(2):
                            if t > 0:
                                pe.transpose(ps[:, tb, 256 * h:256 * h + 128], P[:, pb, h, 0:128], ident[:, :])
                            last = pe.transpose(ps[:, tb, 256 * h + 128:256 * h + 256], P[:, pb, h, 128:256], ident[:, :])
                        last.then_inc(*full[tb].mark((key, b, p, t)))
                    if u >= 2:
                        p, t = units[u - 2]
                        pb, ob = u % 2, 6 + p % 2
                        pe.wait_ge(*turned.at((key, b, p, t)))
                        if t == 0:
                            take(pe, ob)
                            if p == 0:
                                pe.wait_ge(*v_ready.at((key, b, NT - 1)))
                        for h in range(2):
                            o = ps[64 * h:64 * h + 64, ob, 128 * t:128 * t + 128]
                            f = 128 * p + 64 * h
                            last = pe.matmul(o, V[:, t, f:f + 64], PT[:, pb, h, 128:256], start=True, stop=t == 0)
                            if t > 0:
                                last = pe.matmul(o, V[96:128, t - 1, f:f + 64], PT[96:128, pb, h, 0:128],
                                                 start=False, stop=True, tile_position=(96, 64 * h))
                        last.then_inc(*full[ob].mark((key, b, p, t)))
                take(pe, 6)
                for p in range(NP):
                    pe.wait_ge(*merged.at((key, b, p)))
                    last = pe.matmul(ps[:, 6, :], Wo[:, p, :], OT[:, p, :], start=p == 0, stop=p == NP - 1)
                last.then_inc(*full[6].mark((key, b, "y")))

        def l2_pe(pe, key, b, p):
            pe.wait_ge(*k_sq.at((key, b, p)))
            if p == 0:
                take(pe, 6, 7)
            m = pe.matmul(ps[0:16, 6, :], seg[:, p, :], sqh[:, 2 + p % 2, :], start=p == 0, stop=p == NP - 1)
            pe.wait_ge(*q_sq.at((key, b, p)))
            for t in range(NT):
                last = pe.matmul(ps[:, 7, 16 * t + 2 * p:16 * t + 2 * p + 2], sqh[:, p % 2, 128 * t:128 * t + 128],
                                 seg[:, 0, 0:2], start=True, stop=True)
            last.then_inc(*full[7].mark((key, b, "ssq", p)))
            if p == NP - 1:
                pass

        def attn_act(act, key, l2):
            for b in range(B):
                for p in range(NP):
                    if l2:
                        if p >= 2:
                            act.wait_ge(*full[7].at((key, b, "ssq", p - 2)))
                        act.wait_ge(*full[0].at((key, b, p)))
                        act.activation(sqh[:, p % 2, :], ps[:, 0, :], ACT.Square).then_inc(*q_sq.mark((key, b, p)))
                        act.wait_ge(*full[2].at((key, b, p)))
                        act.activation(sqh[:, 2 + p % 2, :], ps[:, 2, :], ACT.Square).then_inc(*k_sq.mark((key, b, p)))
                for t in range(NT):
                    for hf in range(2):
                        act.wait_ge(*full[4 + hf].at((key, b, "v", t)))
                        act.activation(V[:, t, 512 * hf:512 * hf + 512], ps[:, 4 + hf, :], ACT.Copy)\
                            .then_inc(*(free[4].mark() if hf == 0 else v_ready.mark((key, b, t))))
                    act.wait_ge(*v_ready.at((key, b, t)))
                    act.sem_inc(free[5].mark()[0], 1)
                if l2:
                    act.wait_ge(*part1.at((key, b, "guard")))
                    step(act, act_step, act.activation(rk[0:16, :], rk[0:16, :], ACT.Ln, scale=2.0 ** 20))
                    act.activation(rk[0:16, :], rk[0:16, :], ACT.Exp, scale=-0.5, bias=eps5[0:16, 3:4])\
                        .then_inc(*k_norm.mark((key, b)))
                    step(act, act_step, act.activation(rq, rq, ACT.Ln, scale=2.0 ** 20))
                    act.activation(rq, rq, ACT.Exp, scale=-0.5, bias=eps5[:, 3:4]).then_inc(*q_norm.mark((key, b)))
                units = [(p, t) for p in range(NP) for t in range(NT)]
                for u in range(len(units) + 1):
                    if u < len(units):
                        p, t = units[u]
                        sl, pb = 2 * (u % 2), u % 2
                        k0 = WIN if t == 0 else 0
                        act.wait_ge(*topped.at((key, b, p, t)))
                        for h in range(2):
                            sc = rq8[:, t, 2 * p + h:2 * p + h + 1] if l2 else D ** -0.5
                            ins = act.activation(P[:, pb, h, 96 + k0:256], ps[:, sl + h, k0:160], ACT.Exp,
                                                 bias=nm[:, u % 2, 2 + h:3 + h], scale=sc,
                                                 accum_out=nm[:, u % 2, 4 + h:5 + h])
                            if h == 0:
                                ins.then_inc(*free[sl].mark())
                            else:
                                ins.then_inc(*exped.mark((key, b, p, t)))
                        act.wait_ge(*exped.at((key, b, p, t)))
                        act.sem_inc(free[sl + 1].mark()[0], 1)
                    if u >= 1:
                        p, t = units[u - 1]
                        tb, pb = 4 + (u - 1) % 2, (u - 1) % 2
                        act.wait_ge(*full[tb].at((key, b, p, t)))
                        src_ = ps[:, tb, :].rearrange("p (h k) -> p h k", h=2)
                        if t == 0:
                            ins = act.activation(PT[:, pb, :, 128:256], src_[:, :, 128:256], ACT.Copy)
                        else:
                            step(act, act_step, act.activation(PT[96:128, pb, :, 0:128], src_[96:128, :, 0:128], ACT.Copy))
                            ins = act.activation(PT[:, pb, :, 128:256], src_[:, :, 128:256], ACT.Copy)
                        ins.then_inc(*turned.mark((key, b, p, t)))
                        act.wait_ge(*turned.at((key, b, p, t)))
                        act.sem_inc(free[tb].mark()[0], 1)

        rq8 = sb("rq8", [128, NT, H])

        def attn_dve(dve, key, l2):
            for b in range(B):
                for p in range(NP):
                    for j, w in enumerate(QKV):
                        if l2 and w == "q":
                            dve.wait_ge(*q_sq.at((key, b, p)))
                        elif l2 and w == "k":
                            dve.wait_ge(*k_sq.at((key, b, p)))
                        else:
                            dve.wait_ge(*full[j].at((key, b, p)))
                        if (b, p) != (0, 0):
                            pp = (b, p - 1) if p else (b - 1, NP - 1)
                            dve.wait_ge(*roped.at((key, *pp, "q" if j < 2 else "k")))
                        dve.tensor_tensor(tmp[:, j, :], ps[:, j, :], (tab if l2 else tab0)[:, j, :], ALU.mult)\
                            .then_inc(*(part1 if j < 2 else part2).mark((key, b, p, j)))
                        dve.wait_ge(*(part1 if j < 2 else part2).at((key, b, p, j)))
                        dve.sem_inc(free[j].mark()[0], 1)
                if l2:
                    dve.wait_ge(*full[7].at((key, b, "ssq", NP - 1)))
                    step(dve, dve_step, dve.tensor_scalar(rk[0:16, :], ps[0:16, 6, :], 1e-24, None, ALU.max))
                    dve.sem_inc(free[6].mark()[0], 1)
                    dve.tensor_scalar(rq, ps[:, 7, 0:64].rearrange("p (t h) -> p t h", t=NT), 1e-24, None, ALU.max)\
                        .then_inc(*part1.mark((key, b, "guard")))
                    dve.wait_ge(*part1.at((key, b, "guard")))
                    dve.sem_inc(free[7].mark()[0], 1)
                    for p in range(NP):
                        k = p % 4
                        dve.wait_ge(*full[k].at((key, b, "kn", p)))
                        dve.wait_ge(*roped.at((key, b, p, "k")))
                        dve.tensor_tensor(KT[:, p, :], KT[:, p, :], ps[:, k, :], ALU.mult)\
                            .then_inc(*k_raised.mark((key, b, p)))
                        dve.wait_ge(*k_raised.at((key, b, p)))
                        dve.sem_inc(free[k].mark()[0], 1)
                    dve.wait_ge(*q_norm.at((key, b)))
                    step(dve, dve_step, dve.tensor_scalar(rq8[:, :, :], rq, 8.0, None, ALU.mult))
                units = [(p, t) for p in range(NP) for t in range(NT)]
                for u in range(len(units) + 1):
                    if u < len(units):
                        p, t = units[u]
                        sl, i = 2 * (u % 2), u % 2
                        k0 = WIN if t == 0 else 0
                        dve.wait_ge(*full[sl].at((key, b, p, t)))
                        dve.wait_ge(*full[sl + 1].at((key, b, p, t)))
                        if u >= 2:
                            dve.wait_ge(*exped.at((key, b, *units[u - 2])))
                        step(dve, dve_step, dve.tensor_reduce(nm[:, i, 0:2], ps[:, sl:sl + 2, k0:160], AX, ALU.max))
                        if l2:
                            step(dve, dve_step, dve.tensor_tensor(nm[:, i, 0:2], nm[:, i, 0:2], rq8[:, t, 2 * p:2 * p + 2], ALU.mult))
                        dve.tensor_scalar(nm[:, i, 2:4], nm[:, i, 0:2], -1.0 if l2 else -D ** -0.5, None, ALU.mult)\
                            .then_inc(*topped.mark((key, b, p, t)))
                    if u >= 1:
                        p, t = units[u - 1]
                        i = (u - 1) % 2
                        k0 = WIN if t == 0 else 0
                        dve.wait_ge(*exped.at((key, b, p, t)))
                        step(dve, dve_step, dve.reciprocal(nm[:, i, 6:8], nm[:, i, 4:6]))
                        for h in range(2):
                            ins = dve.tensor_scalar(P[:, i, h, 96 + k0:256], P[:, i, h, 96 + k0:256],
                                                    nm[:, i, 6 + h:7 + h], None, ALU.mult)
                        ins.then_inc(*scaled.mark((key, b, p, t)))
                        if t == 1 and p > 0:
                            merge_dve(dve, key, b, p - 1)
                merge_dve(dve, key, b, NP - 1)
                dve.wait_ge(*full[6].at((key, b, "y")))
                dve.tensor_tensor(x[:, T * b:T * b + T], x[:, T * b:T * b + T], ps[:, 6, :], ALU.add)\
                    .then_inc(*x_new.mark((key, b)))
                dve.wait_ge(*x_new.at((key, b)))
                dve.sem_inc(free[6].mark()[0], 1)

        def merge_dve(dve, key, b, p):
            ob = 6 + p % 2
            dve.wait_ge(*full[ob].at((key, b, p, NT - 1)))
            dve.tensor_copy(OT[:, p, :], ps[:, ob, :]).then_inc(*merged.mark((key, b, p)))
            dve.wait_ge(*merged.at((key, b, p)))
            dve.sem_inc(free[ob].mark()[0], 1)

        def attn_pool(pool, key):
            for b in range(B):
                for p in range(NP):
                    pool.wait_ge(*part1.at((key, b, p, 1)))
                    pool.tensor_tensor(QT[:, p, :], tmp[:, 0, :], tmp[:, 1, :], ALU.add).then_inc(*roped.mark((key, b, p, "q")))
                    pool.wait_ge(*part2.at((key, b, p, 3)))
                    pool.tensor_tensor(KT[:, p, :], tmp[:, 2, :], tmp[:, 3, :], ALU.add).then_inc(*roped.mark((key, b, p, "k")))

        def src_ready(pe, key, b):
            if key == "A":
                pe.wait_ge(*normed.at(("A2", b)))
            else:
                pe.wait_ge(*shifted.at(("F1", b)))

        cols = lambda b: slice(T * b, T * b + T)

        fix = sb("fix", [128, 3100])
        fat = [0]

        def keep(*dims):
            n = math.prod(dims)
            v = fix[:, fat[0]:fat[0] + n]
            fat[0] += n
            assert fat[0] <= 3100, fat[0]
            return v if len(dims) == 1 else v.rearrange("p (a b) -> p a b", a=dims[0]) if len(dims) == 2 else \
                v.rearrange("p (a b c) -> p a b c", a=dims[0], b=dims[1])
        ctxT = keep(B, S)
        Bw = keep(4, C)
        Bb = keep(4)
        Ew = keep(4, C)
        Eb = keep(4)
        hmask = keep(HS)
        Cw = keep(70, FB)
        tri = keep(128)
        a2 = Area()
        qt = a2(T)
        kt = a2(S)
        vt = a2(2, C)
        vt1 = a2(2, HS * 9)
        sc_ = a2(2, S)
        rem = a2(2, S)
        pe_ = a2(2, S)
        msk = a2(S)
        m8 = a2(2, 40)
        pt2 = a2(2, 512)
        ctxo = a2(T)
        KB = a2(HS, S)
        PE_ = a2(HS, S)
        mx = a2(2, 16)
        atok = a2(128)
        aT = a2(T)
        rd = a2(HS)
        gT = a2(I0)
        uT = a2(I0)
        dT = a2(3, C)
        xq = a2(B, T)
        xqT = a2(B, T)
        hq = a2(B, NT * I0)
        hT = a2(3, T)
        qa = a2(1408)
        qu = a2(1408)
        qs = a2(1408)
        qb = a2(3, 88)
        eg = a2(2, I0)
        q_ready, k_ready, vv_ready = sg("q_ready"), sg("k_ready"), sg("vv_ready")
        picked, b_exp, b_prob, b_turn, b_ctx = sg("picked"), sg("b_exp"), sg("b_prob"), sg("b_turn"), sg("b_ctx")
        signed, q4, turned4, expg, hgate = sg("signed"), sg("q4"), sg("turned4"), sg("expg"), sg("hgate")
        kb_ready, e_max, e_exp, e_turn_a, e_turn_d, e_norm = sg("kb_ready"), sg("e_max"), sg("e_exp"), sg("e_turn_a"), sg("e_turn_d"), sg("e_norm")

        def read(eng, bank, sgn, key):
            eng.wait_ge(*sgn.at(key))
            eng.sem_inc(free[bank].mark()[0], 1)

        def qkv_pe(pe, key, b, w):
            pe.wait_ge(*normed.at((key + "1", b)))
            take(pe, 0)
            pe.matmul(ps[:, 0, :], w[:, 0, :], xn[:, b, :], start=True, stop=True).then_inc(*full[0].mark((key, b, "q")))
            take(pe, 1)
            pe.matmul(ps[:, 1, 0:S], w[:, 1, :], ctxT[:, b, :], start=True, stop=True).then_inc(*full[1].mark((key, b, "k")))
            take(pe, 2)
            for hf in range(2):
                last = pe.matmul(ps[0:SH, 2, 128 * hf:128 * hf + 128], ctxT[:, b, SH * hf:SH * hf + SH], w[:, 2, :],
                                 start=True, stop=True)
            last.then_inc(*full[2].mark((key, b, "v")))

        def qkv_act(act, key, b, bias):
            act.wait_ge(*full[0].at((key, b, "q")))
            act.activation(qt, ps[:, 0, :], ACT.Identity, bias=bias[:, 0:1]).then_inc(*q_ready.mark((key, b)))
            read(act, 0, q_ready, (key, b))
            act.wait_ge(*full[1].at((key, b, "k")))
            act.activation(kt, ps[:, 1, 0:S], ACT.Identity, bias=bias[:, 1:2]).then_inc(*k_ready.mark((key, b)))
            read(act, 1, k_ready, (key, b))
            act.wait_ge(*full[2].at((key, b, "v")))
            src = ps[0:SH, 2, 0:256].rearrange("p (a c) -> p a c", a=2)
            if key == "B":
                ins = act.activation(vt[0:SH, :, :], src, ACT.Copy)
            else:
                src = ps[0:SH, 2, 0:256].rearrange("p (a d) -> p a d", d=DS)
                ins = act.activation(vt1.rearrange("p a (h d) -> p (a h) d", d=9)[0:SH, :, 0:DS], src, ACT.Copy)
            ins.then_inc(*vv_ready.mark((key, b)))
            read(act, 2, vv_ready, (key, b))

        def out_pe(pe, key, b, w, src, wait):
            pe.wait_ge(*wait)
            take(pe, 3)
            pe.matmul(ps[:, 3, :], w, src, start=True, stop=True).then_inc(*full[3].mark((key, b, "y")))

        def out_dve(dve, key, b, bias, bank=3):
            dve.wait_ge(*full[bank].at((key, b, "y")))
            dve.scalar_tensor_tensor(x[:, cols(b)], ps[:, bank, :], bias, x[:, cols(b)], ALU.add, ALU.add)\
                .then_inc(*x_new.mark((key, b)))
            read(dve, bank, x_new, (key, b))

        def b_pe(pe):
            for b in range(B):
                norm_pe(pe, "B1", b, b, x[:, cols(b)], wait=(x_new.at(("A", b)),))
            for b in range(B):
                qkv_pe(pe, "B", b, Bw)
                pe.wait_ge(*q_ready.at(("B", b)))
                pe.wait_ge(*k_ready.at(("B", b)))
                for t in range(NT + 1):
                    if t < NT:
                        k = 4 + t % 2
                        take(pe, k)
                        pe.matmul(ps[:, k, 0:S], qt[:, 128 * t:128 * t + 128], kt, start=True, stop=True)\
                            .then_inc(*full[k].mark(("B", b, t)))
                    if t > 0:
                        u = t - 1
                        k = 6 + u % 2
                        pe.wait_ge(*b_prob.at((b, u)))
                        take(pe, k)
                        for hf in range(2):
                            last = pe.transpose(ps[0:SH, k, 128 * hf:128 * hf + 128], pe_[:, u % 2, SH * hf:SH * hf + SH], ident[:, :])
                        last.then_inc(*full[k].mark(("B", b, u)))
                        pe.wait_ge(*b_turn.at((b, u)))
                        if u == 0:
                            pe.wait_ge(*vv_ready.at(("B", b)))
                            take(pe, 2)
                        for hf in range(2):
                            last = pe.matmul(ps[:, 2, 128 * u:128 * u + 128], vt[0:SH, hf, :], pt2[0:SH, u % 2, 128 * hf:128 * hf + 128],
                                             start=hf == 0, stop=hf == 1)
                last.then_inc(*full[2].mark(("B", b, "o")))
                out_pe(pe, "B", b, Bw[:, 3, :], ctxo, b_ctx.at(("B", b)))

        def b_act(act):
            for b in range(B):
                norm_act(act, "B1", b, b, None, 0)
            for b in range(B):
                qkv_act(act, "B", b, Bb)
                for t in range(NT + 1):
                    if t < NT:
                        act.wait_ge(*picked.at((b, t)))
                        act.activation(pe_[:, t % 2, :], sc_[:, t % 2, :], ACT.Exp, bias=m8[:, t % 2, 32:33], scale=C ** -0.5)\
                            .then_inc(*b_exp.mark((b, t)))
                    if t > 0:
                        u = t - 1
                        k = 6 + u % 2
                        act.wait_ge(*full[k].at(("B", b, u)))
                        act.activation(pt2[0:SH, u % 2, 0:256], ps[0:SH, k, 0:256], ACT.Copy).then_inc(*b_turn.mark((b, u)))
                        read(act, k, b_turn, (b, u))
                act.wait_ge(*full[2].at(("B", b, "o")))
                act.activation(ctxo, ps[:, 2, :], ACT.Identity, bias=Bb[:, 2:3]).then_inc(*b_ctx.mark(("B", b)))
                read(act, 2, b_ctx, ("B", b))

        def b_dve(dve):
            for b in range(B):
                norm_dve(dve, "B1", b, b, x[:, cols(b)])
            for b in range(B):
                for t in range(NT + 1):
                    if t < NT:
                        i, k = t % 2, 4 + t % 2
                        dve.wait_ge(*full[k].at(("B", b, t)))
                        if t >= 2:
                            dve.wait_ge(*full[6 + i].at(("B", b, t - 2)))
                        step(dve, dve_step, dve.tensor_copy(sc_[:, i, :], ps[:, k, 0:S]))
                        dve.sem_inc(free[k].mark()[0], 1)
                        for r in range(TOPK // 8):
                            src = sc_[:, i, :] if r == 0 else rem[:, i, :]
                            step(dve, dve_step, dve.max(m8[:, i, 8 * r:8 * r + 8], src))
                            step(dve, dve_step, dve.match_replace(rem[:, i, :], m8[:, i, 8 * r:8 * r + 8], src, -3e38))
                        dve.tensor_scalar(m8[:, i, 32:33], m8[:, i, 0:1], -C ** -0.5, None, ALU.mult).then_inc(*picked.mark((b, t)))
                    if t > 0:
                        u, i = t - 1, (t - 1) % 2
                        step(dve, dve_step, dve.tensor_tensor(msk, rem[:, i, :], sc_[:, i, :], ALU.not_equal))
                        dve.wait_ge(*b_exp.at((b, u)))
                        step(dve, dve_step, dve.tensor_tensor(pe_[:, i, :], pe_[:, i, :], msk, ALU.mult))
                        step(dve, dve_step, dve.tensor_reduce(m8[:, i, 33:34], pe_[:, i, :], AX, ALU.add))
                        step(dve, dve_step, dve.reciprocal(m8[:, i, 34:35], m8[:, i, 33:34]))
                        dve.tensor_scalar(pe_[:, i, :], pe_[:, i, :], m8[:, i, 34:35], None, ALU.mult).then_inc(*b_prob.mark((b, u)))
                out_dve(dve, "B", b, Bb[:, 3:4])

        def fp4(dve, key, src, nb, dst):
            n = nb * FB
            s3 = lambda v: v[:, 0:n].rearrange("p (a b) -> p a b", b=FB)
            wide = lambda v: v.unsqueeze(2).to_broadcast([128, nb, FB])
            big_, sca, inv = qb[:, 0, 0:nb], qb[:, 1, 0:nb], qb[:, 2, 0:nb]
            step(dve, dve_step, dve.tensor_reduce(big_, src, AX, ALU.max, apply_absolute_value=True))
            step(dve, dve_step, dve.tensor_scalar(sca, big_, 1 / 6, 1e-12, ALU.mult, ALU.max))
            step(dve, dve_step, dve.reciprocal(inv, sca))
            step(dve, dve_step, dve.tensor_tensor(s3(qa), src, wide(inv), ALU.mult))
            step(dve, dve_step, dve.scalar_tensor_tensor(qa[:, 0:n], qa[:, 0:n], -1.0, qa[:, 0:n], ALU.mult, ALU.max))
            a_, u_ = qa[:, 0:n], qu[:, 0:n]
            step(dve, dve_step, dve.tensor_scalar(u_, a_, 5.0, 2.0, ALU.is_gt, ALU.mult))
            for m in (3.5, 2.5):
                step(dve, dve_step, dve.scalar_tensor_tensor(u_, a_, m, u_, ALU.is_gt, ALU.add))
            step(dve, dve_step, dve.tensor_scalar(u_, u_, 2.0, None, ALU.mult))
            for m in (1.75, 1.25, 0.75, 0.25):
                step(dve, dve_step, dve.scalar_tensor_tensor(u_, a_, m, u_, ALU.is_gt, ALU.add))
            dve.wait_ge(*signed.at(key))
            step(dve, dve_step, dve.scalar_tensor_tensor(u_, u_, 0.5, qs[:, 0:n], ALU.mult, ALU.mult))
            dve.tensor_tensor(dst, s3(qu), wide(sca), ALU.mult).then_inc(*q4.mark(key))
            dve.wait_ge(*q4.at(key))

        def sign_act(act, key, src, n):
            act.activation(qs[:, 0:n], src, ACT.Sign).then_inc(*signed.mark(key))

        def c_pe(pe):
            pe.wait_ge(*q4.at("w"))
            for j, off in enumerate((0, 24, 48)):
                take(pe, j)
                for ch in range(3):
                    m = min(128, I0 - 128 * ch)
                    if j < 2:
                        last = pe.transpose(ps[:, j, 128 * ch:128 * ch + m],
                                            Cw[0:m, off + 8 * ch:off + 8 * ch + 8, :].rearrange("p a b -> p (a b)"), ident[0:m, 0:m])
                    else:
                        last = pe.transpose(ps[0:m, j, 128 * ch:128 * ch + 128],
                                            Cw[:, off + 8 * ch:off + 8 * ch + m // FB, :].rearrange("p a b -> p (a b)"), ident[:, :])
                last.then_inc(*full[j].mark(("C", "w", j)))
            for b in range(B):
                norm_pe(pe, "C1", b, 6 + b, x[:, cols(b)], wait=(x_new.at(("B", b)),))
            for b in range(B):
                pe.wait_ge(*normed.at(("C1", b)))
                take(pe, b)
                for t in range(NT):
                    last = pe.transpose(ps[:, b, 128 * t:128 * t + 128], xn[:, b, 128 * t:128 * t + 128], ident[:, :])
                last.then_inc(*full[b].mark(("C", b, "x")))
            for b in range(B):
                pe.wait_ge(*q4.at(("x", b)))
                take(pe, 2)
                for t in range(NT):
                    last = pe.transpose(ps[:, 2, 128 * t:128 * t + 128], xq[:, b, 128 * t:128 * t + 128], ident[:, :])
                last.then_inc(*full[2].mark(("C", b, "xt")))
                pe.wait_ge(*turned4.at(("x", b)))
                if b == 0:
                    pe.wait_ge(*turned4.at(("w", 2)))
                for t in range(NT):
                    for j, w in enumerate((gT, uT)):
                        k = 4 + 2 * (t % 2) + j
                        take(pe, k)
                        pe.matmul(ps[:, k, 0:I0], xqT[:, b, 128 * t:128 * t + 128], w, start=True, stop=True)\
                            .then_inc(*full[k].mark(("C", b, t, j)))
            for b in range(B):
                pe.wait_ge(*q4.at(("h", b)))
                for t in range(NT):
                    k = t % 2
                    take(pe, k)
                    for ch in range(3):
                        m = min(128, I0 - 128 * ch)
                        last = pe.transpose(ps[0:m, k, 128 * ch:128 * ch + 128], hq[:, b, I0 * t + 128 * ch:I0 * t + 128 * ch + m], ident[:, :])
                    last.then_inc(*full[k].mark(("C", b, "h", t)))
                pe.wait_ge(*turned4.at(("h", b, NT - 1)))
                take(pe, 3)
                for ch in range(3):
                    m = min(128, I0 - 128 * ch)
                    last = pe.matmul(ps[:, 3, :], dT[0:m, ch, :], hT[0:m, ch, :], start=ch == 0, stop=ch == 2)
                last.then_inc(*full[3].mark(("C", b, "y")))

        def c_act(act):
            sign_act(act, "w", Cw.rearrange("p a b -> p (a b)"), 1120)
            for j, dst in enumerate((gT, uT)):
                act.wait_ge(*full[j].at(("C", "w", j)))
                act.activation(dst, ps[:, j, 0:I0], ACT.Copy).then_inc(*turned4.mark(("w", j)))
                read(act, j, turned4, ("w", j))
            act.wait_ge(*full[2].at(("C", "w", 2)))
            step(act, act_step, act.activation(dT[:, 0:2, :], ps[:, 2, 0:256].rearrange("p (a b) -> p a b", a=2), ACT.Copy))
            act.activation(dT[0:96, 2, :], ps[0:96, 2, 256:384], ACT.Copy).then_inc(*turned4.mark(("w", 2)))
            read(act, 2, turned4, ("w", 2))
            for b in range(B):
                norm_act(act, "C1", b, 6 + b, None, 0)
            for b in range(B):
                act.wait_ge(*q4.at("w" if b == 0 else ("x", b - 1)))
                act.wait_ge(*centred.at(("xc", b)))
                sign_act(act, ("x", b), xq[:, b, :], T)
                act.wait_ge(*full[2].at(("C", b, "xt")))
                act.activation(xqT[:, b, :], ps[:, 2, :], ACT.Copy).then_inc(*turned4.mark(("x", b)))
                read(act, 2, turned4, ("x", b))
                for t in range(NT):
                    k = 4 + 2 * (t % 2)
                    act.wait_ge(*full[k].at(("C", b, t, 0)))
                    if t >= 2:
                        act.wait_ge(*hgate.at((b, t - 2)))
                    act.activation(eg[:, t % 2, :], ps[:, k, 0:I0], ACT.Exp, scale=-1.0).then_inc(*expg.mark((b, t)))
            for b in range(B):
                act.wait_ge(*hgate.at((b, NT - 1)))
                act.wait_ge(*q4.at(("x", 1) if b == 0 else ("h", b - 1)))
                sign_act(act, ("h", b), hq[:, b, :], NT * I0)
                for t in range(NT):
                    k = t % 2
                    act.wait_ge(*full[k].at(("C", b, "h", t)))
                    step(act, act_step, act.activation(hT[:, 0:2, 128 * t:128 * t + 128],
                                                       ps[:, k, 0:256].rearrange("p (a b) -> p a b", a=2), ACT.Copy))
                    act.activation(hT[0:96, 2, 128 * t:128 * t + 128], ps[0:96, k, 256:384], ACT.Copy).then_inc(*turned4.mark(("h", b, t)))
                    read(act, k, turned4, ("h", b, t))

        def c_dve(dve):
            fp4(dve, "w", Cw, 70, Cw)
            for b in range(B):
                norm_dve(dve, "C1", b, 6 + b, x[:, cols(b)])
            b3 = lambda v: v.rearrange("p (a b) -> p a b", b=FB)
            for b in range(B):
                dve.wait_ge(*full[b].at(("C", b, "x")))
                dve.tensor_copy(xq[:, b, :], ps[:, b, :]).then_inc(*centred.mark(("xc", b)))
                read(dve, b, centred, ("xc", b))
            for b in range(B):
                fp4(dve, ("x", b), b3(xq[:, b, :]), 32, b3(xq[:, b, :]))
                for t in range(NT):
                    k, i = 4 + 2 * (t % 2), t % 2
                    h_ = hq[:, b, I0 * t:I0 * t + I0]
                    dve.wait_ge(*expg.at((b, t)))
                    step(dve, dve_step, dve.tensor_scalar(eg[:, i, :], eg[:, i, :], 1.0, None, ALU.add))
                    step(dve, dve_step, dve.reciprocal(eg[:, i, :], eg[:, i, :]))
                    step(dve, dve_step, dve.tensor_tensor(h_, eg[:, i, :], ps[:, k, 0:I0], ALU.mult))
                    dve.sem_inc(free[k].mark()[0], 1)
                    dve.wait_ge(*full[k + 1].at(("C", b, t, 1)))
                    dve.tensor_tensor(h_, h_, ps[:, k + 1, 0:I0], ALU.mult).then_inc(*hgate.mark((b, t)))
                    read(dve, k + 1, hgate, (b, t))
            for b in range(B):
                fp4(dve, ("h", b), b3(hq[:, b, :]), NT * I0 // FB, b3(hq[:, b, :]))
                dve.wait_ge(*full[3].at(("C", b, "y")))
                dve.tensor_tensor(x[:, cols(b)], x[:, cols(b)], ps[:, 3, :], ALU.add).then_inc(*x_new.mark(("C", b)))
                read(dve, 3, x_new, ("C", b))

        def e_pe(pe, before):
            for b in range(B):
                norm_pe(pe, "E1", b, b, x[:, cols(b)], wait=(x_new.at((before, b)),))
            for b in range(B):
                qkv_pe(pe, "E", b, Ew)
                pe.wait_ge(*q_ready.at(("E", b)))
                pe.wait_ge(*kb_ready.at(b))
                pe.wait_ge(*vv_ready.at(("E", b)))
                for t in range(NT):
                    for g in range(6):
                        n = min(3, HS - 3 * g)
                        k = (6 * t + g) % 5
                        take(pe, k)
                        pe.matmul(ps[:, k, 0:n * S], qt[:, 128 * t:128 * t + 128],
                                  KB[:, 3 * g:3 * g + n, :].rearrange("p a b -> p (a b)"), start=True, stop=True)\
                            .then_inc(*full[k].mark(("E", b, t, g)))
                    pe.wait_ge(*e_exp.at((b, t)))
                    take(pe, 5)
                    for m in range(9):
                        if m < 8:
                            k = 6 + m % 2
                            take(pe, k)
                            for q_ in range(4):
                                last = pe.transpose(ps[0:SH, k, 128 * q_:128 * q_ + 128],
                                                    PE_[:, 2 * m + q_ // 2, SH * (q_ % 2):SH * (q_ % 2) + SH], ident[:, :])
                            last.then_inc(*full[k].mark(("E", b, t, m)))
                        if m > 0:
                            w = m - 1
                            pe.wait_ge(*(e_turn_a if w % 2 == 0 else e_turn_d).at((b, t, w)))
                            for q_ in range(4):
                                h = 2 * w + q_ // 2
                                last = pe.matmul(ps[:, 5, 9 * h:9 * h + 9], pt2[0:SH, w % 2, 128 * q_:128 * q_ + 128],
                                                 vt1[0:SH, q_ % 2, 9 * h:9 * h + 9], start=q_ % 2 == 0, stop=q_ % 2 == 1)
                    last.then_inc(*full[5].mark(("E", b, t, "o")))
                    pe.wait_ge(*e_norm.at((b, t)))
                    take(pe, 5)
                    pe.transpose(ps[:, 5, 0:128], atok, ident[:, :]).then_inc(*full[5].mark(("E", b, t, "a")))
                out_pe(pe, "E", b, Ew[:, 3, :], aT, b_ctx.at(("E", b, NT - 1)))

        def e_act(act):
            for b in range(B):
                norm_act(act, "E1", b, b, None, 0)
            for b in range(B):
                qkv_act(act, "E", b, Eb)
                for t in range(NT):
                    for h in range(HS):
                        g, j = h // 3, h % 3
                        k = (6 * t + g) % 5
                        if j == 0:
                            act.wait_ge(*e_max.at((b, t, g)))
                        ins = act.activation(PE_[:, h, :], ps[:, k, S * j:S * j + S], ACT.Exp, bias=mx[:, 1, h:h + 1], scale=DS ** -0.5)
                        if j == 2:
                            ins.then_inc(*free[k].mark())
                        elif h == HS - 1:
                            ins.then_inc(*e_exp.mark((b, t)))
                            read(act, k, e_exp, (b, t))
                    for m in range(0, 8, 2):
                        act.wait_ge(*full[6].at(("E", b, t, m)))
                        act.activation(pt2[0:SH, 0, :], ps[0:SH, 6, :], ACT.Copy).then_inc(*e_turn_a.mark((b, t, m)))
                        read(act, 6, e_turn_a, (b, t, m))
                    act.wait_ge(*full[5].at(("E", b, t, "a")))
                    act.activation(aT[:, 128 * t:128 * t + 128], ps[:, 5, 0:128], ACT.Identity, bias=Eb[:, 2:3])\
                        .then_inc(*b_ctx.mark(("E", b, t)))
                    read(act, 5, b_ctx, ("E", b, t))

        def e_dve(dve):
            dve.wait_ge(*x_new.at(("D", 1)))
            dve.memset(vt1, 1.0).then_inc(*vv_one.mark("ones"))
            for b in range(B):
                norm_dve(dve, "E1", b, b, x[:, cols(b)])
            for b in range(B):
                dve.wait_ge(*k_ready.at(("E", b)))
                dve.tensor_tensor(KB, kt.unsqueeze(1).to_broadcast([128, HS, S]), hmask.unsqueeze(2).to_broadcast([128, HS, S]), ALU.mult)\
                    .then_inc(*kb_ready.mark(b))
                for t in range(NT):
                    if (b, t) != (0, 0):
                        dve.wait_ge(*e_exp.at((b, t - 1) if t else (b - 1, NT - 1)))
                    for g in range(6):
                        n = min(3, HS - 3 * g)
                        k = (6 * t + g) % 5
                        dve.wait_ge(*full[k].at(("E", b, t, g)))
                        hs = slice(3 * g, 3 * g + n)
                        step(dve, dve_step, dve.tensor_reduce(mx[:, 0, hs], ps[:, k, 0:n * S].rearrange("p (a b) -> p a b", a=n), AX, ALU.max))
                        dve.tensor_scalar(mx[:, 1, hs], mx[:, 0, hs], -DS ** -0.5, None, ALU.mult).then_inc(*e_max.mark((b, t, g)))
                    for m in range(1, 8, 2):
                        dve.wait_ge(*full[7].at(("E", b, t, m)))
                        dve.tensor_copy(pt2[0:SH, 1, :], ps[0:SH, 7, :]).then_inc(*e_turn_d.mark((b, t, m)))
                        read(dve, 7, e_turn_d, (b, t, m))
                    dve.wait_ge(*full[5].at(("E", b, t, "o")))
                    o = ps[:, 5, 0:144].rearrange("p (h d) -> p h d", d=9)
                    step(dve, dve_step, dve.reciprocal(rd, o[:, :, 8]))
                    dve.tensor_tensor(atok.rearrange("p (h d) -> p h d", d=DS), o[:, :, 0:DS], rd.unsqueeze(2).to_broadcast([128, HS, DS]),
                                      ALU.mult).then_inc(*e_norm.mark((b, t)))
                    read(dve, 5, e_norm, (b, t))
                out_dve(dve, "E", b, Eb[:, 3:4])
        vv_one = sg("vv_one")

        a4 = Area()
        o = a4(N)
        Dw = a4(4, C)
        Db = a4(20)
        bv = a4(C)
        omr = a4(DS)
        OmS = a4(512)
        Bn = a4(512)
        Om = a4(512)
        DW1 = a4(DFF)
        DW2 = a4(4, C)
        dq = a4(2, T)
        dsq = a4(2, T)
        Qf = a4(4, T)
        Kf = a4(4, T)
        Kt = a4(3, 512)
        V1 = a4(NT, HS * 9)
        st = a4(3, 144)
        own = a4(144)
        sT = a4(4, 512)
        da = a4(128)
        dd = a4(2, HS)
        dT_ = a4(T)
        h0 = a4(B, T)
        h1 = a4(B, T)
        rel = a4(4, T)
        d_in, d_q, d_k, d_v, d_sq, d_om = sg("d_in"), sg("d_q"), sg("d_k"), sg("d_v"), sg("d_sq"), sg("d_om")
        phi, ktok, state, masked, d_norm, d_turn = sg("phi"), sg("ktok"), sg("state"), sg("masked"), sg("d_norm"), sg("d_turn")
        res1, affine, relued, res2, d_used = sg("res1"), sg("affine"), sg("relued"), sg("res2"), sg("d_used")
        d_const, d_loaded = raw("d_const"), raw("d_loaded")

        def d_pe_layer(pe, L):
            pe.wait_ge(d_loaded, L * (16 * 7) + 16 * 7)
            pe.wait_ge(*d_om.at("om"))
            for b in range(B):
                pe.wait_ge(*d_in.at(b))
                for j in range(2):
                    take(pe, j)
                    pe.matmul(ps[:, j, :], Dw[:, j, :], o[:, cols(b)], start=True, stop=True).then_inc(*full[j].mark(("D", b, j)))
                take(pe, 2)
                for t in range(NT):
                    pe.matmul(ps[:, 2, 128 * t:128 * t + 128], o[:, T * b + 128 * t:T * b + 128 * t + 128], Dw[:, 2, :], start=True, stop=False)
                    last = pe.matmul(ps[:, 2, 128 * t:128 * t + 128], ones[0:1, :], bv[0:1, :], start=False, stop=True)
                last.then_inc(*full[2].mark(("D", b, 2)))
                for j, done in enumerate((d_q, d_k)):
                    pe.wait_ge(*done.at(b))
                    pe.wait_ge(*d_sq.at((b, j)))
                    for g in range(4):
                        k = 3 + (4 * j + g) % 5
                        take(pe, k)
                        pe.matmul(ps[:, k, :], Om[:, 128 * g:128 * g + 128], dq[:, j, :], start=True, stop=False)
                        pe.matmul(ps[:, k, :], Bn[:, 128 * g:128 * g + 128], dsq[:, j, :], start=False, stop=True)\
                            .then_inc(*full[k].mark(("D", b, "phi", j, g)))
                for ch in range(3):
                    take(pe, ch)
                    sl = slice(128 * ch, 128 * ch + 128)
                    pe.matmul(ps[:, ch, :], dq[:, 1, sl], Om, start=True, stop=False)
                    pe.matmul(ps[:, ch, :], dsq[:, 1, sl], Bn, start=False, stop=True).then_inc(*full[ch].mark(("D", b, "kt", ch)))
                pe.wait_ge(*d_v.at(b))
                for ch in range(3):
                    k = 3 + ch
                    pe.wait_ge(*ktok.at((b, ch)))
                    take(pe, k)
                    for g in range(4):
                        last = pe.matmul(ps[:, k, 36 * g:36 * g + 36], Kt[:, ch, 128 * g:128 * g + 128], V1[:, ch, 36 * g:36 * g + 36],
                                         start=True, stop=True)
                    last.then_inc(*full[k].mark(("D", b, "st", ch)))
                for ch in range(NT):
                    sl = slice(128 * ch, 128 * ch + 128)
                    pe.wait_ge(*phi.at((b, 1, 3)))
                    for r in range(4):
                        take(pe, r)
                    for g in range(4):
                        for r in range(4):
                            last = pe.matmul(ps[:, r, 128 * g:128 * g + 128], Kf[32 * r:32 * r + 16, g, sl], Qf[32 * r:32 * r + 16, g, sl],
                                             start=True, stop=True, tile_position=(32 * r, 0))
                            if g == 3:
                                last.then_inc(*full[r].mark(("D", b, ch, r)))
                    k = 6 + ch % 2
                    take(pe, k)
                    if ch > 0:
                        pe.wait_ge(*state.at((b, ch - 1)))
                        for g in range(4):
                            pe.matmul(ps[:, k, 36 * g:36 * g + 36], Qf[:, g, sl], st[:, ch - 1, 36 * g:36 * g + 36],
                                      start=g == 0, stop=False)
                    for r in range(4):
                        pe.wait_ge(*masked.at((b, ch, r)))
                        for g in range(4):
                            h = 4 * g + r
                            last = pe.matmul(ps[:, k, 9 * h:9 * h + 9], sT[:, r, 128 * g:128 * g + 128], V1[:, ch, 9 * h:9 * h + 9],
                                             start=ch == 0, stop=ch == 0 or (r, g) == (3, 3))
                    last.then_inc(*full[k].mark(("D", b, "num", ch)))
                    pe.wait_ge(*d_norm.at((b, ch)))
                    take(pe, k)
                    pe.transpose(ps[:, k, 0:128], da, ident[:, :]).then_inc(*full[k].mark(("D", b, "a", ch)))
                pe.wait_ge(*d_turn.at((b, NT - 1)))
                take(pe, 4)
                pe.matmul(ps[:, 4, :], Dw[:, 3, :], dT_, start=True, stop=True).then_inc(*full[4].mark(("D", b, "wo")))
            for b in range(B):
                norm_pe(pe, "D1", b, b, h0[:, b, :], wait=(res1.at(b),))
            for b in range(B):
                pe.wait_ge(*affine.at((b, 1)))
                for f_ in range(4):
                    k = 2 + f_
                    take(pe, k)
                    pe.matmul(ps[:, k, :], DW1[:, 128 * f_:128 * f_ + 128], h1[:, b, :], start=True, stop=True).then_inc(*full[k].mark(("D", b, "f", f_)))
                take(pe, 6)
                for f_ in range(4):
                    pe.wait_ge(*relued.at((b, f_)))
                    last = pe.matmul(ps[:, 6, :], DW2[:, f_, :], rel[:, f_, :], start=f_ == 0, stop=f_ == 3)
                last.then_inc(*full[6].mark(("D", b, "f2")))
            for b in range(B):
                norm_pe(pe, "D2", b, b, h0[:, b, :], wait=(res2.at(b),))

        def d_pe(pe):
            for b in range(B):
                norm_pe(pe, "D0", b, b, x[:, cols(b)], wait=(x_new.at(("C", b)),))
            pe.wait_ge(d_const, 48)
            with layers(pe, "D") as L:
                d_pe_layer(pe, L)

        def d_act_layer(act, L):
            act.wait_ge(*d_om.at("om"))
            for b in range(B):
                for j, done in enumerate((d_q, d_k)):
                    act.wait_ge(*full[j].at(("D", b, j)))
                    act.activation(dq[:, j, :], ps[:, j, :], ACT.Identity, bias=Db[:, 12 + j:13 + j], scale=DS ** -0.25).then_inc(*done.mark(b))
                    read(act, j, done, b)
                    act.activation(dsq[:, j, :], dq[:, j, :], ACT.Square).then_inc(*d_sq.mark((b, j)))
                act.wait_ge(*full[2].at(("D", b, 2)))
                act.activation(V1.rearrange("p t (h d) -> p t h d", d=9)[:, :, :, 0:DS],
                               ps[:, 2, :].rearrange("p (t h d) -> p t h d", t=NT, d=DS), ACT.Copy).then_inc(*d_v.mark(b))
                read(act, 2, d_v, b)
                for j in range(2):
                    for g in range(4):
                        k = 3 + (4 * j + g) % 5
                        act.wait_ge(*full[k].at(("D", b, "phi", j, g)))
                        act.activation((Qf, Kf)[j][:, g, :], ps[:, k, :], ACT.Exp, bias=eps5[:, 2:3]).then_inc(*phi.mark((b, j, g)))
                        read(act, k, phi, (b, j, g))
                for ch in range(3):
                    act.wait_ge(*full[ch].at(("D", b, "kt", ch)))
                    act.activation(Kt[:, ch, :], ps[:, ch, :], ACT.Exp, bias=eps5[:, 2:3]).then_inc(*ktok.mark((b, ch)))
                    read(act, ch, ktok, (b, ch))
                for ch in range(NT):
                    k = 6 + ch % 2
                    act.wait_ge(*full[k].at(("D", b, "a", ch)))
                    act.activation(dT_[:, 128 * ch:128 * ch + 128], ps[:, k, 0:128], ACT.Copy).then_inc(*d_turn.mark((b, ch)))
                    read(act, k, d_turn, (b, ch))
            for b in range(B):
                norm_act(act, "D1", b, b, None, 0)
            for b in range(B):
                act.wait_ge(*normed.at(("D1", b)))
                act.activation(h1[:, b, :], xn[:, b, :], ACT.Identity, bias=Db[:, 4:5], scale=Db[:, 3:4]).then_inc(*affine.mark((b, 1)))
                for f_ in range(4):
                    k = 2 + f_
                    act.wait_ge(*full[k].at(("D", b, "f", f_)))
                    if b == 1 and f_ == 0:
                        act.wait_ge(*full[6].at(("D", 0, "f2")))
                    act.activation(rel[:, f_, :], ps[:, k, :], ACT.Relu, bias=Db[:, 8 + f_:9 + f_]).then_inc(*relued.mark((b, f_)))
                    read(act, k, relued, (b, f_))
            for b in range(B):
                norm_act(act, "D2", b, b, None, 0)
            for b in range(B):
                act.wait_ge(*normed.at(("D2", b)))
                act.activation(o[:, cols(b)], xn[:, b, :], ACT.Identity, bias=Db[:, 6:7], scale=Db[:, 5:6]).then_inc(*affine.mark((b, 2)))
            act.wait_ge(*affine.at((1, 2)))
            act.sem_inc(d_used.mark("layer")[0], 1)

        def d_act(act):
            for b in range(B):
                norm_act(act, "D0", b, b, None, 0)
            with layers(act, "D") as L:
                d_act_layer(act, L)

        def d_dve_layer(dve, L):
            dve.wait_ge(d_loaded, L * (16 * 7) + 16 * 7)
            step(dve, dve_step, dve.tensor_scalar(Db[:, 12:14], Db[:, 0:2], DS ** -0.25, None, ALU.mult))
            dve.tensor_tensor(Om.rearrange("p (a d) -> p a d", d=DS), OmS.rearrange("p (a d) -> p a d", d=DS),
                              omr.unsqueeze(1).to_broadcast([128, 64, DS]), ALU.mult).then_inc(*d_om.mark("om"))
            for b in range(B):
                dve.wait_ge(*d_om.at("om"))
                dve.sem_inc(d_in.mark(b)[0], 1)
                for ch in range(3):
                    k = 3 + ch
                    dve.wait_ge(*full[k].at(("D", b, "st", ch)))
                    ins = dve.tensor_tensor(st[:, ch, :], ps[:, k, 0:144], own, ALU.mult)
                    if ch > 0:
                        step(dve, dve_step, ins)
                        ins = dve.tensor_tensor(st[:, ch, :], st[:, ch - 1, :], st[:, ch, :], ALU.add)
                    ins.then_inc(*state.mark((b, ch)))
                    read(dve, k, state, (b, ch))
                for ch in range(NT):
                    if ch > 0:
                        dve.wait_ge(*full[6 + (ch - 1) % 2].at(("D", b, "num", ch - 1)))
                    for r in range(4):
                        dve.wait_ge(*full[r].at(("D", b, ch, r)))
                        dve.tensor_tensor(sT[:, r, :].rearrange("p (g i) -> p g i", g=4), ps[:, r, :].rearrange("p (g i) -> p g i", g=4),
                                          tri.unsqueeze(1).to_broadcast([128, 4, 128]), ALU.mult).then_inc(*masked.mark((b, ch, r)))
                        read(dve, r, masked, (b, ch, r))
                    k = 6 + ch % 2
                    dve.wait_ge(*full[k].at(("D", b, "num", ch)))
                    nd = ps[:, k, 0:144].rearrange("p (h d) -> p h d", d=9)
                    step(dve, dve_step, dve.tensor_scalar(dd[:, 0, :], nd[:, :, 8], 1e-6, None, ALU.add))
                    step(dve, dve_step, dve.reciprocal(dd[:, 1, :], dd[:, 0, :]))
                    if ch > 0:
                        dve.wait_ge(*full[6 + (ch - 1) % 2].at(("D", b, "a", ch - 1)))
                    dve.tensor_tensor(da.rearrange("p (h d) -> p h d", d=DS), nd[:, :, 0:DS],
                                      dd[:, 1, :].unsqueeze(2).to_broadcast([128, HS, DS]), ALU.mult).then_inc(*d_norm.mark((b, ch)))
                    read(dve, k, d_norm, (b, ch))
                dve.wait_ge(*full[4].at(("D", b, "wo")))
                dve.scalar_tensor_tensor(h0[:, b, :], ps[:, 4, :], Db[:, 2:3], o[:, cols(b)], ALU.add, ALU.add).then_inc(*res1.mark(b))
                read(dve, 4, res1, b)
            for b in range(B):
                norm_dve(dve, "D1", b, b, h0[:, b, :])
            for b in range(B):
                dve.wait_ge(*affine.at((b, 1)))
                dve.wait_ge(*full[6].at(("D", b, "f2")))
                dve.scalar_tensor_tensor(h0[:, b, :], ps[:, 6, :], Db[:, 7:8], h1[:, b, :], ALU.add, ALU.add).then_inc(*res2.mark(b))
                read(dve, 6, res2, b)
            for b in range(B):
                norm_dve(dve, "D2", b, b, h0[:, b, :])
            dve.wait_ge(*affine.at((1, 2)))

        def d_dve(dve):
            step(dve, dve_step, dve.memset(V1, 1.0))
            for b in range(B):
                norm_dve(dve, "D0", b, b, x[:, cols(b)], out_=o[:, cols(b)])
                dve.wait_ge(*normed.at(("D0", b)))
            dve.wait_ge(d_const, 48)
            with layers(dve, "D") as L:
                d_dve_layer(dve, L)
            for b in range(B):
                dve.tensor_tensor(x[:, cols(b)], x[:, cols(b)], o[:, cols(b)], ALU.add).then_inc(*x_new.mark(("D", b)))

        def d_weights(sp, l):
            def at_(name, w):
                return A[name][bass.ds(l * 128, 128), :]
            for dst, name in ((Dw.rearrange("p a b -> p (a b)"), "D_w"), (Db[:, 0:12], "D_b"), (omr, "D_om"), (DW1, "D_w1"),
                              (DW2.rearrange("p a b -> p (a b)"), "D_w2")):
                sp.dma_start(dst, A[name][bass.ds(l * 128, 128), :]).then_inc(d_loaded, 16)
            sp.dma_start(bv[0:1, 0:64], A["D_bv"][bass.ds(l, 1), 0:64]).then_inc(d_loaded, 16)
            sp.dma_start(bv[0:1, 64:128], A["D_bv"][bass.ds(l, 1), 64:128]).then_inc(d_loaded, 16)

        def d_sp(sp):
            sp.wait_ge(*x_new.at(("C", 1)))
            sp.dma_start(OmS, A["OmS"]).then_inc(d_const, 16)
            sp.dma_start(Bn, A["Bn"]).then_inc(d_const, 16)
            sp.dma_start(own, A["own"]).then_inc(d_const, 16)
            d_weights(sp, 0)
            with layers(sp, "D", LAYERS - 1) as L:
                sp.wait_ge(*d_used.at("layer"))
                d_weights(sp, L + 1)

        f_tab, f_used, ga, gg, f_mul = sg("f_tab"), sg("f_used"), sg("ga"), sg("gg"), sg("f_mul")
        f_const, fa_loaded, ff_loaded, fa_used = raw("f_const"), raw("fa_loaded"), raw("ff_loaded"), sg("fa_used")

        def f_pe_layer(pe, L):
            pe.wait_ge(fa_loaded, L * 48 + 48)
            attn_pe(pe, "F", lambda b: xsh[:, b, :], True)
            pe.wait_ge(ff_loaded, L * 80 + 80)
            for b in range(B):
                norm_pe(pe, "F1", b, b, xsh[:, b, :], wait=(shifted.at(("F2", b)),))
            for b in range(B):
                pe.wait_ge(*affine.at(("F", b)))
                for i, (c0, m) in enumerate(DIC):
                    for j in range(2):
                        k = 2 * i + j
                        take(pe, k)
                        pe.matmul(ps[0:m, k, :], W1[:, DI * j + c0:DI * j + c0 + m], xn[:, b, :], start=True, stop=True)\
                            .then_inc(*full[k].mark(("F", b, "f", k)))
                take(pe, 6)
                for i, (c0, m) in enumerate(DIC):
                    pe.wait_ge(*f_mul.at((b, i)))
                    last = pe.matmul(ps[:, 6, :], W2[0:m, i, :], fh[0:m, i, :], start=i == 0, stop=i == 2)
                last.then_inc(*full[6].mark(("F", b, "f2")))

        def f_pe(pe):
            for b in range(B):
                norm_pe(pe, "F0", b, b, x[:, cols(b)], wait=(x_new.at(("E", b)),))
            pe.wait_ge(f_const, 48)
            with layers(pe, "F") as L:
                f_pe_layer(pe, L)

        def f_act_layer(act, L):
            attn_act(act, "F", True)
            for b in range(B):
                norm_act(act, "F1", b, b, None, 0)
            for b in range(B):
                act.wait_ge(*normed.at(("F1", b)))
                act.activation(xn[:, b, :], xn[:, b, :], ACT.Identity, bias=lng[:, 1:2], scale=lng[:, 0:1]).then_inc(*affine.mark(("F", b)))
            for b in range(B):
                for i, (c0, m) in enumerate(DIC):
                    k = 2 * i + 1
                    act.wait_ge(*full[k].at(("F", b, "f", k)))
                    if b == 1:
                        act.wait_ge(*f_mul.at((0, i)))
                    act.activation(fg[0:m, i, :], ps[0:m, k, :], ACT.Gelu, bias=b1[0:m, 3 + i:4 + i]).then_inc(*gg.mark((b, i)))
                    read(act, k, gg, (b, i))
            act.preload_act_table_set("natural_log_exp_and_others")

        def f_act(act):
            for b in range(B):
                norm_act(act, "F0", b, b, None, 0)
            act.preload_act_table_set("natural_log_exp_and_others")
            with layers(act, "F") as L:
                f_act_layer(act, L)

        xsh = sb("xsh", [128, B, T])
        aside = sb("aside", [128, B, T])

        def shift_dve(dve, key, b):
            step(dve, dve_step, dve.tensor_copy(xsh[0:64, b, :], x[0:64, cols(b)]))
            dve.tensor_copy(xsh[64:128, b, 1:T], x[64:128, T * b:T * b + T - 1]).then_inc(*shifted.mark((key, b)))

        def f_dve_layer(dve, L):
            dve.wait_ge(fa_loaded, L * 48 + 48)
            for j in range(4):
                ins = dve.tensor_scalar(tab[:, j, :], tab0[:, j, :], scl[:, j:j + 1], None, ALU.mult)
            step(dve, dve_step, ins)
            for b in range(B):
                shift_dve(dve, "F1", b)
            attn_dve(dve, "F", True)
            for b in range(B):
                dve.wait_ge(*x_new.at(("F", b)))
                shift_dve(dve, "F2", b)
                dve.wait_ge(*shifted.at(("F2", b)))
            for b in range(B):
                norm_dve(dve, "F1", b, b, xsh[:, b, :])
            dve.wait_ge(ff_loaded, L * 80 + 80)
            for b in range(B):
                for i, (c0, m) in enumerate(DIC):
                    k = 2 * i
                    dve.wait_ge(*full[k].at(("F", b, "f", k)))
                    dve.wait_ge(*gg.at((b, i)))
                    if b == 1:
                        dve.wait_ge(*full[6].at(("F", 0, "f2")))
                    dve.scalar_tensor_tensor(fh[0:m, i, :], ps[0:m, k, :], b1[0:m, i:i + 1], fg[0:m, i, :], ALU.add, ALU.mult)\
                        .then_inc(*f_mul.mark((b, i)))
                    read(dve, k, f_mul, (b, i))
                dve.wait_ge(*full[6].at(("F", b, "f2")))
                dve.scalar_tensor_tensor(x[:, cols(b)], ps[:, 6, :], lng[:, 2:3], x[:, cols(b)], ALU.add, ALU.add).then_inc(*x_new.mark(("Ff", b)))
                read(dve, 6, x_new, ("Ff", b))
            dve.sem_inc(f_used.mark("layer")[0], 1)

        def f_dve(dve):
            step(dve, dve_step, dve.memset(xsh[:, :, :], 0.0))
            step(dve, dve_step, dve.memset(P, 0.0))
            for b in range(B):
                norm_dve(dve, "F0", b, b, x[:, cols(b)])
                dve.tensor_copy(aside[:, b, :], x[:, cols(b)]).then_inc(*x_new.mark(("aside", b)))
                dve.wait_ge(*x_new.at(("aside", b)))
                dve.wait_ge(*normed.at(("F0", b)))
                dve.tensor_copy(x[:, cols(b)], xn[:, b, :]).then_inc(*x_new.mark(("F0", b)))
                dve.wait_ge(*x_new.at(("F0", b)))
            dve.wait_ge(f_const, 48)
            with layers(dve, "F") as L:
                f_dve_layer(dve, L)
            for b in range(B):
                dve.wait_ge(*x_new.at(("Ff", b)))
                dve.tensor_tensor(x[:, cols(b)], x[:, cols(b)], aside[:, b, :], ALU.add).then_inc(*x_new.mark(("F_end", b)))

        def f_pool(pool):
            with layers(pool, "F") as L:
                attn_pool(pool, "F")

        def fa_weights(sp, l):
            for dst, name in ((Wqkv.rearrange("p a b -> p (a b)"), "F_w"), (scl, "F_scl"), (Wo.rearrange("p a b -> p (a b)"), "F_wo")):
                sp.dma_start(dst, A[name][bass.ds(l * 128, 128), :]).then_inc(fa_loaded, 16)

        def ff_weights(sp, l):
            for dst, name in ((W1, "F_w1"), (W2.rearrange("p a b -> p (a b)"), "F_w2"), (b1, "F_b1"), (lng[:, 0:2], "F_ln"), (lng[:, 2:3], "F_b2")):
                sp.dma_start(dst, A[name][bass.ds(l * 128, 128), :]).then_inc(ff_loaded, 16)

        def f_sp(sp):
            sp.wait_ge(*x_new.at(("E", 1)))
            for dst, name in ((tab0, "tabF"), (seg, "seg"), (spread, "spread")):
                sp.dma_start(dst, A[name]).then_inc(f_const, 16)
            fa_weights(sp, 0)
            ff_weights(sp, 0)
            with layers(sp, "F", LAYERS - 1) as L:
                sp.wait_ge(*x_new.at(("F", 1)))
                fa_weights(sp, L + 1)
                sp.wait_ge(*f_used.at("layer"))
                ff_weights(sp, L + 1)
        block = c.enter_context(nc.Block())

        def load(eng, dst, src, sem):
            eng.dma_start(dst, src).then_inc(sem, 16)

        n_const = 18 * 16

        @block.sync
        def _(sp):
            lst = ((x[:, :], "x"), (mean_m[:, :], "mean_m"), (ident[:, :], "ident"), (identb[:, :], "identb"),
                   (band[:, :], "band"), (ones[:, :], "ones"), (eps5[:, :], "eps5"), (tab0, "tab0"), (Wqkv, "A_w"),
                   (Wo, "A_wo"), (ctxT, "ctx"), (Bw, "B_w"), (Bb, "B_b"), (Ew, "E_w"), (Eb, "E_b"), (hmask, "hmask"),
                   (Cw, "C_w"), (tri, "tri"))
            for dst, name in lst:
                load(sp, dst, A[name], const_in)
            if STAGE >= 4:
                d_sp(sp)
            if STAGE >= 6:
                f_sp(sp)
            sp.wait_ge(*x_new.at((LAST if STAGE < 6 else "F_end", 1)))
            sp.dma_start(out, x[:, :]).then_inc(stored, 16)
            sp.wait_ge(stored, 16)

        @block.tensor
        def _(pe):
            pe.wait_ge(const_in, n_const)
            for b in range(B):
                norm_pe(pe, "A1", b, b, x[:, cols(b)])
            for b in range(B):
                norm_pe(pe, "A2", b, b, None, center=False)
            attn_pe(pe, "A", lambda b: xn[:, b, :], False)
            if STAGE >= 2:
                b_pe(pe)
            if STAGE >= 3:
                c_pe(pe)
            if STAGE >= 4:
                d_pe(pe)
            if STAGE >= 5:
                e_pe(pe, "D")
            if STAGE >= 6:
                f_pe(pe)

        @block.scalar
        def _(act):
            act.preload_act_table_set("natural_log_exp_and_others")
            act.wait_ge(const_in, n_const)
            for b in range(B):
                norm_act(act, "A1", b, b, None, 0)
            for b in range(B):
                norm_act(act, "A2", b, b, xn[:, b, :], 1, center=False, wait=(normed.at(("A1", b)),))
            attn_act(act, "A", False)
            if STAGE >= 2:
                b_act(act)
            if STAGE >= 3:
                c_act(act)
            if STAGE >= 4:
                d_act(act)
            if STAGE >= 5:
                act.wait_ge(*vv_one.at("ones"))
                e_act(act)
            if STAGE >= 6:
                f_act(act)

        @block.vector
        def _(dve):
            step(dve, dve_step, dve.memset(P, 0.0))
            dve.wait_ge(const_in, n_const)
            for b in range(B):
                norm_dve(dve, "A1", b, b, x[:, cols(b)])
            for b in range(B):
                norm_dve(dve, "A2", b, b, xn[:, b, :], center=False)
            attn_dve(dve, "A", False)
            if STAGE >= 2:
                b_dve(dve)
            if STAGE >= 3:
                c_dve(dve)
            if STAGE >= 4:
                d_dve(dve)
            if STAGE >= 5:
                e_dve(dve)
            if STAGE >= 6:
                f_dve(dve)

        @block.gpsimd
        def _(pool):
            attn_pool(pool, "A")
            if STAGE >= 6:
                f_pool(pool)
        print([(taken[k].n, free[k].n) for k in range(8)])


def swapped(w):
    w = w.reshape(*w.shape[:-1], H, 2, D // 2)
    return w[..., ::-1, :].reshape(*w.shape[:-3], INNER)

def five(w):
    q, k, v = (w[..., i * INNER:(i + 1) * INNER] for i in range(3))
    import numpy as np
    return np.stack([q, k, v, swapped(q), swapped(k)], -2)


def more(a, f, np):
    w = lambda p: np.stack([f(p + n).T for n in ("Wq", "Wk", "Wv", "Wo")], 1)
    bb = lambda p: np.stack([f(p + n) for n in ("bq", "bk", "bv", "bo")], 1)
    a["ctx"] = f("ctx_1024").transpose(2, 0, 1)
    a["B_w"], a["B_b"] = w("L0_xattn_"), bb("L0_xattn_")
    a["E_w"], a["E_b"] = w("L1_xattn_"), bb("L1_xattn_")
    a["hmask"] = (np.arange(128)[:, None] // DS == np.arange(HS)[None, :]).astype(np.float32)
    cw = np.zeros((128, 70 * FB), np.float32)
    for j, n in enumerate(("gate", "up")):
        for ch in range(3):
            part = f("L0_ffn_w_" + n)[128 * ch:128 * ch + 128]
            cw[:len(part), 384 * j + 128 * ch:384 * j + 128 * ch + 128] = part
    cw[:, 768:] = f("L0_ffn_w_down")
    a["C_w"] = cw.reshape(128, 70, FB)
    i = np.arange(128)
    a["tri"] = (i[:, None] <= i[None, :]).astype(np.float32)
    lay = lambda name: f("L1_attn_" + name)
    rows = lambda v: v.reshape(-1, v.shape[-1])
    L = LAYERS
    a["D_w"] = rows(np.stack([lay(n) for n in ("Wq", "Wk", "Wv", "Wo")], 2).reshape(L, 128, 512))
    a["D_b"] = rows(np.concatenate([np.stack([lay(n) for n in ("bq", "bk", "bo", "g1", "be1", "g2", "be2", "bf2")], 2),
                                    lay("bf1").reshape(L, 4, 128).transpose(0, 2, 1)], 2))
    a["D_bv"] = lay("bv")
    a["D_om"] = rows(np.tile(lay("omega"), (1, HS, 1)))
    a["D_w1"] = rows(lay("W1"))
    a["D_w2"] = rows(lay("W2").reshape(L, 4, 128, 128).transpose(0, 2, 1, 3).reshape(L, 128, 512))
    same = np.arange(128)[:, None] // DS == np.arange(512)[None, :] // 32
    slot = np.arange(512)[None, :] % 32
    a["OmS"] = (same * np.where(slot < 8, 1.0, np.where(slot < 16, -1.0, 0.0))).astype(np.float32)
    a["Bn"] = (same * np.where(slot < 16, -0.5, 0.0)).astype(np.float32)
    p_, c_ = np.arange(128)[:, None], np.arange(144)[None, :]
    a["own"] = ((p_ // 32 == c_ // 9 % 4) & (p_ % 32 < 16)).astype(np.float32)
    g = lambda name: f("L1_ffn_" + name)
    a["F_w"] = rows(five(g("Wqkv")).reshape(L, 128, 5 * INNER))
    a["F_wo"] = rows(g("Wo").reshape(L, NP, 128, C).transpose(0, 2, 1, 3).reshape(L, 128, NP * C))
    sw = lambda v: np.concatenate([v[:, D // 2:], v[:, :D // 2]], 1)
    qs_, ks_ = g("q_scale"), g("k_scale")
    a["F_scl"] = rows(np.stack([np.tile(v, (1, 2)) for v in (qs_, sw(qs_), ks_, sw(ks_))], 2))
    a["F_w1"] = rows(g("W1"))

    def parts(v):
        z = np.zeros((L, 3 * 128, v.shape[2]), np.float32)
        z[:, :DI] = v
        return z.reshape(L, 3, 128, -1).transpose(0, 2, 1, 3)
    a["F_w2"] = rows(parts(g("W2")).reshape(L, 128, 3 * C))
    a["F_b1"] = rows(np.concatenate([parts(g("b1")[:, :DI, None])[..., 0], parts(g("b1")[:, DI:, None])[..., 0]], 2))
    a["F_ln"] = rows(np.stack([g("ln_g"), g("ln_b")], 2))
    a["F_b2"] = rows(g("b2")[:, :, None])
    seg = np.zeros((128, NP, H), np.float32)
    spread = np.zeros((128, NP, 128), np.float32)
    for p in range(NP):
        for j in range(2):
            seg[64 * j:64 * j + 64, p, 2 * p + j] = 1
            spread[2 * p + j, p, 64 * j:64 * j + 64] = 1
    a["seg"], a["spread"] = seg, spread



def kernel(**inp):
    import numpy as np
    import concourse.bacc as bacc
    from concourse.bass_utils import run_bass_kernel_spmd as run

    f = lambda name: np.asarray(inp[name])
    a = {}
    a["x"] = f("x").reshape(N, C).T
    a["mean_m"] = np.full((128, 128), 1 / 128, np.float32)
    a["ident"] = np.eye(128, dtype=np.float32)
    import ml_dtypes
    a["identb"] = np.eye(128).astype(ml_dtypes.bfloat16)
    q, k = np.arange(128)[:, None], np.arange(160)[None, :]
    a["band"] = np.where((k >= q) & (k <= q + WIN), 0.0, NEG).astype(ml_dtypes.bfloat16)
    a["ones"] = np.ones((1, 128), np.float32)
    e = np.zeros((128, 4), np.float32)
    e[:] = [1e-5, 1e-6, math.log(0.25), 10 * math.log(2)]
    a["eps5"] = e
    half = np.arange(0, D, 2, dtype=np.float32)
    freqs = np.arange(T, dtype=np.float32)[:, None] * (1.0 / 10000.0 ** (half / D)).astype(np.float32)[None, :]
    cos, sin = np.cos(freqs).T, np.sin(freqs).T
    cos2 = np.concatenate([cos] * 4, 0)
    sin2 = np.concatenate([-sin, sin] * 2, 0)
    a["tab0"] = np.stack([cos2, sin2, cos2, sin2], 1).astype(np.float32)
    base = (half + 0.4 * D) / (1.4 * D)
    power = (np.arange(T, dtype=np.float32) - T // 2) / (WIN // 2)
    sc = (base[:, None] ** power[None, :]).astype(np.float32)
    sc = np.concatenate([sc] * 4, 0)
    a["tabF"] = np.stack([cos2 * sc, sin2 * sc, cos2 / sc, sin2 / sc], 1).astype(np.float32)

    a["A_w"] = five(f("L0_attn_w_qkv").T)
    a["A_wo"] = f("L0_attn_w_out").T.reshape(NP, 128, C).transpose(1, 0, 2)
    more(a, f, np)
    a = {k: np.ascontiguousarray(v) for k, v in a.items()}
    book = {}
    for turn in range(2):
        nc = bacc.Bacc("TRN2", target_bir_lowering=False, num_devices=1)
        A = {k: nc.dram_tensor(f"in_{k}", v.shape, mybir.dt.from_np(v.dtype), kind="ExternalInput").ap() for k, v in a.items()}
        out = nc.dram_tensor("out_x", (128, N), F32, kind="ExternalOutput").ap()
        build(nc, A, out, book)
    r = run(nc, [{f"in_{k}": v for k, v in a.items()}], core_ids=[0])
    return np.ascontiguousarray(r.results[0]["out_x"].T).reshape(B, T, C)
```

```python
import math
from contextlib import ExitStack, contextmanager

import concourse.bass as bass
from concourse import mybir

F32 = mybir.dt.float32
BF16 = mybir.dt.bfloat16
ALU = mybir.AluOpType
ACT = mybir.ActivationFunctionType
AX = mybir.AxisListType.X

B, T, C = 2, 512, 128
N = B * T
NT = T // 128
S = 154
SH = S // 2
H, D = 16, 64
NP = H // 2
WIN = 32
INNER = H * D
TOPK = 32
I0 = 352
FB = 16
HS, DS = 16, 8
DFF = 512
LAYERS = 6
DI = int(128 * 4 * 2 / 3)
DIC = [(0, 128), (128, 128), (256, DI - 256)]
NEG = -1e30
STAGE = 6
LAST = 'ABCDEF'[STAGE - 1]


class Signal:
    every = []

    def __init__(self, book, name, sem):
        self.book = book.setdefault(name, {"key": {}, "per": {}})
        self.sem, self.name, self.n = sem, name, 0
        self.seen = set()
        Signal.every.append(self)

    def mark(self, key=None):
        self.n += 1
        if key is not None:
            assert key not in self.seen, key
            self.seen.add(key)
            self.book["key"][key] = (Loop.now, self.n)
        return self.sem, 1

    def value(self, loop, n):
        if loop is None:
            return n
        per = self.book["per"].get(loop, 0)
        if Loop.now == loop:
            return Loop.reg * per + n if per else n
        return n + (LAYERS - 1) * per

    def at(self, key):
        loop, n = self.book["key"].get(key, (None, 1))
        return self.sem, self.value(loop, n)


class Loop:
    now, reg = None, None


@contextmanager
def layers(eng, name, trips=LAYERS):
    before = {s: s.n for s in Signal.every}
    with eng.Fori(0, trips) as reg:
        Loop.now, Loop.reg = name, reg
        yield reg
    for s, n in before.items():
        if s.n != n:
            s.book["per"][name] = s.n - n
            s.n = n + trips * (s.n - n)
    Loop.now = None


def build(nc, A, out, book, stage=99):
    Signal.every = []
    nc.disable_value_cache = True
    with ExitStack() as c:
        def sb(name, shape, dt=F32):
            return c.enter_context(nc.sbuf_tensor(name, shape, dt))

        def sg(name):
            return Signal(book, name, c.enter_context(nc.semaphore(name)))

        def raw(name):
            return c.enter_context(nc.semaphore(name))

        ps = c.enter_context(nc.psum_tensor("ps", [128, 8, 512], F32))

        x = sb("x", [128, N])
        mean_m = sb("mean_m", [128, 128])
        ident = sb("ident", [128, 128])
        identb = sb("identb", [128, 128], BF16)
        band = sb("band", [128, 480], BF16)
        ones = sb("ones", [1, 128])
        eps5 = sb("eps5", [128, 4])
        xc = sb("xc", [128, B, T])
        sq = sb("sq", [128, B, T])
        rs = sb("rs", [128, B, T])
        xn = sb("xn", [128, B, T])
        big = sb("big", [128, 40000])

        class Area:
            def __init__(self):
                self.at = 0

            def __call__(self, *dims):
                n = math.prod(dims)
                v = big[:, self.at:self.at + n]
                self.at += n
                assert self.at <= 40000, self.at
                if len(dims) == 2:
                    return v.rearrange("p (a b) -> p a b", a=dims[0])
                if len(dims) == 3:
                    return v.rearrange("p (a b c) -> p a b c", a=dims[0], b=dims[1])
                return v

        loaded = {}
        full = [sg(f"full{k}") for k in range(8)]
        free = [sg(f"free{k}") for k in range(8)]
        taken = [Signal(book, f"taken{k}", None) for k in range(8)]
        dve_step, act_step, pool_step = sg("dve_step"), sg("act_step"), sg("pool_step")
        const_in, stored = raw("const_in"), raw("stored")
        centred, squared, rooted, normed = sg("centred"), sg("squared"), sg("rooted"), sg("normed")
        x_new = sg("x_new")
        S_ = {}

        def take(pe, *banks):
            for k in banks:
                t = taken[k]
                per = t.book["per"].get(Loop.now, 0) if Loop.now else 0
                v = (Loop.reg * per + t.n) if per else t.n
                if t.n > 0:
                    pe.wait_ge(free[k].sem, v)
                t.mark()

        def step(eng, sgn, ins, extra=None):
            ins.then_inc(*sgn.mark(("step", sgn.n)))
            eng.wait_ge(*sgn.at(("step", sgn.n - 1)))

        def read(eng, bank, sgn, key):
            eng.wait_ge(*sgn.at(key))
            eng.sem_inc(free[bank].mark()[0], 1)

        def norm_pe(pe, key, b, bank, src, wait=(), center=True):
            for w in wait:
                pe.wait_ge(*w)
            if center:
                take(pe, bank)
                pe.matmul(ps[:, bank, :], mean_m[:, :], src, start=True, stop=True).then_inc(*full[bank].mark((key, b, "mean")))
            pe.wait_ge(*squared.at((key, b)))
            take(pe, bank)
            pe.matmul(ps[:, bank, :], mean_m[:, :], sq[:, b, :], start=True, stop=True).then_inc(*full[bank].mark((key, b, "var")))

        def norm_dve(dve, key, b, bank, src, center=True, out_=None):
            if center:
                dve.wait_ge(*full[bank].at((key, b, "mean")))
                dve.tensor_tensor(xc[:, b, :], src, ps[:, bank, :], ALU.subtract).then_inc(*centred.mark((key, b)))
                dve.wait_ge(*centred.at((key, b)))
            dve.wait_ge(*rooted.at((key, b)))
            dve.tensor_tensor(xn[:, b, :] if out_ is None else out_, xc[:, b, :] if center else src, rs[:, b, :],
                              ALU.mult).then_inc(*normed.mark((key, b)))

        def norm_act(act, key, b, bank, src, eps, center=True, wait=()):
            if center:
                act.wait_ge(*centred.at((key, b)))
                act.sem_inc(free[bank].mark()[0], 1)
                act.activation(sq[:, b, :], xc[:, b, :], ACT.Square).then_inc(*squared.mark((key, b)))
            else:
                for w in wait:
                    act.wait_ge(*w)
                act.activation(sq[:, b, :], src, ACT.Square).then_inc(*squared.mark((key, b)))
            act.wait_ge(*full[bank].at((key, b, "var")))
            step(act, act_step, act.activation(rs[:, b, :], ps[:, bank, :], ACT.Ln, bias=eps5[:, eps:eps + 1]))
            act.sem_inc(free[bank].mark()[0], 1)
            act.activation(rs[:, b, :], rs[:, b, :], ACT.Exp, scale=-0.5).then_inc(*rooted.mark((key, b)))

        ar = Area()
        Wqkv = ar(5, INNER)
        Wo = ar(NP, C)
        QT = ar(NP, T)
        KT = ar(NP, T)
        V = ar(NT, INNER)
        OT = ar(NP, T)
        tab0 = ar(4, T)
        tab = ar(4, T)
        P = ar(3, 4, 256)
        PT = ar(2, 4, 128)
        PTb = ar(2, 4, 64)
        knr = ar(2, T)
        tmp = ar(2, 4, T)
        sqh = ar(4, T)
        rq = ar(NT, H)
        seg = ar(2)
        spread = ar(128)
        scl = ar(4)
        W1 = ar(2 * DI)
        W2 = ar(3, C)
        b1 = ar(6)
        fg = QT[:, 0:3, :]
        fh = QT[:, 3:6, :]
        lng = ar(3)
        nm = sb("nm", [128, 3, 16])
        QKV = ("q", "r", "k", "s")
        wsel = {"q": 0, "k": 1, "v": 2, "r": 3, "s": 4}
        roped, raised, v_ready, k_sq, q_sq = sg("roped"), sg("raised"), sg("v_ready"), sg("k_sq"), sg("q_sq")
        part1, part2 = sg("part1"), sg("part2")
        k_norm, q_norm, k_raised = sg("k_norm"), sg("q_norm"), sg("k_raised")
        guarded, turned_b = sg("guarded"), sg("turned_b")
        topped, exped, scaled, turned, merged = sg("topped"), sg("exped"), sg("scaled"), sg("turned"), sg("merged")
        tabs_ready, gated, shifted = sg("tabs_ready"), sg("gated"), sg("shifted")
        attn_loaded, ffn_loaded = raw("attn_loaded"), raw("ffn_loaded")

        UNITS = 2 * NP

        def unit(u):
            return u // 2, 2 * (u % 2), 2 * (u % 2)

        def attn_pe(pe, key, src, l2):
            for b in range(B):
                src_ready(pe, key, b)
                for p in range(NP + 1):
                    if p < NP:
                        for j, w in enumerate(QKV):
                            take(pe, j)
                            pe.matmul(ps[:, j, :], Wqkv[:, wsel[w], 128 * p:128 * p + 128], src(b), start=True, stop=True)\
                                .then_inc(*full[j].mark((key, b, p)))
                        t, hf = p // 2, p % 2
                        take(pe, 4)
                        pe.matmul(ps[:, 4, :], src(b)[:, 128 * t:128 * t + 128], Wqkv[:, 2, 512 * hf:512 * hf + 512],
                                  start=True, stop=True).then_inc(*full[4].mark((key, b, "v", p)))
                    if l2 and p > 0:
                        l2_pe(pe, key, b, p - 1)
                for u in range(UNITS + 3):
                    if u < UNITS:
                        p, t0, sl = unit(u)
                        pe.wait_ge(*roped.at((key, b, p, "q")))
                        pe.wait_ge(*(k_raised.at((key, b, p)) if l2 else roped.at((key, b, p, "k"))))
                        take(pe, sl, sl + 1)
                        for h in range(2):
                            m0 = 0 if t0 == 0 else 160
                            pe.matmul(ps[:, sl + h, 0:320], identb[:, :], band[:, m0:m0 + 320], start=True, stop=False)
                        for i in range(2):
                            t = t0 + i
                            k0 = WIN if t == 0 else 0
                            for h in range(2):
                                last = pe.matmul(ps[:, sl + h, 160 * i + k0:160 * i + 160],
                                                 QT[64 * h:64 * h + 64, p, 128 * t:128 * t + 128],
                                                 KT[64 * h:64 * h + 64, p, 128 * t - WIN + k0:128 * t + 128],
                                                 start=False, stop=i == 1)
                                if i == 1:
                                    last.then_inc(*full[sl + h].mark((key, b, "s", u)))
                    if 0 <= u - 2 < UNITS:
                        w = u - 2
                        p, t0, _ = unit(w)
                        tb = 4 + w % 2
                        pe.wait_ge(*scaled.at((key, b, w)))
                        take(pe, tb, 6)
                        for j in range(4):
                            last = pe.transpose(ps[:, tb, 128 * j:128 * j + 128], P[:, w % 3, j, 96 + WIN:256], ident[:, :])
                        last.then_inc(*full[tb].mark((key, b, w)))
                        for j in range(4):
                            if t0 + j % 2 > 0:
                                last = pe.transpose(ps[:, 6, 64 * j:64 * j + 64], P[0:64, w % 3, j, 0:128], ident[0:64, 0:64])
                        last.then_inc(*full[6].mark((key, b, w)))
                    if u >= 3:
                        w = u - 3
                        p, t0, _ = unit(w)
                        pe.wait_ge(*turned.at((key, b, w)))
                        pe.wait_ge(*turned_b.at((key, b, w)))
                        if w == 0:
                            pe.wait_ge(*v_ready.at((key, b, NP - 1)))
                        if t0 == 0:
                            take(pe, 7)
                        for j in range(4):
                            h, t = j // 2, t0 + j % 2
                            f = 128 * p + 64 * h
                            last = pe.matmul(ps[64 * h:64 * h + 64, 7, 128 * t:128 * t + 128], V[:, t, f:f + 64],
                                             PT[:, w % 2, j, :], start=True, stop=t == 0)
                            if t > 0:
                                last = pe.matmul(ps[64 * h:64 * h + 64, 7, 128 * t:128 * t + 64], V[96:128, t - 1, f:f + 64],
                                                 PTb[96:128, w % 2, j, :], start=False, stop=True, tile_position=(96, 64 * h))
                        last.then_inc(*full[7].mark((key, b, w)))
                take(pe, 6)
                for p in range(NP):
                    pe.wait_ge(*merged.at((key, b, p)))
                    last = pe.matmul(ps[:, 6, :], Wo[:, p, :], OT[:, p, :], start=p == 0, stop=p == NP - 1)
                last.then_inc(*full[6].mark((key, b, "y")))

        def l2_pe(pe, key, b, p):
            pe.wait_ge(*k_sq.at((key, b, p)))
            take(pe, 5)
            pe.matmul(ps[:, 5, :], spread[:, :], sqh[:, 2 + p % 2, :], start=True, stop=True).then_inc(*full[5].mark((key, b, "ssk", p)))
            pe.wait_ge(*q_sq.at((key, b, p)))
            if p == 0:
                take(pe, 7)
            for t in range(NT):
                last = pe.matmul(ps[:, 7, 16 * t + 2 * p:16 * t + 2 * p + 2], sqh[:, p % 2, 128 * t:128 * t + 128],
                                 seg[:, 0:2], start=True, stop=True)
            last.then_inc(*full[7].mark((key, b, "ssq", p)))

        def attn_act(act, key, l2):
            for b in range(B):
                for p in range(NP + 1):
                    if p < NP:
                        if l2:
                            if p >= 2:
                                act.wait_ge(*full[7].at((key, b, "ssq", p - 2)))
                            act.wait_ge(*full[0].at((key, b, p)))
                            act.activation(sqh[:, p % 2, :], ps[:, 0, :], ACT.Square).then_inc(*q_sq.mark((key, b, p)))
                            act.wait_ge(*full[2].at((key, b, p)))
                            act.activation(sqh[:, 2 + p % 2, :], ps[:, 2, :], ACT.Square).then_inc(*k_sq.mark((key, b, p)))
                        t, hf = p // 2, p % 2
                        act.wait_ge(*full[4].at((key, b, "v", p)))
                        act.activation(V[:, t, 512 * hf:512 * hf + 512], ps[:, 4, :], ACT.Copy).then_inc(*v_ready.mark((key, b, p)))
                        read(act, 4, v_ready, (key, b, p))
                    if l2 and p > 0:
                        w = p - 1
                        kn = knr[:, w % 2, :]
                        act.wait_ge(*guarded.at((key, b, w)))
                        step(act, act_step, act.activation(kn, kn, ACT.Ln, scale=2.0 ** 20))
                        act.activation(kn, kn, ACT.Exp, scale=-0.5, bias=eps5[:, 3:4]).then_inc(*k_norm.mark((key, b, w)))
                if l2:
                    act.wait_ge(*guarded.at((key, b, "q")))
                    step(act, act_step, act.activation(rq, rq, ACT.Ln, scale=2.0 ** 20))
                    act.activation(rq, rq, ACT.Exp, scale=-0.5, bias=eps5[:, 3:4]).then_inc(*q_norm.mark((key, b)))
                for u in range(UNITS + 2):
                    if u >= 2:
                        w = u - 2
                        tb = 4 + w % 2
                        act.wait_ge(*full[tb].at((key, b, w)))
                        act.activation(PT[:, w % 2, :, :], ps[:, tb, :].rearrange("p (j k) -> p j k", j=4), ACT.Copy)\
                            .then_inc(*turned.mark((key, b, w)))
                        read(act, tb, turned, (key, b, w))
                    if u < UNITS:
                        p, t0, sl = unit(u)
                        act.wait_ge(*topped.at((key, b, u)))
                        for j in range(4):
                            h, i = j // 2, j % 2
                            sc = rq8[:, t0 + i, 2 * p + h:2 * p + h + 1] if l2 else D ** -0.5
                            ins = act.activation(P[:, u % 3, j, 96:256], ps[:, sl + h, 160 * i:160 * i + 160], ACT.Exp,
                                                 bias=nm[:, u % 3, 4 + j:5 + j], scale=sc, accum_out=nm[:, u % 3, 8 + j:9 + j])
                            if j == 1:
                                ins.then_inc(*free[sl].mark())
                        ins.then_inc(*exped.mark((key, b, u)))
                        read(act, sl + 1, exped, (key, b, u))

        rq8 = sb("rq8", [128, NT, H])

        def attn_dve(dve, key, l2):
            for b in range(B):
                for p in range(NP + 1):
                    if p < NP:
                        for j, w in enumerate(QKV):
                            if l2 and w == "q":
                                dve.wait_ge(*q_sq.at((key, b, p)))
                            elif l2 and w == "k":
                                dve.wait_ge(*k_sq.at((key, b, p)))
                            else:
                                dve.wait_ge(*full[j].at((key, b, p)))
                            if (b, p) not in ((0, 0), (0, 1)):
                                pp = (b, p - 2) if p >= 2 else (b - 1, NP - 2 + p)
                                dve.wait_ge(*roped.at((key, *pp, "q" if j < 2 else "k")))
                            part = part1 if j < 2 else part2
                            dve.tensor_tensor(tmp[:, p % 2, j, :], ps[:, j, :], (tab if l2 else tab0)[:, j, :], ALU.mult)\
                                .then_inc(*part.mark((key, b, p, j)))
                            read(dve, j, part, (key, b, p, j))
                    if l2 and p > 0:
                        w = p - 1
                        dve.wait_ge(*full[5].at((key, b, "ssk", w)))
                        if w >= 2:
                            dve.wait_ge(*k_raised.at((key, b, w - 2)))
                        elif b > 0:
                            dve.wait_ge(*k_raised.at((key, b - 1, NP - 2 + w)))
                        dve.tensor_scalar(knr[:, w % 2, :], ps[:, 5, :], 1e-24, None, ALU.max).then_inc(*guarded.mark((key, b, w)))
                        read(dve, 5, guarded, (key, b, w))
                if l2:
                    dve.wait_ge(*full[7].at((key, b, "ssq", NP - 1)))
                    dve.tensor_scalar(rq, ps[:, 7, 0:64].rearrange("p (t h) -> p t h", t=NT), 1e-24, None, ALU.max)\
                        .then_inc(*guarded.mark((key, b, "q")))
                    read(dve, 7, guarded, (key, b, "q"))
                    dve.wait_ge(*q_norm.at((key, b)))
                    step(dve, dve_step, dve.tensor_scalar(rq8[:, :, :], rq, 8.0, None, ALU.mult))
                for u in range(UNITS + 4):
                    if u >= 5 and u % 2 == 1:
                        merge_dve(dve, key, b, (u - 5) // 2)
                    if u < UNITS:
                        p, t0, sl = unit(u)
                        i = u % 3
                        dve.wait_ge(*full[sl].at((key, b, "s", u)))
                        dve.wait_ge(*full[sl + 1].at((key, b, "s", u)))
                        step(dve, dve_step, dve.tensor_reduce(nm[:, i, 0:4], ps[:, sl:sl + 2, 0:320].rearrange("p h (i k) -> p h i k", i=2),
                                                              AX, ALU.max))
                        if l2:
                            step(dve, dve_step, dve.tensor_tensor(
                                nm[:, i, 0:4].rearrange("p (h i) -> p h i", h=2), nm[:, i, 0:4].rearrange("p (h i) -> p h i", h=2),
                                rq8[:, t0:t0 + 2, 2 * p:2 * p + 2].rearrange("p i h -> p h i"), ALU.mult))
                        dve.tensor_scalar(nm[:, i, 4:8], nm[:, i, 0:4], -1.0 if l2 else -D ** -0.5, None, ALU.mult)\
                            .then_inc(*topped.mark((key, b, u)))
                    if 2 <= u < UNITS + 2:
                        w = u - 2
                        j0 = 1 if w % 2 == 0 else 0
                        v = lambda a: a.rearrange("p (h i k) -> p h i k", h=2, i=2)[96:128, :, j0:2, :]
                        dve.wait_ge(*full[6].at((key, b, w)))
                        dve.tensor_copy(v(PTb[:, w % 2, :, :].rearrange("p j k -> p (j k)")), v(ps[:, 6, 0:256]))\
                            .then_inc(*turned_b.mark((key, b, w)))
                        read(dve, 6, turned_b, (key, b, w))
                    if 1 <= u <= UNITS:
                        w = u - 1
                        i = w % 3
                        dve.wait_ge(*exped.at((key, b, w)))
                        step(dve, dve_step, dve.reciprocal(nm[:, i, 12:16], nm[:, i, 8:12]))
                        dve.tensor_tensor(P[:, i, :, 96:256], P[:, i, :, 96:256],
                                          nm[:, i, 12:16].unsqueeze(2).to_broadcast([128, 4, 160]), ALU.mult)\
                            .then_inc(*scaled.mark((key, b, w)))
                dve.wait_ge(*full[6].at((key, b, "y")))
                dve.tensor_tensor(x[:, T * b:T * b + T], x[:, T * b:T * b + T], ps[:, 6, :], ALU.add)\
                    .then_inc(*x_new.mark((key, b)))
                read(dve, 6, x_new, (key, b))

        def merge_dve(dve, key, b, p):
            dve.wait_ge(*full[7].at((key, b, 2 * p + 1)))
            dve.tensor_copy(OT[:, p, :], ps[:, 7, :]).then_inc(*merged.mark((key, b, p)))
            read(dve, 7, merged, (key, b, p))

        def attn_pool(pool, key, l2):
            for b in range(B):
                for p in range(NP + 1):
                    if p < NP:
                        pool.wait_ge(*part1.at((key, b, p, 1)))
                        pool.tensor_tensor(QT[:, p, :], tmp[:, p % 2, 0, :], tmp[:, p % 2, 1, :], ALU.add).then_inc(*roped.mark((key, b, p, "q")))
                        pool.wait_ge(*part2.at((key, b, p, 3)))
                        pool.tensor_tensor(KT[:, p, :], tmp[:, p % 2, 2, :], tmp[:, p % 2, 3, :], ALU.add).then_inc(*roped.mark((key, b, p, "k")))
                    if l2 and p > 0:
                        w = p - 1
                        pool.wait_ge(*roped.at((key, b, w, "k")))
                        pool.wait_ge(*k_norm.at((key, b, w)))
                        pool.tensor_tensor(KT[:, w, :], KT[:, w, :], knr[:, w % 2, :], ALU.mult).then_inc(*k_raised.mark((key, b, w)))

        def src_ready(pe, key, b):
            if key == "A":
                pe.wait_ge(*normed.at(("A2", b)))
            else:
                pe.wait_ge(*shifted.at(("F1", b)))

        cols = lambda b: slice(T * b, T * b + T)

        fix = sb("fix", [128, 3100])
        fat = [0]

        def keep(*dims):
            n = math.prod(dims)
            v = fix[:, fat[0]:fat[0] + n]
            fat[0] += n
            assert fat[0] <= 3100, fat[0]
            return v if len(dims) == 1 else v.rearrange("p (a b) -> p a b", a=dims[0]) if len(dims) == 2 else \
                v.rearrange("p (a b c) -> p a b c", a=dims[0], b=dims[1])
        ctxT = keep(B, S)
        Bw = keep(4, C)
        Bb = keep(4)
        Ew = keep(4, C)
        Eb = keep(4)
        hmask = keep(HS)
        Cw = keep(70, FB)
        tri = keep(128)
        a2 = Area()
        qt = a2(T)
        kt = a2(S)
        vt = a2(2, C)
        vt1 = a2(2, HS * 9)
        sc_ = a2(2, S)
        rem = a2(2, S)
        pe_ = a2(2, S)
        msk = a2(S)
        m8 = a2(2, 40)
        pt2 = a2(2, 512)
        ctxo = a2(T)
        KB = a2(HS, S)
        PE_ = a2(HS, S)
        mx = a2(2, 16)
        atok = a2(128)
        aT = a2(T)
        rd = a2(HS)
        gT = a2(I0)
        uT = a2(I0)
        dT = a2(3, C)
        xq = a2(B, T)
        xqT = a2(B, T)
        hq = a2(B, NT * I0)
        hT = a2(3, T)
        qa = a2(1408)
        qu = a2(1408)
        qs = a2(1408)
        qb = a2(3, 88)
        eg = a2(2, I0)
        q_ready, k_ready, vv_ready = sg("q_ready"), sg("k_ready"), sg("vv_ready")
        picked, b_exp, b_prob, b_turn, b_ctx = sg("picked"), sg("b_exp"), sg("b_prob"), sg("b_turn"), sg("b_ctx")
        signed, q4, turned4, expg, hgate = sg("signed"), sg("q4"), sg("turned4"), sg("expg"), sg("hgate")
        kb_ready, e_max, e_exp, e_turn_a, e_turn_d, e_norm = sg("kb_ready"), sg("e_max"), sg("e_exp"), sg("e_turn_a"), sg("e_turn_d"), sg("e_norm")

        def qkv_pe(pe, key, b, w):
            pe.wait_ge(*normed.at((key + "1", b)))
            take(pe, 0)
            pe.matmul(ps[:, 0, :], w[:, 0, :], xn[:, b, :], start=True, stop=True).then_inc(*full[0].mark((key, b, "q")))
            take(pe, 1)
            pe.matmul(ps[:, 1, 0:S], w[:, 1, :], ctxT[:, b, :], start=True, stop=True).then_inc(*full[1].mark((key, b, "k")))
            take(pe, 2)
            for hf in range(2):
                last = pe.matmul(ps[0:SH, 2, 128 * hf:128 * hf + 128], ctxT[:, b, SH * hf:SH * hf + SH], w[:, 2, :],
                                 start=True, stop=True)
            last.then_inc(*full[2].mark((key, b, "v")))

        def qkv_act(act, key, b, bias):
            act.wait_ge(*full[0].at((key, b, "q")))
            act.activation(qt, ps[:, 0, :], ACT.Identity, bias=bias[:, 0:1]).then_inc(*q_ready.mark((key, b)))
            read(act, 0, q_ready, (key, b))
            act.wait_ge(*full[1].at((key, b, "k")))
            act.activation(kt, ps[:, 1, 0:S], ACT.Identity, bias=bias[:, 1:2]).then_inc(*k_ready.mark((key, b)))
            read(act, 1, k_ready, (key, b))
            act.wait_ge(*full[2].at((key, b, "v")))
            src = ps[0:SH, 2, 0:256].rearrange("p (a c) -> p a c", a=2)
            if key == "B":
                ins = act.activation(vt[0:SH, :, :], src, ACT.Copy)
            else:
                src = ps[0:SH, 2, 0:256].rearrange("p (a d) -> p a d", d=DS)
                ins = act.activation(vt1.rearrange("p a (h d) -> p (a h) d", d=9)[0:SH, :, 0:DS], src, ACT.Copy)
            ins.then_inc(*vv_ready.mark((key, b)))
            read(act, 2, vv_ready, (key, b))

        def out_pe(pe, key, b, w, src, wait):
            pe.wait_ge(*wait)
            take(pe, 3)
            pe.matmul(ps[:, 3, :], w, src, start=True, stop=True).then_inc(*full[3].mark((key, b, "y")))

        def out_dve(dve, key, b, bias, bank=3):
            dve.wait_ge(*full[bank].at((key, b, "y")))
            dve.scalar_tensor_tensor(x[:, cols(b)], ps[:, bank, :], bias, x[:, cols(b)], ALU.add, ALU.add)\
                .then_inc(*x_new.mark((key, b)))
            read(dve, bank, x_new, (key, b))

        def b_pe(pe):
            for b in range(B):
                norm_pe(pe, "B1", b, b, x[:, cols(b)], wait=(x_new.at(("A", b)),))
            for b in range(B):
                qkv_pe(pe, "B", b, Bw)
                pe.wait_ge(*q_ready.at(("B", b)))
                pe.wait_ge(*k_ready.at(("B", b)))
                for t in range(NT + 1):
                    if t < NT:
                        k = 4 + t % 2
                        take(pe, k)
                        pe.matmul(ps[:, k, 0:S], qt[:, 128 * t:128 * t + 128], kt, start=True, stop=True)\
                            .then_inc(*full[k].mark(("B", b, t)))
                    if t > 0:
                        u = t - 1
                        k = 6 + u % 2
                        pe.wait_ge(*b_prob.at((b, u)))
                        take(pe, k)
                        for hf in range(2):
                            last = pe.transpose(ps[0:SH, k, 128 * hf:128 * hf + 128], pe_[:, u % 2, SH * hf:SH * hf + SH], ident[:, :])
                        last.then_inc(*full[k].mark(("B", b, u)))
                        pe.wait_ge(*b_turn.at((b, u)))
                        if u == 0:
                            pe.wait_ge(*vv_ready.at(("B", b)))
                            take(pe, 2)
                        for hf in range(2):
                            last = pe.matmul(ps[:, 2, 128 * u:128 * u + 128], vt[0:SH, hf, :], pt2[0:SH, u % 2, 128 * hf:128 * hf + 128],
                                             start=hf == 0, stop=hf == 1)
                last.then_inc(*full[2].mark(("B", b, "o")))
                out_pe(pe, "B", b, Bw[:, 3, :], ctxo, b_ctx.at(("B", b)))

        def b_act(act):
            for b in range(B):
                norm_act(act, "B1", b, b, None, 0)
            for b in range(B):
                qkv_act(act, "B", b, Bb)
                for t in range(NT + 1):
                    if t < NT:
                        act.wait_ge(*picked.at((b, t)))
                        act.activation(pe_[:, t % 2, :], sc_[:, t % 2, :], ACT.Exp, bias=m8[:, t % 2, 32:33], scale=C ** -0.5)\
                            .then_inc(*b_exp.mark((b, t)))
                    if t > 0:
                        u = t - 1
                        k = 6 + u % 2
                        act.wait_ge(*full[k].at(("B", b, u)))
                        act.activation(pt2[0:SH, u % 2, 0:256], ps[0:SH, k, 0:256], ACT.Copy).then_inc(*b_turn.mark((b, u)))
                        read(act, k, b_turn, (b, u))
                act.wait_ge(*full[2].at(("B", b, "o")))
                act.activation(ctxo, ps[:, 2, :], ACT.Identity, bias=Bb[:, 2:3]).then_inc(*b_ctx.mark(("B", b)))
                read(act, 2, b_ctx, ("B", b))

        def b_dve(dve):
            for b in range(B):
                norm_dve(dve, "B1", b, b, x[:, cols(b)])
            for b in range(B):
                for t in range(NT + 1):
                    if t < NT:
                        i, k = t % 2, 4 + t % 2
                        dve.wait_ge(*full[k].at(("B", b, t)))
                        if t >= 2:
                            dve.wait_ge(*full[6 + i].at(("B", b, t - 2)))
                        step(dve, dve_step, dve.tensor_copy(sc_[:, i, :], ps[:, k, 0:S]))
                        dve.sem_inc(free[k].mark()[0], 1)
                        for r in range(TOPK // 8):
                            src = sc_[:, i, :] if r == 0 else rem[:, i, :]
                            step(dve, dve_step, dve.max(m8[:, i, 8 * r:8 * r + 8], src))
                            step(dve, dve_step, dve.match_replace(rem[:, i, :], m8[:, i, 8 * r:8 * r + 8], src, -3e38))
                        dve.tensor_scalar(m8[:, i, 32:33], m8[:, i, 0:1], -C ** -0.5, None, ALU.mult).then_inc(*picked.mark((b, t)))
                    if t > 0:
                        u, i = t - 1, (t - 1) % 2
                        step(dve, dve_step, dve.tensor_tensor(msk, rem[:, i, :], sc_[:, i, :], ALU.not_equal))
                        dve.wait_ge(*b_exp.at((b, u)))
                        step(dve, dve_step, dve.tensor_tensor(pe_[:, i, :], pe_[:, i, :], msk, ALU.mult))
                        step(dve, dve_step, dve.tensor_reduce(m8[:, i, 33:34], pe_[:, i, :], AX, ALU.add))
                        step(dve, dve_step, dve.reciprocal(m8[:, i, 34:35], m8[:, i, 33:34]))
                        dve.tensor_scalar(pe_[:, i, :], pe_[:, i, :], m8[:, i, 34:35], None, ALU.mult).then_inc(*b_prob.mark((b, u)))
                out_dve(dve, "B", b, Bb[:, 3:4])

        def fp4(dve, key, src, nb, dst):
            n = nb * FB
            s3 = lambda v: v[:, 0:n].rearrange("p (a b) -> p a b", b=FB)
            wide = lambda v: v.unsqueeze(2).to_broadcast([128, nb, FB])
            big_, sca, inv = qb[:, 0, 0:nb], qb[:, 1, 0:nb], qb[:, 2, 0:nb]
            step(dve, dve_step, dve.tensor_reduce(big_, src, AX, ALU.max, apply_absolute_value=True))
            step(dve, dve_step, dve.tensor_scalar(sca, big_, 1 / 6, 1e-12, ALU.mult, ALU.max))
            step(dve, dve_step, dve.reciprocal(inv, sca))
            step(dve, dve_step, dve.tensor_tensor(s3(qa), src, wide(inv), ALU.mult))
            step(dve, dve_step, dve.scalar_tensor_tensor(qa[:, 0:n], qa[:, 0:n], -1.0, qa[:, 0:n], ALU.mult, ALU.max))
            a_, u_ = qa[:, 0:n], qu[:, 0:n]
            step(dve, dve_step, dve.tensor_scalar(u_, a_, 5.0, 2.0, ALU.is_gt, ALU.mult))
            for m in (3.5, 2.5):
                step(dve, dve_step, dve.scalar_tensor_tensor(u_, a_, m, u_, ALU.is_gt, ALU.add))
            step(dve, dve_step, dve.tensor_scalar(u_, u_, 2.0, None, ALU.mult))
            for m in (1.75, 1.25, 0.75, 0.25):
                step(dve, dve_step, dve.scalar_tensor_tensor(u_, a_, m, u_, ALU.is_gt, ALU.add))
            dve.wait_ge(*signed.at(key))
            step(dve, dve_step, dve.scalar_tensor_tensor(u_, u_, 0.5, qs[:, 0:n], ALU.mult, ALU.mult))
            dve.tensor_tensor(dst, s3(qu), wide(sca), ALU.mult).then_inc(*q4.mark(key))
            dve.wait_ge(*q4.at(key))

        def sign_act(act, key, src, n):
            act.activation(qs[:, 0:n], src, ACT.Sign).then_inc(*signed.mark(key))

        def c_pe(pe):
            pe.wait_ge(*q4.at("w"))
            for j, off in enumerate((0, 24, 48)):
                take(pe, j)
                for ch in range(3):
                    m = min(128, I0 - 128 * ch)
                    if j < 2:
                        last = pe.transpose(ps[:, j, 128 * ch:128 * ch + m],
                                            Cw[0:m, off + 8 * ch:off + 8 * ch + 8, :].rearrange("p a b -> p (a b)"), ident[0:m, 0:m])
                    else:
                        last = pe.transpose(ps[0:m, j, 128 * ch:128 * ch + 128],
                                            Cw[:, off + 8 * ch:off + 8 * ch + m // FB, :].rearrange("p a b -> p (a b)"), ident[:, :])
                last.then_inc(*full[j].mark(("C", "w", j)))
            for b in range(B):
                norm_pe(pe, "C1", b, 6 + b, x[:, cols(b)], wait=(x_new.at(("B", b)),))
            for b in range(B):
                pe.wait_ge(*normed.at(("C1", b)))
                take(pe, b)
                for t in range(NT):
                    last = pe.transpose(ps[:, b, 128 * t:128 * t + 128], xn[:, b, 128 * t:128 * t + 128], ident[:, :])
                last.then_inc(*full[b].mark(("C", b, "x")))
            for b in range(B):
                pe.wait_ge(*q4.at(("x", b)))
                take(pe, 2)
                for t in range(NT):
                    last = pe.transpose(ps[:, 2, 128 * t:128 * t + 128], xq[:, b, 128 * t:128 * t + 128], ident[:, :])
                last.then_inc(*full[2].mark(("C", b, "xt")))
                pe.wait_ge(*turned4.at(("x", b)))
                if b == 0:
                    pe.wait_ge(*turned4.at(("w", 2)))
                for t in range(NT):
                    for j, w in enumerate((gT, uT)):
                        k = 4 + 2 * (t % 2) + j
                        take(pe, k)
                        pe.matmul(ps[:, k, 0:I0], xqT[:, b, 128 * t:128 * t + 128], w, start=True, stop=True)\
                            .then_inc(*full[k].mark(("C", b, t, j)))
            for b in range(B):
                pe.wait_ge(*q4.at(("h", b)))
                for t in range(NT):
                    k = t % 2
                    take(pe, k)
                    for ch in range(3):
                        m = min(128, I0 - 128 * ch)
                        last = pe.transpose(ps[0:m, k, 128 * ch:128 * ch + 128], hq[:, b, I0 * t + 128 * ch:I0 * t + 128 * ch + m], ident[:, :])
                    last.then_inc(*full[k].mark(("C", b, "h", t)))
                pe.wait_ge(*turned4.at(("h", b, NT - 1)))
                take(pe, 3)
                for ch in range(3):
                    m = min(128, I0 - 128 * ch)
                    last = pe.matmul(ps[:, 3, :], dT[0:m, ch, :], hT[0:m, ch, :], start=ch == 0, stop=ch == 2)
                last.then_inc(*full[3].mark(("C", b, "y")))

        def c_act(act):
            sign_act(act, "w", Cw.rearrange("p a b -> p (a b)"), 1120)
            for j, dst in enumerate((gT, uT)):
                act.wait_ge(*full[j].at(("C", "w", j)))
                act.activation(dst, ps[:, j, 0:I0], ACT.Copy).then_inc(*turned4.mark(("w", j)))
                read(act, j, turned4, ("w", j))
            act.wait_ge(*full[2].at(("C", "w", 2)))
            step(act, act_step, act.activation(dT[:, 0:2, :], ps[:, 2, 0:256].rearrange("p (a b) -> p a b", a=2), ACT.Copy))
            act.activation(dT[0:96, 2, :], ps[0:96, 2, 256:384], ACT.Copy).then_inc(*turned4.mark(("w", 2)))
            read(act, 2, turned4, ("w", 2))
            for b in range(B):
                norm_act(act, "C1", b, 6 + b, None, 0)
            for b in range(B):
                act.wait_ge(*q4.at("w" if b == 0 else ("x", b - 1)))
                act.wait_ge(*centred.at(("xc", b)))
                sign_act(act, ("x", b), xq[:, b, :], T)
                act.wait_ge(*full[2].at(("C", b, "xt")))
                act.activation(xqT[:, b, :], ps[:, 2, :], ACT.Copy).then_inc(*turned4.mark(("x", b)))
                read(act, 2, turned4, ("x", b))
                for t in range(NT):
                    k = 4 + 2 * (t % 2)
                    act.wait_ge(*full[k].at(("C", b, t, 0)))
                    if t >= 2:
                        act.wait_ge(*hgate.at((b, t - 2)))
                    act.activation(eg[:, t % 2, :], ps[:, k, 0:I0], ACT.Exp, scale=-1.0).then_inc(*expg.mark((b, t)))
            for b in range(B):
                act.wait_ge(*hgate.at((b, NT - 1)))
                act.wait_ge(*q4.at(("x", 1) if b == 0 else ("h", b - 1)))
                sign_act(act, ("h", b), hq[:, b, :], NT * I0)
                for t in range(NT):
                    k = t % 2
                    act.wait_ge(*full[k].at(("C", b, "h", t)))
                    step(act, act_step, act.activation(hT[:, 0:2, 128 * t:128 * t + 128],
                                                       ps[:, k, 0:256].rearrange("p (a b) -> p a b", a=2), ACT.Copy))
                    act.activation(hT[0:96, 2, 128 * t:128 * t + 128], ps[0:96, k, 256:384], ACT.Copy).then_inc(*turned4.mark(("h", b, t)))
                    read(act, k, turned4, ("h", b, t))

        def c_dve(dve):
            fp4(dve, "w", Cw, 70, Cw)
            for b in range(B):
                norm_dve(dve, "C1", b, 6 + b, x[:, cols(b)])
            b3 = lambda v: v.rearrange("p (a b) -> p a b", b=FB)
            for b in range(B):
                dve.wait_ge(*full[b].at(("C", b, "x")))
                dve.tensor_copy(xq[:, b, :], ps[:, b, :]).then_inc(*centred.mark(("xc", b)))
                read(dve, b, centred, ("xc", b))
            for b in range(B):
                fp4(dve, ("x", b), b3(xq[:, b, :]), 32, b3(xq[:, b, :]))
                for t in range(NT):
                    k, i = 4 + 2 * (t % 2), t % 2
                    h_ = hq[:, b, I0 * t:I0 * t + I0]
                    dve.wait_ge(*expg.at((b, t)))
                    step(dve, dve_step, dve.tensor_scalar(eg[:, i, :], eg[:, i, :], 1.0, None, ALU.add))
                    step(dve, dve_step, dve.reciprocal(eg[:, i, :], eg[:, i, :]))
                    step(dve, dve_step, dve.tensor_tensor(h_, eg[:, i, :], ps[:, k, 0:I0], ALU.mult))
                    dve.sem_inc(free[k].mark()[0], 1)
                    dve.wait_ge(*full[k + 1].at(("C", b, t, 1)))
                    dve.tensor_tensor(h_, h_, ps[:, k + 1, 0:I0], ALU.mult).then_inc(*hgate.mark((b, t)))
                    read(dve, k + 1, hgate, (b, t))
            for b in range(B):
                fp4(dve, ("h", b), b3(hq[:, b, :]), NT * I0 // FB, b3(hq[:, b, :]))
                dve.wait_ge(*full[3].at(("C", b, "y")))
                dve.tensor_tensor(x[:, cols(b)], x[:, cols(b)], ps[:, 3, :], ALU.add).then_inc(*x_new.mark(("C", b)))
                read(dve, 3, x_new, ("C", b))

        def e_pe(pe, before):
            for b in range(B):
                norm_pe(pe, "E1", b, b, x[:, cols(b)], wait=(x_new.at((before, b)),))
            for b in range(B):
                qkv_pe(pe, "E", b, Ew)
                pe.wait_ge(*q_ready.at(("E", b)))
                pe.wait_ge(*kb_ready.at(b))
                pe.wait_ge(*vv_ready.at(("E", b)))
                for t in range(NT):
                    for g in range(6):
                        n = min(3, HS - 3 * g)
                        k = (6 * t + g) % 5
                        take(pe, k)
                        pe.matmul(ps[:, k, 0:n * S], qt[:, 128 * t:128 * t + 128],
                                  KB[:, 3 * g:3 * g + n, :].rearrange("p a b -> p (a b)"), start=True, stop=True)\
                            .then_inc(*full[k].mark(("E", b, t, g)))
                    pe.wait_ge(*e_exp.at((b, t)))
                    take(pe, 5)
                    for m in range(9):
                        if m < 8:
                            k = 6 + m % 2
                            take(pe, k)
                            for q_ in range(4):
                                last = pe.transpose(ps[0:SH, k, 128 * q_:128 * q_ + 128],
                                                    PE_[:, 2 * m + q_ // 2, SH * (q_ % 2):SH * (q_ % 2) + SH], ident[:, :])
                            last.then_inc(*full[k].mark(("E", b, t, m)))
                        if m > 0:
                            w = m - 1
                            pe.wait_ge(*(e_turn_a if w % 2 == 0 else e_turn_d).at((b, t, w)))
                            for q_ in range(4):
                                h = 2 * w + q_ // 2
                                last = pe.matmul(ps[:, 5, 9 * h:9 * h + 9], pt2[0:SH, w % 2, 128 * q_:128 * q_ + 128],
                                                 vt1[0:SH, q_ % 2, 9 * h:9 * h + 9], start=q_ % 2 == 0, stop=q_ % 2 == 1)
                    last.then_inc(*full[5].mark(("E", b, t, "o")))
                    pe.wait_ge(*e_norm.at((b, t)))
                    take(pe, 5)
                    pe.transpose(ps[:, 5, 0:128], atok, ident[:, :]).then_inc(*full[5].mark(("E", b, t, "a")))
                out_pe(pe, "E", b, Ew[:, 3, :], aT, b_ctx.at(("E", b, NT - 1)))

        def e_act(act):
            for b in range(B):
                norm_act(act, "E1", b, b, None, 0)
            for b in range(B):
                qkv_act(act, "E", b, Eb)
                for t in range(NT):
                    for h in range(HS):
                        g, j = h // 3, h % 3
                        k = (6 * t + g) % 5
                        if j == 0:
                            act.wait_ge(*e_max.at((b, t, g)))
                        ins = act.activation(PE_[:, h, :], ps[:, k, S * j:S * j + S], ACT.Exp, bias=mx[:, 1, h:h + 1], scale=DS ** -0.5)
                        if j == 2:
                            ins.then_inc(*free[k].mark())
                        elif h == HS - 1:
                            ins.then_inc(*e_exp.mark((b, t)))
                            read(act, k, e_exp, (b, t))
                    for m in range(0, 8, 2):
                        act.wait_ge(*full[6].at(("E", b, t, m)))
                        act.activation(pt2[0:SH, 0, :], ps[0:SH, 6, :], ACT.Copy).then_inc(*e_turn_a.mark((b, t, m)))
                        read(act, 6, e_turn_a, (b, t, m))
                    act.wait_ge(*full[5].at(("E", b, t, "a")))
                    act.activation(aT[:, 128 * t:128 * t + 128], ps[:, 5, 0:128], ACT.Identity, bias=Eb[:, 2:3])\
                        .then_inc(*b_ctx.mark(("E", b, t)))
                    read(act, 5, b_ctx, ("E", b, t))

        def e_dve(dve):
            dve.wait_ge(*x_new.at(("D", 1)))
            dve.memset(vt1, 1.0).then_inc(*vv_one.mark("ones"))
            for b in range(B):
                norm_dve(dve, "E1", b, b, x[:, cols(b)])
            for b in range(B):
                dve.wait_ge(*k_ready.at(("E", b)))
                dve.tensor_tensor(KB, kt.unsqueeze(1).to_broadcast([128, HS, S]), hmask.unsqueeze(2).to_broadcast([128, HS, S]), ALU.mult)\
                    .then_inc(*kb_ready.mark(b))
                for t in range(NT):
                    if (b, t) != (0, 0):
                        dve.wait_ge(*e_exp.at((b, t - 1) if t else (b - 1, NT - 1)))
                    for g in range(6):
                        n = min(3, HS - 3 * g)
                        k = (6 * t + g) % 5
                        dve.wait_ge(*full[k].at(("E", b, t, g)))
                        hs = slice(3 * g, 3 * g + n)
                        step(dve, dve_step, dve.tensor_reduce(mx[:, 0, hs], ps[:, k, 0:n * S].rearrange("p (a b) -> p a b", a=n), AX, ALU.max))
                        dve.tensor_scalar(mx[:, 1, hs], mx[:, 0, hs], -DS ** -0.5, None, ALU.mult).then_inc(*e_max.mark((b, t, g)))
                    for m in range(1, 8, 2):
                        dve.wait_ge(*full[7].at(("E", b, t, m)))
                        dve.tensor_copy(pt2[0:SH, 1, :], ps[0:SH, 7, :]).then_inc(*e_turn_d.mark((b, t, m)))
                        read(dve, 7, e_turn_d, (b, t, m))
                    dve.wait_ge(*full[5].at(("E", b, t, "o")))
                    o = ps[:, 5, 0:144].rearrange("p (h d) -> p h d", d=9)
                    step(dve, dve_step, dve.reciprocal(rd, o[:, :, 8]))
                    dve.tensor_tensor(atok.rearrange("p (h d) -> p h d", d=DS), o[:, :, 0:DS], rd.unsqueeze(2).to_broadcast([128, HS, DS]),
                                      ALU.mult).then_inc(*e_norm.mark((b, t)))
                    read(dve, 5, e_norm, (b, t))
                out_dve(dve, "E", b, Eb[:, 3:4])
        vv_one = sg("vv_one")

        a4 = Area()
        o = a4(N)
        Dw = a4(4, C)
        Db = a4(20)
        bv = a4(C)
        omr = a4(DS)
        OmS = a4(512)
        Bn = a4(512)
        Om = a4(512)
        DW1 = a4(DFF)
        DW2 = a4(4, C)
        dq = a4(2, T)
        dsq = a4(2, T)
        Qf = a4(4, T)
        Kf = a4(4, T)
        Kt = a4(3, 512)
        V1 = a4(NT, HS * 9)
        st = a4(3, 144)
        own = a4(144)
        sT = a4(4, 512)
        da = a4(128)
        dd = a4(2, HS)
        dT_ = a4(T)
        h0 = a4(B, T)
        h1 = a4(B, T)
        rel = a4(4, T)
        d_in, d_q, d_k, d_v, d_sq, d_om = sg("d_in"), sg("d_q"), sg("d_k"), sg("d_v"), sg("d_sq"), sg("d_om")
        phi, ktok, state, masked, d_norm, d_turn = sg("phi"), sg("ktok"), sg("state"), sg("masked"), sg("d_norm"), sg("d_turn")
        res1, affine, relued, res2, d_used = sg("res1"), sg("affine"), sg("relued"), sg("res2"), sg("d_used")
        d_const, d_loaded = raw("d_const"), raw("d_loaded")

        def d_pe_layer(pe, L):
            pe.wait_ge(d_loaded, L * (16 * 7) + 16 * 7)
            pe.wait_ge(*d_om.at("om"))
            for b in range(B):
                pe.wait_ge(*d_in.at(b))
                for j in range(2):
                    take(pe, j)
                    pe.matmul(ps[:, j, :], Dw[:, j, :], o[:, cols(b)], start=True, stop=True).then_inc(*full[j].mark(("D", b, j)))
                take(pe, 2)
                for t in range(NT):
                    pe.matmul(ps[:, 2, 128 * t:128 * t + 128], o[:, T * b + 128 * t:T * b + 128 * t + 128], Dw[:, 2, :], start=True, stop=False)
                    last = pe.matmul(ps[:, 2, 128 * t:128 * t + 128], ones[0:1, :], bv[0:1, :], start=False, stop=True)
                last.then_inc(*full[2].mark(("D", b, 2)))
                for j, done in enumerate((d_q, d_k)):
                    pe.wait_ge(*done.at(b))
                    pe.wait_ge(*d_sq.at((b, j)))
                    for g in range(4):
                        k = 3 + (4 * j + g) % 5
                        take(pe, k)
                        pe.matmul(ps[:, k, :], Om[:, 128 * g:128 * g + 128], dq[:, j, :], start=True, stop=False)
                        pe.matmul(ps[:, k, :], Bn[:, 128 * g:128 * g + 128], dsq[:, j, :], start=False, stop=True)\
                            .then_inc(*full[k].mark(("D", b, "phi", j, g)))
                for ch in range(3):
                    take(pe, ch)
                    sl = slice(128 * ch, 128 * ch + 128)
                    pe.matmul(ps[:, ch, :], dq[:, 1, sl], Om, start=True, stop=False)
                    pe.matmul(ps[:, ch, :], dsq[:, 1, sl], Bn, start=False, stop=True).then_inc(*full[ch].mark(("D", b, "kt", ch)))
                pe.wait_ge(*d_v.at(b))
                for ch in range(3):
                    k = 3 + ch
                    pe.wait_ge(*ktok.at((b, ch)))
                    take(pe, k)
                    for g in range(4):
                        last = pe.matmul(ps[:, k, 36 * g:36 * g + 36], Kt[:, ch, 128 * g:128 * g + 128], V1[:, ch, 36 * g:36 * g + 36],
                                         start=True, stop=True)
                    last.then_inc(*full[k].mark(("D", b, "st", ch)))
                for ch in range(NT):
                    sl = slice(128 * ch, 128 * ch + 128)
                    pe.wait_ge(*phi.at((b, 1, 3)))
                    for r in range(4):
                        take(pe, r)
                    for g in range(4):
                        for r in range(4):
                            last = pe.matmul(ps[:, r, 128 * g:128 * g + 128], Kf[32 * r:32 * r + 16, g, sl], Qf[32 * r:32 * r + 16, g, sl],
                                             start=True, stop=True, tile_position=(32 * r, 0))
                            if g == 3:
                                last.then_inc(*full[r].mark(("D", b, ch, r)))
                    k = 6 + ch % 2
                    take(pe, k)
                    if ch > 0:
                        pe.wait_ge(*state.at((b, ch - 1)))
                        for g in range(4):
                            pe.matmul(ps[:, k, 36 * g:36 * g + 36], Qf[:, g, sl], st[:, ch - 1, 36 * g:36 * g + 36],
                                      start=g == 0, stop=False)
                    for r in range(4):
                        pe.wait_ge(*masked.at((b, ch, r)))
                        for g in range(4):
                            h = 4 * g + r
                            last = pe.matmul(ps[:, k, 9 * h:9 * h + 9], sT[:, r, 128 * g:128 * g + 128], V1[:, ch, 9 * h:9 * h + 9],
                                             start=ch == 0, stop=ch == 0 or (r, g) == (3, 3))
                    last.then_inc(*full[k].mark(("D", b, "num", ch)))
                    pe.wait_ge(*d_norm.at((b, ch)))
                    take(pe, k)
                    pe.transpose(ps[:, k, 0:128], da, ident[:, :]).then_inc(*full[k].mark(("D", b, "a", ch)))
                pe.wait_ge(*d_turn.at((b, NT - 1)))
                take(pe, 4)
                pe.matmul(ps[:, 4, :], Dw[:, 3, :], dT_, start=True, stop=True).then_inc(*full[4].mark(("D", b, "wo")))
            for b in range(B):
                norm_pe(pe, "D1", b, b, h0[:, b, :], wait=(res1.at(b),))
            for b in range(B):
                pe.wait_ge(*affine.at((b, 1)))
                for f_ in range(4):
                    k = 2 + f_
                    take(pe, k)
                    pe.matmul(ps[:, k, :], DW1[:, 128 * f_:128 * f_ + 128], h1[:, b, :], start=True, stop=True).then_inc(*full[k].mark(("D", b, "f", f_)))
                take(pe, 6)
                for f_ in range(4):
                    pe.wait_ge(*relued.at((b, f_)))
                    last = pe.matmul(ps[:, 6, :], DW2[:, f_, :], rel[:, f_, :], start=f_ == 0, stop=f_ == 3)
                last.then_inc(*full[6].mark(("D", b, "f2")))
            for b in range(B):
                norm_pe(pe, "D2", b, b, h0[:, b, :], wait=(res2.at(b),))

        def d_pe(pe):
            for b in range(B):
                norm_pe(pe, "D0", b, b, x[:, cols(b)], wait=(x_new.at(("C", b)),))
            pe.wait_ge(d_const, 48)
            with layers(pe, "D") as L:
                d_pe_layer(pe, L)

        def d_act_layer(act, L):
            act.wait_ge(*d_om.at("om"))
            for b in range(B):
                for j, done in enumerate((d_q, d_k)):
                    act.wait_ge(*full[j].at(("D", b, j)))
                    act.activation(dq[:, j, :], ps[:, j, :], ACT.Identity, bias=Db[:, 12 + j:13 + j], scale=DS ** -0.25).then_inc(*done.mark(b))
                    read(act, j, done, b)
                    act.activation(dsq[:, j, :], dq[:, j, :], ACT.Square).then_inc(*d_sq.mark((b, j)))
                act.wait_ge(*full[2].at(("D", b, 2)))
                act.activation(V1.rearrange("p t (h d) -> p t h d", d=9)[:, :, :, 0:DS],
                               ps[:, 2, :].rearrange("p (t h d) -> p t h d", t=NT, d=DS), ACT.Copy).then_inc(*d_v.mark(b))
                read(act, 2, d_v, b)
                for j in range(2):
                    for g in range(4):
                        k = 3 + (4 * j + g) % 5
                        act.wait_ge(*full[k].at(("D", b, "phi", j, g)))
                        act.activation((Qf, Kf)[j][:, g, :], ps[:, k, :], ACT.Exp, bias=eps5[:, 2:3]).then_inc(*phi.mark((b, j, g)))
                        read(act, k, phi, (b, j, g))
                for ch in range(3):
                    act.wait_ge(*full[ch].at(("D", b, "kt", ch)))
                    act.activation(Kt[:, ch, :], ps[:, ch, :], ACT.Exp, bias=eps5[:, 2:3]).then_inc(*ktok.mark((b, ch)))
                    read(act, ch, ktok, (b, ch))
                for ch in range(NT):
                    k = 6 + ch % 2
                    act.wait_ge(*full[k].at(("D", b, "a", ch)))
                    act.activation(dT_[:, 128 * ch:128 * ch + 128], ps[:, k, 0:128], ACT.Copy).then_inc(*d_turn.mark((b, ch)))
                    read(act, k, d_turn, (b, ch))
            for b in range(B):
                norm_act(act, "D1", b, b, None, 0)
            for b in range(B):
                act.wait_ge(*normed.at(("D1", b)))
                act.activation(h1[:, b, :], xn[:, b, :], ACT.Identity, bias=Db[:, 4:5], scale=Db[:, 3:4]).then_inc(*affine.mark((b, 1)))
                for f_ in range(4):
                    k = 2 + f_
                    act.wait_ge(*full[k].at(("D", b, "f", f_)))
                    if b == 1 and f_ == 0:
                        act.wait_ge(*full[6].at(("D", 0, "f2")))
                    act.activation(rel[:, f_, :], ps[:, k, :], ACT.Relu, bias=Db[:, 8 + f_:9 + f_]).then_inc(*relued.mark((b, f_)))
                    read(act, k, relued, (b, f_))
            for b in range(B):
                norm_act(act, "D2", b, b, None, 0)
            for b in range(B):
                act.wait_ge(*normed.at(("D2", b)))
                act.activation(o[:, cols(b)], xn[:, b, :], ACT.Identity, bias=Db[:, 6:7], scale=Db[:, 5:6]).then_inc(*affine.mark((b, 2)))
            act.wait_ge(*affine.at((1, 2)))
            act.sem_inc(d_used.mark("layer")[0], 1)

        def d_act(act):
            for b in range(B):
                norm_act(act, "D0", b, b, None, 0)
            with layers(act, "D") as L:
                d_act_layer(act, L)

        def d_dve_layer(dve, L):
            dve.wait_ge(d_loaded, L * (16 * 7) + 16 * 7)
            step(dve, dve_step, dve.tensor_scalar(Db[:, 12:14], Db[:, 0:2], DS ** -0.25, None, ALU.mult))
            dve.tensor_tensor(Om.rearrange("p (a d) -> p a d", d=DS), OmS.rearrange("p (a d) -> p a d", d=DS),
                              omr.unsqueeze(1).to_broadcast([128, 64, DS]), ALU.mult).then_inc(*d_om.mark("om"))
            for b in range(B):
                dve.wait_ge(*d_om.at("om"))
                dve.sem_inc(d_in.mark(b)[0], 1)
                for ch in range(3):
                    k = 3 + ch
                    dve.wait_ge(*full[k].at(("D", b, "st", ch)))
                    ins = dve.tensor_tensor(st[:, ch, :], ps[:, k, 0:144], own, ALU.mult)
                    if ch > 0:
                        step(dve, dve_step, ins)
                        ins = dve.tensor_tensor(st[:, ch, :], st[:, ch - 1, :], st[:, ch, :], ALU.add)
                    ins.then_inc(*state.mark((b, ch)))
                    read(dve, k, state, (b, ch))
                for ch in range(NT):
                    if ch > 0:
                        dve.wait_ge(*full[6 + (ch - 1) % 2].at(("D", b, "num", ch - 1)))
                    for r in range(4):
                        dve.wait_ge(*full[r].at(("D", b, ch, r)))
                        dve.tensor_tensor(sT[:, r, :].rearrange("p (g i) -> p g i", g=4), ps[:, r, :].rearrange("p (g i) -> p g i", g=4),
                                          tri.unsqueeze(1).to_broadcast([128, 4, 128]), ALU.mult).then_inc(*masked.mark((b, ch, r)))
                        read(dve, r, masked, (b, ch, r))
                    k = 6 + ch % 2
                    dve.wait_ge(*full[k].at(("D", b, "num", ch)))
                    nd = ps[:, k, 0:144].rearrange("p (h d) -> p h d", d=9)
                    step(dve, dve_step, dve.tensor_scalar(dd[:, 0, :], nd[:, :, 8], 1e-6, None, ALU.add))
                    step(dve, dve_step, dve.reciprocal(dd[:, 1, :], dd[:, 0, :]))
                    if ch > 0:
                        dve.wait_ge(*full[6 + (ch - 1) % 2].at(("D", b, "a", ch - 1)))
                    dve.tensor_tensor(da.rearrange("p (h d) -> p h d", d=DS), nd[:, :, 0:DS],
                                      dd[:, 1, :].unsqueeze(2).to_broadcast([128, HS, DS]), ALU.mult).then_inc(*d_norm.mark((b, ch)))
                    read(dve, k, d_norm, (b, ch))
                dve.wait_ge(*full[4].at(("D", b, "wo")))
                dve.scalar_tensor_tensor(h0[:, b, :], ps[:, 4, :], Db[:, 2:3], o[:, cols(b)], ALU.add, ALU.add).then_inc(*res1.mark(b))
                read(dve, 4, res1, b)
            for b in range(B):
                norm_dve(dve, "D1", b, b, h0[:, b, :])
            for b in range(B):
                dve.wait_ge(*affine.at((b, 1)))
                dve.wait_ge(*full[6].at(("D", b, "f2")))
                dve.scalar_tensor_tensor(h0[:, b, :], ps[:, 6, :], Db[:, 7:8], h1[:, b, :], ALU.add, ALU.add).then_inc(*res2.mark(b))
                read(dve, 6, res2, b)
            for b in range(B):
                norm_dve(dve, "D2", b, b, h0[:, b, :])
            dve.wait_ge(*affine.at((1, 2)))

        def d_dve(dve):
            step(dve, dve_step, dve.memset(V1, 1.0))
            for b in range(B):
                norm_dve(dve, "D0", b, b, x[:, cols(b)], out_=o[:, cols(b)])
                dve.wait_ge(*normed.at(("D0", b)))
            dve.wait_ge(d_const, 48)
            with layers(dve, "D") as L:
                d_dve_layer(dve, L)
            for b in range(B):
                dve.tensor_tensor(x[:, cols(b)], x[:, cols(b)], o[:, cols(b)], ALU.add).then_inc(*x_new.mark(("D", b)))

        def d_weights(sp, l):
            def at_(name, w):
                return A[name][bass.ds(l * 128, 128), :]
            for dst, name in ((Dw.rearrange("p a b -> p (a b)"), "D_w"), (Db[:, 0:12], "D_b"), (omr, "D_om"), (DW1, "D_w1"),
                              (DW2.rearrange("p a b -> p (a b)"), "D_w2")):
                sp.dma_start(dst, A[name][bass.ds(l * 128, 128), :]).then_inc(d_loaded, 16)
            sp.dma_start(bv[0:1, 0:64], A["D_bv"][bass.ds(l, 1), 0:64]).then_inc(d_loaded, 16)
            sp.dma_start(bv[0:1, 64:128], A["D_bv"][bass.ds(l, 1), 64:128]).then_inc(d_loaded, 16)

        def d_sp(sp):
            sp.wait_ge(*x_new.at(("C", 1)))
            sp.dma_start(OmS, A["OmS"]).then_inc(d_const, 16)
            sp.dma_start(Bn, A["Bn"]).then_inc(d_const, 16)
            sp.dma_start(own, A["own"]).then_inc(d_const, 16)
            d_weights(sp, 0)
            with layers(sp, "D", LAYERS - 1) as L:
                sp.wait_ge(*d_used.at("layer"))
                d_weights(sp, L + 1)

        f_tab, f_used, ga, gg, f_mul = sg("f_tab"), sg("f_used"), sg("ga"), sg("gg"), sg("f_mul")
        f_const, fa_loaded, ff_loaded, fa_used = raw("f_const"), raw("fa_loaded"), raw("ff_loaded"), sg("fa_used")

        def f_pe_layer(pe, L):
            pe.wait_ge(fa_loaded, L * 48 + 48)
            attn_pe(pe, "F", lambda b: xsh[:, b, :], True)
            pe.wait_ge(ff_loaded, L * 80 + 80)
            for b in range(B):
                norm_pe(pe, "F1", b, b, xsh[:, b, :], wait=(shifted.at(("F2", b)),))
            for b in range(B):
                pe.wait_ge(*affine.at(("F", b)))
                for i, (c0, m) in enumerate(DIC):
                    for j in range(2):
                        k = 2 * i + j
                        take(pe, k)
                        pe.matmul(ps[0:m, k, :], W1[:, DI * j + c0:DI * j + c0 + m], xn[:, b, :], start=True, stop=True)\
                            .then_inc(*full[k].mark(("F", b, "f", k)))
                take(pe, 6)
                for i, (c0, m) in enumerate(DIC):
                    pe.wait_ge(*f_mul.at((b, i)))
                    last = pe.matmul(ps[:, 6, :], W2[0:m, i, :], fh[0:m, i, :], start=i == 0, stop=i == 2)
                last.then_inc(*full[6].mark(("F", b, "f2")))

        def f_pe(pe):
            for b in range(B):
                norm_pe(pe, "F0", b, b, x[:, cols(b)], wait=(x_new.at(("E", b)),))
            pe.wait_ge(f_const, 48)
            with layers(pe, "F") as L:
                f_pe_layer(pe, L)

        def f_act_layer(act, L):
            attn_act(act, "F", True)
            for b in range(B):
                norm_act(act, "F1", b, b, None, 0)
            for b in range(B):
                act.wait_ge(*normed.at(("F1", b)))
                act.activation(xn[:, b, :], xn[:, b, :], ACT.Identity, bias=lng[:, 1:2], scale=lng[:, 0:1]).then_inc(*affine.mark(("F", b)))
            for b in range(B):
                for i, (c0, m) in enumerate(DIC):
                    k = 2 * i + 1
                    act.wait_ge(*full[k].at(("F", b, "f", k)))
                    if b == 1:
                        act.wait_ge(*f_mul.at((0, i)))
                    act.activation(fg[0:m, i, :], ps[0:m, k, :], ACT.Gelu, bias=b1[0:m, 3 + i:4 + i]).then_inc(*gg.mark((b, i)))
                    read(act, k, gg, (b, i))
            act.preload_act_table_set("natural_log_exp_and_others")

        def f_act(act):
            for b in range(B):
                norm_act(act, "F0", b, b, None, 0)
            act.preload_act_table_set("natural_log_exp_and_others")
            with layers(act, "F") as L:
                f_act_layer(act, L)

        xsh = sb("xsh", [128, B, T])
        aside = sb("aside", [128, B, T])

        def shift_dve(dve, key, b):
            step(dve, dve_step, dve.tensor_copy(xsh[0:64, b, :], x[0:64, cols(b)]))
            dve.tensor_copy(xsh[64:128, b, 1:T], x[64:128, T * b:T * b + T - 1]).then_inc(*shifted.mark((key, b)))

        def f_dve_layer(dve, L):
            dve.wait_ge(fa_loaded, L * 48 + 48)
            for j in range(4):
                ins = dve.tensor_scalar(tab[:, j, :], tab0[:, j, :], scl[:, j:j + 1], None, ALU.mult)
            step(dve, dve_step, ins)
            for b in range(B):
                shift_dve(dve, "F1", b)
            attn_dve(dve, "F", True)
            for b in range(B):
                dve.wait_ge(*x_new.at(("F", b)))
                shift_dve(dve, "F2", b)
                dve.wait_ge(*shifted.at(("F2", b)))
            for b in range(B):
                norm_dve(dve, "F1", b, b, xsh[:, b, :])
            dve.wait_ge(ff_loaded, L * 80 + 80)
            for b in range(B):
                for i, (c0, m) in enumerate(DIC):
                    k = 2 * i
                    dve.wait_ge(*full[k].at(("F", b, "f", k)))
                    dve.wait_ge(*gg.at((b, i)))
                    if b == 1:
                        dve.wait_ge(*full[6].at(("F", 0, "f2")))
                    dve.scalar_tensor_tensor(fh[0:m, i, :], ps[0:m, k, :], b1[0:m, i:i + 1], fg[0:m, i, :], ALU.add, ALU.mult)\
                        .then_inc(*f_mul.mark((b, i)))
                    read(dve, k, f_mul, (b, i))
                dve.wait_ge(*full[6].at(("F", b, "f2")))
                dve.scalar_tensor_tensor(x[:, cols(b)], ps[:, 6, :], lng[:, 2:3], x[:, cols(b)], ALU.add, ALU.add).then_inc(*x_new.mark(("Ff", b)))
                read(dve, 6, x_new, ("Ff", b))
            dve.sem_inc(f_used.mark("layer")[0], 1)

        def f_dve(dve):
            step(dve, dve_step, dve.memset(xsh[:, :, :], 0.0))
            step(dve, dve_step, dve.memset(P, 0.0))
            for b in range(B):
                norm_dve(dve, "F0", b, b, x[:, cols(b)])
                dve.tensor_copy(aside[:, b, :], x[:, cols(b)]).then_inc(*x_new.mark(("aside", b)))
                dve.wait_ge(*x_new.at(("aside", b)))
                dve.wait_ge(*normed.at(("F0", b)))
                dve.tensor_copy(x[:, cols(b)], xn[:, b, :]).then_inc(*x_new.mark(("F0", b)))
                dve.wait_ge(*x_new.at(("F0", b)))
            dve.wait_ge(f_const, 48)
            with layers(dve, "F") as L:
                f_dve_layer(dve, L)
            for b in range(B):
                dve.wait_ge(*x_new.at(("Ff", b)))
                dve.tensor_tensor(x[:, cols(b)], x[:, cols(b)], aside[:, b, :], ALU.add).then_inc(*x_new.mark(("F_end", b)))

        def f_pool(pool):
            with layers(pool, "F") as L:
                attn_pool(pool, "F", True)

        def fa_weights(sp, l):
            for dst, name in ((Wqkv.rearrange("p a b -> p (a b)"), "F_w"), (scl, "F_scl"), (Wo.rearrange("p a b -> p (a b)"), "F_wo")):
                sp.dma_start(dst, A[name][bass.ds(l * 128, 128), :]).then_inc(fa_loaded, 16)

        def ff_weights(sp, l):
            for dst, name in ((W1, "F_w1"), (W2.rearrange("p a b -> p (a b)"), "F_w2"), (b1, "F_b1"), (lng[:, 0:2], "F_ln"), (lng[:, 2:3], "F_b2")):
                sp.dma_start(dst, A[name][bass.ds(l * 128, 128), :]).then_inc(ff_loaded, 16)

        def f_sp(sp):
            sp.wait_ge(*x_new.at(("E", 1)))
            for dst, name in ((tab0, "tabF"), (seg, "seg"), (spread, "spread")):
                sp.dma_start(dst, A[name]).then_inc(f_const, 16)
            fa_weights(sp, 0)
            ff_weights(sp, 0)
            with layers(sp, "F", LAYERS - 1) as L:
                sp.wait_ge(*x_new.at(("F", 1)))
                fa_weights(sp, L + 1)
                sp.wait_ge(*f_used.at("layer"))
                ff_weights(sp, L + 1)
        block = c.enter_context(nc.Block())

        def load(eng, dst, src, sem):
            eng.dma_start(dst, src).then_inc(sem, 16)

        n_const = 18 * 16

        @block.sync
        def _(sp):
            lst = ((x[:, :], "x"), (mean_m[:, :], "mean_m"), (ident[:, :], "ident"), (identb[:, :], "identb"),
                   (band[:, :], "band"), (ones[:, :], "ones"), (eps5[:, :], "eps5"), (tab0, "tab0"), (Wqkv, "A_w"),
                   (Wo, "A_wo"), (ctxT, "ctx"), (Bw, "B_w"), (Bb, "B_b"), (Ew, "E_w"), (Eb, "E_b"), (hmask, "hmask"),
                   (Cw, "C_w"), (tri, "tri"))
            for dst, name in lst:
                load(sp, dst, A[name], const_in)
            if STAGE >= 4:
                d_sp(sp)
            if STAGE >= 6:
                f_sp(sp)
            sp.wait_ge(*x_new.at((LAST if STAGE < 6 else "F_end", 1)))
            sp.dma_start(out, x[:, :]).then_inc(stored, 16)
            sp.wait_ge(stored, 16)

        @block.tensor
        def _(pe):
            pe.wait_ge(const_in, n_const)
            for b in range(B):
                norm_pe(pe, "A1", b, b, x[:, cols(b)])
            for b in range(B):
                norm_pe(pe, "A2", b, b, None, center=False)
            attn_pe(pe, "A", lambda b: xn[:, b, :], False)
            if STAGE >= 2:
                b_pe(pe)
            if STAGE >= 3:
                c_pe(pe)
            if STAGE >= 4:
                d_pe(pe)
            if STAGE >= 5:
                e_pe(pe, "D")
            if STAGE >= 6:
                f_pe(pe)

        @block.scalar
        def _(act):
            act.preload_act_table_set("natural_log_exp_and_others")
            act.wait_ge(const_in, n_const)
            for b in range(B):
                norm_act(act, "A1", b, b, None, 0)
            for b in range(B):
                norm_act(act, "A2", b, b, xn[:, b, :], 1, center=False, wait=(normed.at(("A1", b)),))
            attn_act(act, "A", False)
            if STAGE >= 2:
                b_act(act)
            if STAGE >= 3:
                c_act(act)
            if STAGE >= 4:
                d_act(act)
            if STAGE >= 5:
                act.wait_ge(*vv_one.at("ones"))
                e_act(act)
            if STAGE >= 6:
                f_act(act)

        @block.vector
        def _(dve):
            step(dve, dve_step, dve.memset(P, 0.0))
            dve.wait_ge(const_in, n_const)
            for b in range(B):
                norm_dve(dve, "A1", b, b, x[:, cols(b)])
            for b in range(B):
                norm_dve(dve, "A2", b, b, xn[:, b, :], center=False)
            attn_dve(dve, "A", False)
            if STAGE >= 2:
                b_dve(dve)
            if STAGE >= 3:
                c_dve(dve)
            if STAGE >= 4:
                d_dve(dve)
            if STAGE >= 5:
                e_dve(dve)
            if STAGE >= 6:
                f_dve(dve)

        @block.gpsimd
        def _(pool):
            attn_pool(pool, "A", False)
            if STAGE >= 6:
                f_pool(pool)
        print([(taken[k].n, free[k].n) for k in range(8)])


def swapped(w):
    w = w.reshape(*w.shape[:-1], H, 2, D // 2)
    return w[..., ::-1, :].reshape(*w.shape[:-3], INNER)

def five(w):
    q, k, v = (w[..., i * INNER:(i + 1) * INNER] for i in range(3))
    import numpy as np
    return np.stack([q, k, v, swapped(q), swapped(k)], -2)


def more(a, f, np):
    w = lambda p: np.stack([f(p + n).T for n in ("Wq", "Wk", "Wv", "Wo")], 1)
    bb = lambda p: np.stack([f(p + n) for n in ("bq", "bk", "bv", "bo")], 1)
    a["ctx"] = f("ctx_1024").transpose(2, 0, 1)
    a["B_w"], a["B_b"] = w("L0_xattn_"), bb("L0_xattn_")
    a["E_w"], a["E_b"] = w("L1_xattn_"), bb("L1_xattn_")
    a["hmask"] = (np.arange(128)[:, None] // DS == np.arange(HS)[None, :]).astype(np.float32)
    cw = np.zeros((128, 70 * FB), np.float32)
    for j, n in enumerate(("gate", "up")):
        for ch in range(3):
            part = f("L0_ffn_w_" + n)[128 * ch:128 * ch + 128]
            cw[:len(part), 384 * j + 128 * ch:384 * j + 128 * ch + 128] = part
    cw[:, 768:] = f("L0_ffn_w_down")
    a["C_w"] = cw.reshape(128, 70, FB)
    i = np.arange(128)
    a["tri"] = (i[:, None] <= i[None, :]).astype(np.float32)
    lay = lambda name: f("L1_attn_" + name)
    rows = lambda v: v.reshape(-1, v.shape[-1])
    L = LAYERS
    a["D_w"] = rows(np.stack([lay(n) for n in ("Wq", "Wk", "Wv", "Wo")], 2).reshape(L, 128, 512))
    a["D_b"] = rows(np.concatenate([np.stack([lay(n) for n in ("bq", "bk", "bo", "g1", "be1", "g2", "be2", "bf2")], 2),
                                    lay("bf1").reshape(L, 4, 128).transpose(0, 2, 1)], 2))
    a["D_bv"] = lay("bv")
    a["D_om"] = rows(np.tile(lay("omega"), (1, HS, 1)))
    a["D_w1"] = rows(lay("W1"))
    a["D_w2"] = rows(lay("W2").reshape(L, 4, 128, 128).transpose(0, 2, 1, 3).reshape(L, 128, 512))
    same = np.arange(128)[:, None] // DS == np.arange(512)[None, :] // 32
    slot = np.arange(512)[None, :] % 32
    a["OmS"] = (same * np.where(slot < 8, 1.0, np.where(slot < 16, -1.0, 0.0))).astype(np.float32)
    a["Bn"] = (same * np.where(slot < 16, -0.5, 0.0)).astype(np.float32)
    p_, c_ = np.arange(128)[:, None], np.arange(144)[None, :]
    a["own"] = ((p_ // 32 == c_ // 9 % 4) & (p_ % 32 < 16)).astype(np.float32)
    g = lambda name: f("L1_ffn_" + name)
    a["F_w"] = rows(five(g("Wqkv")).reshape(L, 128, 5 * INNER))
    a["F_wo"] = rows(g("Wo").reshape(L, NP, 128, C).transpose(0, 2, 1, 3).reshape(L, 128, NP * C))
    sw = lambda v: np.concatenate([v[:, D // 2:], v[:, :D // 2]], 1)
    qs_, ks_ = g("q_scale"), g("k_scale")
    a["F_scl"] = rows(np.stack([np.tile(v, (1, 2)) for v in (qs_, sw(qs_), ks_, sw(ks_))], 2))
    a["F_w1"] = rows(g("W1"))

    def parts(v):
        z = np.zeros((L, 3 * 128, v.shape[2]), np.float32)
        z[:, :DI] = v
        return z.reshape(L, 3, 128, -1).transpose(0, 2, 1, 3)
    a["F_w2"] = rows(parts(g("W2")).reshape(L, 128, 3 * C))
    a["F_b1"] = rows(np.concatenate([parts(g("b1")[:, :DI, None])[..., 0], parts(g("b1")[:, DI:, None])[..., 0]], 2))
    a["F_ln"] = rows(np.stack([g("ln_g"), g("ln_b")], 2))
    a["F_b2"] = rows(g("b2")[:, :, None])
    seg = (i[:, None] // D == np.arange(2)[None, :]).astype(np.float32)
    spread = (i[:, None] // D == i[None, :] // D).astype(np.float32)
    a["seg"], a["spread"] = seg, spread



def kernel(**inp):
    import numpy as np
    import concourse.bacc as bacc
    from concourse.bass_utils import run_bass_kernel_spmd as run

    f = lambda name: np.asarray(inp[name])
    a = {}
    a["x"] = f("x").reshape(N, C).T
    a["mean_m"] = np.full((128, 128), 1 / 128, np.float32)
    a["ident"] = np.eye(128, dtype=np.float32)
    import ml_dtypes
    a["identb"] = np.eye(128).astype(ml_dtypes.bfloat16)
    q, k = np.arange(128)[:, None], np.arange(160)[None, :]
    see = (k >= q) & (k <= q + WIN)
    see = np.concatenate([see & (k >= WIN), see, see], 1)
    a["band"] = np.where(see, 0.0, NEG).astype(ml_dtypes.bfloat16)
    a["ones"] = np.ones((1, 128), np.float32)
    e = np.zeros((128, 4), np.float32)
    e[:] = [1e-5, 1e-6, math.log(0.25), 10 * math.log(2)]
    a["eps5"] = e
    half = np.arange(0, D, 2, dtype=np.float32)
    freqs = np.arange(T, dtype=np.float32)[:, None] * (1.0 / 10000.0 ** (half / D)).astype(np.float32)[None, :]
    cos, sin = np.cos(freqs).T, np.sin(freqs).T
    cos2 = np.concatenate([cos] * 4, 0)
    sin2 = np.concatenate([-sin, sin] * 2, 0)
    a["tab0"] = np.stack([cos2, sin2, cos2, sin2], 1).astype(np.float32)
    base = (half + 0.4 * D) / (1.4 * D)
    power = (np.arange(T, dtype=np.float32) - T // 2) / (WIN // 2)
    sc = (base[:, None] ** power[None, :]).astype(np.float32)
    sc = np.concatenate([sc] * 4, 0)
    a["tabF"] = np.stack([cos2 * sc, sin2 * sc, cos2 / sc, sin2 / sc], 1).astype(np.float32)

    a["A_w"] = five(f("L0_attn_w_qkv").T)
    a["A_wo"] = f("L0_attn_w_out").T.reshape(NP, 128, C).transpose(1, 0, 2)
    more(a, f, np)
    a = {k: np.ascontiguousarray(v) for k, v in a.items()}
    book = {}
    for turn in range(2):
        nc = bacc.Bacc("TRN2", target_bir_lowering=False, num_devices=1)
        A = {k: nc.dram_tensor(f"in_{k}", v.shape, mybir.dt.from_np(v.dtype), kind="ExternalInput").ap() for k, v in a.items()}
        out = nc.dram_tensor("out_x", (128, N), F32, kind="ExternalOutput").ap()
        build(nc, A, out, book)
    r = run(nc, [{f"in_{k}": v for k, v in a.items()}], core_ids=[0])
    return np.ascontiguousarray(r.results[0]["out_x"].T).reshape(B, T, C)
```

```python
import math
from contextlib import ExitStack, contextmanager

import concourse.bass as bass
from concourse import mybir

F32 = mybir.dt.float32
BF16 = mybir.dt.bfloat16
ALU = mybir.AluOpType
ACT = mybir.ActivationFunctionType
AX = mybir.AxisListType.X

B, T, C = 2, 512, 128
N = B * T
NT = T // 128
S = 154
SH = S // 2
H, D = 16, 64
NP = H // 2
WIN = 32
INNER = H * D
TOPK = 32
I0 = 352
FB = 16
FS = 16
HS, DS = 16, 8
DFF = 512
LAYERS = 6
DI = int(128 * 4 * 2 / 3)
DIC = [(0, 128), (128, 128), (256, DI - 256)]
NEG = -1e30


class Signal:
    every = []

    def __init__(self, book, name, sem):
        self.book = book.setdefault(name, {"key": {}, "per": {}})
        self.sem, self.name, self.n = sem, name, 0
        self.seen = set()
        Signal.every.append(self)

    def mark(self, key=None):
        self.n += 1
        if key is not None:
            assert key not in self.seen, key
            self.seen.add(key)
            self.book["key"][key] = (Loop.now, self.n)
        return self.sem, 1

    def value(self, loop, n):
        if loop is None:
            return n
        per = self.book["per"].get(loop, 0)
        if Loop.now == loop:
            return Loop.reg * per + n if per else n
        return n + (LAYERS - 1) * per

    def at(self, key):
        loop, n = self.book["key"].get(key, (None, 1))
        return self.sem, self.value(loop, n)


class Loop:
    now, reg = None, None


@contextmanager
def layers(eng, name, trips=LAYERS):
    before = {s: s.n for s in Signal.every}
    with eng.Fori(0, trips) as reg:
        Loop.now, Loop.reg = name, reg
        yield reg
    for s, n in before.items():
        if s.n != n:
            s.book["per"][name] = s.n - n
            s.n = n + trips * (s.n - n)
    Loop.now = None


def build(nc, A, out, book):
    Signal.every = []
    nc.disable_value_cache = True
    with ExitStack() as c:
        def sb(name, shape, dt=F32):
            return c.enter_context(nc.sbuf_tensor(name, shape, dt))

        def sg(name):
            return Signal(book, name, c.enter_context(nc.semaphore(name)))

        def raw(name):
            return c.enter_context(nc.semaphore(name))

        ps = c.enter_context(nc.psum_tensor("ps", [128, 8, 512], F32))

        x = sb("x", [128, N])
        mean_m = sb("mean_m", [128, 128])
        ident = sb("ident", [128, 128])
        identb = sb("identb", [128, 128], BF16)
        band = sb("band", [128, 480], BF16)
        eps5 = sb("eps5", [128, 6])
        xc = sb("xc", [128, B, T])
        sq = sb("sq", [128, B, T])
        rs = sb("rs", [128, B, T])
        xn = sb("xn", [128, B, T])
        big = sb("big", [128, 40000])

        class Area:
            def __init__(self):
                self.at = 0

            def __call__(self, *dims):
                n = math.prod(dims)
                v = big[:, self.at:self.at + n]
                self.at += n
                assert self.at <= 40000, self.at
                if len(dims) == 2:
                    return v.rearrange("p (a b) -> p a b", a=dims[0])
                if len(dims) == 3:
                    return v.rearrange("p (a b c) -> p a b c", a=dims[0], b=dims[1])
                return v

        full = [sg(f"full{k}") for k in range(8)]
        free = [sg(f"free{k}") for k in range(8)]
        taken = [Signal(book, f"taken{k}", None) for k in range(8)]
        dve_step, act_step = sg("dve_step"), sg("act_step")
        first_in, second_in, third_in, stored = raw("first_in"), raw("second_in"), raw("third_in"), raw("stored")
        centred, squared, rooted, normed = sg("centred"), sg("squared"), sg("rooted"), sg("normed")
        x_new = sg("x_new")

        def take(pe, *banks):
            for k in banks:
                t = taken[k]
                per = t.book["per"].get(Loop.now, 0) if Loop.now else 0
                v = (Loop.reg * per + t.n) if per else t.n
                if t.n > 0:
                    pe.wait_ge(free[k].sem, v)
                t.mark()

        def step(eng, sgn, ins):
            ins.then_inc(*sgn.mark(("step", sgn.n)))
            eng.wait_ge(*sgn.at(("step", sgn.n - 1)))

        def read(eng, bank, sgn, key):
            eng.wait_ge(*sgn.at(key))
            eng.sem_inc(free[bank].mark()[0], 1)

        def norm_pe(pe, key, b, bank, src, wait=(), center=True):
            for w in wait:
                pe.wait_ge(*w)
            if center:
                take(pe, bank)
                pe.matmul(ps[:, bank, :], mean_m[:, :], src, start=True, stop=True).then_inc(*full[bank].mark((key, b, "mean")))
            pe.wait_ge(*squared.at((key, b)))
            take(pe, bank)
            pe.matmul(ps[:, bank, :], mean_m[:, :], sq[:, b, :], start=True, stop=True).then_inc(*full[bank].mark((key, b, "var")))

        def norm_dve(dve, key, b, bank, src, center=True, out_=None):
            if center:
                dve.wait_ge(*full[bank].at((key, b, "mean")))
                dve.tensor_tensor(xc[:, b, :], src, ps[:, bank, :], ALU.subtract).then_inc(*centred.mark((key, b)))
                dve.wait_ge(*centred.at((key, b)))
            dve.wait_ge(*rooted.at((key, b)))
            dve.tensor_tensor(xn[:, b, :] if out_ is None else out_, xc[:, b, :] if center else src, rs[:, b, :],
                              ALU.mult).then_inc(*normed.mark((key, b)))

        def norm_act(act, key, b, bank, src, eps, center=True, wait=()):
            if center:
                act.wait_ge(*centred.at((key, b)))
                act.sem_inc(free[bank].mark()[0], 1)
                act.activation(sq[:, b, :], xc[:, b, :], ACT.Square).then_inc(*squared.mark((key, b)))
            else:
                for w in wait:
                    act.wait_ge(*w)
                act.activation(sq[:, b, :], src, ACT.Square).then_inc(*squared.mark((key, b)))
            act.wait_ge(*full[bank].at((key, b, "var")))
            step(act, act_step, act.activation(rs[:, b, :], ps[:, bank, :], ACT.Ln, bias=eps5[:, eps:eps + 1]))
            act.sem_inc(free[bank].mark()[0], 1)
            act.activation(rs[:, b, :], rs[:, b, :], ACT.Exp, scale=-0.5).then_inc(*rooted.mark((key, b)))

        ar = Area()
        Wqkv = ar(5, INNER)
        Wo = ar(NP, C)
        KT = ar(NP, T)
        OT = KT
        V = ar(NT, INNER)
        V2 = ar(NT, INNER)
        tab0 = ar(4, T)
        tab = ar(4, T)
        tmp = ar(2, 4, T)
        QZ = ar(NP, 2 * T)
        P = ar(3, 512)
        PT = ar(2, 512)
        rq = ar(NT, H)
        seg = ar(2)
        spread = ar(128)
        scl = ar(4)
        W1 = ar(2 * DI)
        W2 = ar(3, C)
        b1 = ar(6)
        lng = ar(3)
        knr = xc
        qsq, ksq = sq, xn
        fg = KT[:, 0:3, :]
        fh = KT[:, 3:6, :]
        nm = sb("nm", [128, 3, 16])
        QKV = ("q", "r", "k", "s")
        wsel = {"q": 0, "k": 1, "v": 2, "r": 3, "s": 4}
        roped, v_ready, k_sq, q_sq = sg("roped"), sg("v_ready"), sg("k_sq"), sg("q_sq")
        part1, part2 = sg("part1"), sg("part2")
        k_norm, q_norm, k_raised = sg("k_norm"), sg("q_norm"), sg("k_raised")
        guarded, k_added, inverted, rq_ready = sg("guarded"), sg("k_added"), sg("inverted"), sg("rq_ready")
        v2_in, zeroed = raw("v2_in"), sg("zeroed")
        topped, exped, scaled, turned, merged = sg("topped"), sg("exped"), sg("scaled"), sg("turned"), sg("merged")
        shifted = sg("shifted")

        UNITS = 2 * NP
        NW = T // 64
        KW = 64 + WIN
        rq8 = sb("rq8", [128, 2, NT, NP])

        def unit(u):
            return u // 2, 4 * (u % 2)

        def attn_pe(pe, key, src, l2, between={}):
            for b in range(B):
                src_ready(pe, key, b)
                for p in range(NP + 1):
                    if p < NP:
                        for j, w in enumerate(QKV):
                            take(pe, j)
                            pe.matmul(ps[:, j, :], Wqkv[:, wsel[w], 128 * p:128 * p + 128], src(b), start=True, stop=True)\
                                .then_inc(*full[j].mark((key, b, p)))
                            if l2 and p > 0 and w == "q":
                                l2_pe(pe, key, b, p - 1)
                        t, hf = p // 2, p % 2
                        take(pe, 4)
                        pe.matmul(ps[:, 4, :], src(b)[:, 128 * t:128 * t + 128], Wqkv[:, 2, 512 * hf:512 * hf + 512],
                                  start=True, stop=True).then_inc(*full[4].mark((key, b, "v", p)))
                    elif l2:
                        l2_pe(pe, key, b, p - 1)
                for u in range(UNITS + 3):
                    if u < UNITS:
                        p, m0 = unit(u)
                        pe.wait_ge(*roped.at((key, b, p)))
                        pe.wait_ge(*(k_raised if l2 else k_added).at((key, b, p)))
                        sl = u % 3
                        take(pe, sl)
                        off = 0 if m0 == 0 else KW
                        pe.matmul(ps[:, sl, 0:4 * KW], identb[:, :], band[:, off:off + 4 * KW], start=True, stop=False)
                        for j in range(4):
                            m = m0 + j
                            k0 = WIN if m == 0 else 0
                            last = pe.matmul(ps[:, sl, KW * j + k0:KW * j + KW], QZ[:, p, 128 * m:128 * m + 128],
                                             KT[:, p, 64 * m - WIN + k0:64 * m + 64], start=False, stop=j == 3)
                        last.then_inc(*full[sl].mark((key, b, "s", u)))
                    if l2 and u == 0:
                        pe.wait_ge(*q_norm.at((key, b)))
                        take(pe, 6)
                        rv = rq.rearrange("p t (q e) -> p e t q", e=2)
                        for par in range(2):
                            for h in range(2):
                                last = pe.matmul(ps[64 * h:64 * h + 64, 6, 32 * par:32 * par + 32], ident[:, 64 * par:64 * par + 64],
                                                 rv[:, h, :, :], start=True, stop=True, tile_position=(0, 64 * h))
                        last.then_inc(*full[6].mark((key, b, "rq")))
                    if 0 <= u - 2 < UNITS:
                        w = u - 2
                        tb = 4 + w % 2
                        pe.wait_ge(*scaled.at((key, b, w)))
                        take(pe, tb)
                        for j in range(4):
                            last = pe.transpose(ps[:, tb, 128 * j:128 * j + 128], P[:, w % 3, 128 * j:128 * j + 128], ident[:, :])
                        last.then_inc(*full[tb].mark((key, b, w)))
                    if u >= 3:
                        w = u - 3
                        p, m0 = unit(w)
                        ob = 6 + w % 2
                        pe.wait_ge(*turned.at((key, b, w)))
                        if w == 0:
                            pe.wait_ge(v2_in, v2_count(b))
                        take(pe, ob)
                        for j in range(4):
                            m = m0 + j
                            n, vv = (KW, V2) if m % 2 == 0 else (128, V)
                            last = pe.matmul(ps[:, ob, 128 * j:128 * j + 128], vv[0:n, m // 2, 128 * p:128 * p + 128],
                                             PT[0:n, w % 2, 128 * j:128 * j + 128], start=True, stop=True)
                        last.then_inc(*full[ob].mark((key, b, "o", w)))
                    if b == 1 and u in between:
                        between[u]()
                take(pe, 3)
                for p in range(NP):
                    pe.wait_ge(*merged.at((key, b, 2 * p + 1)))
                    last = pe.matmul(ps[:, 3, :], Wo[:, p, :], OT[:, p, :], start=p == 0, stop=p == NP - 1)
                last.then_inc(*full[3].mark((key, b, "y")))

        def l2_pe(pe, key, b, p):
            pe.wait_ge(*k_sq.at((key, b, p)))
            take(pe, 5)
            pe.matmul(ps[:, 5, :], spread[:, :], ksq[:, p % 2, :], start=True, stop=True).then_inc(*full[5].mark((key, b, "ssk", p)))
            pe.wait_ge(*q_sq.at((key, b, p)))
            if p == 0:
                take(pe, 7)
            for t in range(NT):
                last = pe.matmul(ps[:, 7, 16 * t + 2 * p:16 * t + 2 * p + 2], qsq[:, p % 2, 128 * t:128 * t + 128],
                                 seg[:, 0:2], start=True, stop=True)
            last.then_inc(*full[7].mark((key, b, "ssq", p)))

        def k_norm_act(act, key, b, p):
            kn = knr[:, p % 2, :]
            act.wait_ge(*guarded.at((key, b, p)))
            step(act, act_step, act.activation(kn, kn, ACT.Ln, scale=2.0 ** 20))
            act.activation(kn, kn, ACT.Exp, scale=-0.5, bias=eps5[:, 3:4]).then_inc(*k_norm.mark((key, b, p)))

        def k_guard_dve(dve, key, b, p):
            dve.wait_ge(*full[5].at((key, b, "ssk", p)))
            if p >= 2:
                dve.wait_ge(*k_raised.at((key, b, p - 2)))
            elif b > 0:
                dve.wait_ge(*k_raised.at((key, b - 1, NP - 2 + p)))
            dve.tensor_scalar(knr[:, p % 2, :], ps[:, 5, :], 1e-24, None, ALU.max).then_inc(*guarded.mark((key, b, p)))
            read(dve, 5, guarded, (key, b, p))

        def attn_act(act, key, l2, between={}):
            for b in range(B):
                for p in range(NP):
                    if l2:
                        if p >= 2:
                            act.wait_ge(*full[7].at((key, b, "ssq", p - 2)))
                        act.wait_ge(*full[0].at((key, b, p)))
                        act.activation(qsq[:, p % 2, :], ps[:, 0, :], ACT.Square).then_inc(*q_sq.mark((key, b, p)))
                        if p > 0:
                            k_norm_act(act, key, b, p - 1)
                        act.wait_ge(*full[2].at((key, b, p)))
                        act.activation(ksq[:, p % 2, :], ps[:, 2, :], ACT.Square).then_inc(*k_sq.mark((key, b, p)))
                    t, hf = p // 2, p % 2
                    act.wait_ge(*full[4].at((key, b, "v", p)))
                    act.activation(V[:, t, 512 * hf:512 * hf + 512], ps[:, 4, :], ACT.Copy).then_inc(*v_ready.mark((key, b, p)))
                    read(act, 4, v_ready, (key, b, p))
                if l2:
                    act.wait_ge(*guarded.at((key, b, "q")))
                    step(act, act_step, act.activation(rq, rq, ACT.Ln, scale=2.0 ** 20))
                    act.activation(rq, rq, ACT.Exp, scale=-0.5, bias=eps5[:, 3:4]).then_inc(*q_norm.mark((key, b)))
                    k_norm_act(act, key, b, NP - 1)
                for u in range(UNITS + 2):
                    if u < UNITS:
                        p, m0 = unit(u)
                        sl = u % 3
                        act.wait_ge(*topped.at((key, b, u)))
                        for j in range(4):
                            sc = rq8[:, j % 2, (m0 + j) // 2, p:p + 1] if l2 else D ** -0.5
                            at0 = 128 * j + (WIN if j % 2 else 0)
                            ins = act.activation(P[:, u % 3, at0:at0 + KW], ps[:, sl, KW * j:KW * j + KW], ACT.Exp,
                                                 bias=nm[:, u % 3, 4 + j:5 + j], scale=sc, accum_out=nm[:, u % 3, 8 + j:9 + j])
                        ins.then_inc(*exped.mark((key, b, u)))
                        read(act, sl, exped, (key, b, u))
                    if u >= 2:
                        w = u - 2
                        tb = 4 + w % 2
                        act.wait_ge(*full[tb].at((key, b, w)))
                        if w >= 2:
                            act.wait_ge(*full[6 + w % 2].at((key, b, "o", w - 2)))
                        act.activation(PT[:, w % 2, :], ps[:, tb, :], ACT.Copy).then_inc(*turned.mark((key, b, w)))
                        read(act, tb, turned, (key, b, w))
                    if b == 1 and u in between:
                        between[u]()

        def attn_dve(dve, key, l2, between={}):
            for b in range(B):
                for p in range(NP):
                    if l2 and p > 0:
                        k_guard_dve(dve, key, b, p - 1)
                    for j, w in enumerate(QKV):
                        if l2 and w == "q":
                            dve.wait_ge(*q_sq.at((key, b, p)))
                        elif l2 and w == "k":
                            dve.wait_ge(*k_sq.at((key, b, p)))
                        else:
                            dve.wait_ge(*full[j].at((key, b, p)))
                        if j == 0 and (b, p) not in ((0, 0), (0, 1)):
                            dve.wait_ge(*roped.at((key, b, p - 2) if p >= 2 else (key, b - 1, NP - 2 + p)))
                        part = part1 if j < 2 else part2
                        dve.tensor_tensor(tmp[:, p % 2, j, :], ps[:, j, :], (tab if l2 else tab0)[:, j, :], ALU.mult)\
                            .then_inc(*part.mark((key, b, p, j)))
                        read(dve, j, part, (key, b, p, j))
                    dve.tensor_tensor(KT[:, p, :], tmp[:, p % 2, 2, :], tmp[:, p % 2, 3, :], ALU.add).then_inc(*k_added.mark((key, b, p)))
                    dve.wait_ge(*k_added.at((key, b, p)))
                if l2:
                    dve.wait_ge(*full[7].at((key, b, "ssq", NP - 1)))
                    dve.tensor_scalar(rq, ps[:, 7, 0:64].rearrange("p (t h) -> p t h", t=NT), 1e-24, None, ALU.max)\
                        .then_inc(*guarded.mark((key, b, "q")))
                    read(dve, 7, guarded, (key, b, "q"))
                    k_guard_dve(dve, key, b, NP - 1)
                    dve.wait_ge(*full[6].at((key, b, "rq")))
                    dve.tensor_scalar(rq8.rearrange("p a t q -> p (a t q)"), ps[:, 6, 0:64], 8.0, None, ALU.mult)\
                        .then_inc(*rq_ready.mark((key, b)))
                    read(dve, 6, rq_ready, (key, b))
                for u in range(UNITS + 4):
                    if u < UNITS:
                        p, m0 = unit(u)
                        i = u % 3
                        dve.wait_ge(*full[u % 3].at((key, b, "s", u)))
                        step(dve, dve_step, dve.tensor_reduce(nm[:, i, 0:4], ps[:, u % 3, 0:4 * KW].rearrange("p (i k) -> p i k", i=4),
                                                              AX, ALU.max))
                        if l2:
                            step(dve, dve_step, dve.tensor_tensor(
                                nm[:, i, 0:4].rearrange("p (t a) -> p t a", a=2), nm[:, i, 0:4].rearrange("p (t a) -> p t a", a=2),
                                rq8[:, :, m0 // 2:m0 // 2 + 2, p].rearrange("p a t -> p t a"), ALU.mult))
                        dve.tensor_scalar(nm[:, i, 4:8], nm[:, i, 0:4], -1.0 if l2 else -D ** -0.5, None, ALU.mult)\
                            .then_inc(*topped.mark((key, b, u)))
                    if 1 <= u <= UNITS:
                        i = (u - 1) % 3
                        dve.wait_ge(*exped.at((key, b, u - 1)))
                        dve.reciprocal(nm[:, i, 12:16], nm[:, i, 8:12]).then_inc(*inverted.mark((key, b, u - 1)))
                    if u >= 4:
                        merge_dve(dve, key, b, u - 4)
                    if b == 1 and u in between:
                        between[u]()
                dve.wait_ge(*full[3].at((key, b, "y")))
                dve.tensor_tensor(x[:, T * b:T * b + T], x[:, T * b:T * b + T], ps[:, 3, :], ALU.add)\
                    .then_inc(*x_new.mark((key, b)))
                read(dve, 3, x_new, (key, b))

        def merge_dve(dve, key, b, w):
            p, m0 = unit(w)
            ob = 6 + w % 2
            dve.wait_ge(*full[ob].at((key, b, "o", w)))
            for h in range(2):
                rows = slice(64 * h, 64 * h + 64)
                ins = dve.tensor_copy(OT[rows, p, 64 * m0:64 * m0 + 256].rearrange("p (m q) -> p m q", m=4),
                                      ps[rows, ob, :].rearrange("p (m h q) -> p m h q", m=4, h=2)[:, :, h, :])
            ins.then_inc(*merged.mark((key, b, w)))
            read(dve, ob, merged, (key, b, w))

        def attn_pool(pool, key, l2):
            for b in range(B):
                for p in range(NP + 1):
                    if l2 and p > 0:
                        w = p - 1
                        pool.wait_ge(*k_added.at((key, b, w)))
                        pool.wait_ge(*k_norm.at((key, b, w)))
                        pool.tensor_tensor(KT[:, w, :], KT[:, w, :], knr[:, w % 2, :], ALU.mult).then_inc(*k_raised.mark((key, b, w)))
                        pool.wait_ge(*k_raised.at((key, b, w)))
                    if p < NP:
                        pool.wait_ge(*part1.at((key, b, p, 1)))
                        for h in range(2):
                            rows = slice(64 * h, 64 * h + 64)
                            ins = pool.tensor_tensor(QZ[rows, p, :].rearrange("p (m h q) -> p m h q", m=NW, h=2)[:, :, h, :],
                                                     tmp[rows, p % 2, 0, :].rearrange("p (m q) -> p m q", m=NW),
                                                     tmp[rows, p % 2, 1, :].rearrange("p (m q) -> p m q", m=NW), ALU.add)
                        ins.then_inc(*roped.mark((key, b, p)))
                        pool.wait_ge(*roped.at((key, b, p)))
                for w in range(UNITS):
                    i = w % 3
                    pool.wait_ge(*inverted.at((key, b, w)))
                    v = P[:, i, :].rearrange("p (j k) -> p j k", j=4)
                    pool.tensor_tensor(v, v, nm[:, i, 12:16].unsqueeze(2).to_broadcast([128, 4, 128]), ALU.mult)\
                        .then_inc(*scaled.mark((key, b, w)))
                pool.wait_ge(*scaled.at((key, b, UNITS - 1)))

        V2_DMA = (2 * NT - 1) * 16

        def v2_count(b):
            done = Loop.reg * (B * V2_DMA) + (B * V2_DMA + (b + 1) * V2_DMA) if Loop.now else (b + 1) * V2_DMA
            return done

        def v2_sp(sp, key):
            for b in range(B):
                for t in range(NT):
                    sp.wait_ge(*v_ready.at((key, b, 2 * t + 1)))
                    sp.dma_start(V2[WIN:KW, t, :], V[0:64, t, :]).then_inc(v2_in, 16)
                    if t + 1 < NT:
                        sp.dma_start(V2[0:WIN, t + 1, :], V[96:128, t, :]).then_inc(v2_in, 16)

        moved = raw("moved")

        def src_ready(pe, key, b):
            if key == "A":
                pe.wait_ge(*normed.at(("A2", b)))
            else:
                pe.wait_ge(moved, Loop.reg * 2 + (b + 1))

        cols = lambda b: slice(T * b, T * b + T)

        fix = sb("fix", [128, 3100])
        fat = [0]

        def keep(*dims):
            n = math.prod(dims)
            v = fix[:, fat[0]:fat[0] + n]
            fat[0] += n
            assert fat[0] <= 3100, fat[0]
            return v if len(dims) == 1 else v.rearrange("p (a b) -> p a b", a=dims[0]) if len(dims) == 2 else \
                v.rearrange("p (a b c) -> p a b c", a=dims[0], b=dims[1])
        ctxT = keep(B, S)
        Bw = keep(4, C)
        Bb = keep(4)
        Ew = keep(4, C)
        Eb = keep(4)
        hmask = keep(HS)
        Cw = keep(70, FB)
        tri = keep(128)
        a2 = Area()
        qt = a2(T)
        kt = a2(S)
        vt = a2(2, C)
        vt1 = a2(2, HS * 9)
        sc_ = a2(2, S)
        rem = a2(2, S)
        pe_ = a2(2, S)
        msk = a2(S)
        m8 = a2(2, 40)
        pt2 = a2(2, 512)
        ctxo = a2(T)
        KB = a2(HS, S)
        PE_ = a2(HS, S)
        mx = a2(2, 16)
        atok = a2(128)
        aT = a2(T)
        rd = a2(HS)
        gT = a2(I0)
        uT = a2(I0)
        dT = a2(3, C)
        xq = a2(B, T)
        xqT = a2(B, T)
        hq = a2(B, NT * I0)
        hT = a2(3, T)
        qa = a2(1408)
        qu = a2(1408)
        qs = a2(1408)
        qb = a2(3, 88)
        eg = a2(2, I0)
        q_ready, k_ready, vv_ready = sg("q_ready"), sg("k_ready"), sg("vv_ready")
        picked, b_exp, b_prob, b_turn, b_ctx = sg("picked"), sg("b_exp"), sg("b_prob"), sg("b_turn"), sg("b_ctx")
        signed, q4, turned4, expg, hgate = sg("signed"), sg("q4"), sg("turned4"), sg("expg"), sg("hgate")
        kb_ready, e_max, e_exp, e_turn_a, e_turn_d, e_norm = sg("kb_ready"), sg("e_max"), sg("e_exp"), sg("e_turn_a"), sg("e_turn_d"), sg("e_norm")

        def qkv_pe(pe, key, b, w):
            pe.wait_ge(*normed.at((key + "1", b)))
            take(pe, 0)
            pe.matmul(ps[:, 0, :], w[:, 0, :], xn[:, b, :], start=True, stop=True).then_inc(*full[0].mark((key, b, "q")))
            take(pe, 1)
            pe.matmul(ps[:, 1, 0:S], w[:, 1, :], ctxT[:, b, :], start=True, stop=True).then_inc(*full[1].mark((key, b, "k")))
            take(pe, 2)
            for hf in range(2):
                last = pe.matmul(ps[0:SH, 2, 128 * hf:128 * hf + 128], ctxT[:, b, SH * hf:SH * hf + SH], w[:, 2, :],
                                 start=True, stop=True)
            last.then_inc(*full[2].mark((key, b, "v")))

        def qkv_act(act, key, b, bias):
            act.wait_ge(*full[0].at((key, b, "q")))
            act.activation(qt, ps[:, 0, :], ACT.Identity, bias=bias[:, 0:1]).then_inc(*q_ready.mark((key, b)))
            read(act, 0, q_ready, (key, b))
            act.wait_ge(*full[1].at((key, b, "k")))
            act.activation(kt, ps[:, 1, 0:S], ACT.Identity, bias=bias[:, 1:2]).then_inc(*k_ready.mark((key, b)))
            read(act, 1, k_ready, (key, b))
            act.wait_ge(*full[2].at((key, b, "v")))
            src = ps[0:SH, 2, 0:256].rearrange("p (a c) -> p a c", a=2)
            if key == "B":
                ins = act.activation(vt[0:SH, :, :], src, ACT.Copy)
            else:
                src = ps[0:SH, 2, 0:256].rearrange("p (a d) -> p a d", d=DS)
                ins = act.activation(vt1.rearrange("p a (h d) -> p (a h) d", d=9)[0:SH, :, 0:DS], src, ACT.Copy)
            ins.then_inc(*vv_ready.mark((key, b)))
            read(act, 2, vv_ready, (key, b))

        def out_pe(pe, key, b, w, src, wait):
            pe.wait_ge(*wait)
            take(pe, 3)
            pe.matmul(ps[:, 3, :], w, src, start=True, stop=True).then_inc(*full[3].mark((key, b, "y")))

        def out_dve(dve, key, b, bias, bank=3):
            dve.wait_ge(*full[bank].at((key, b, "y")))
            dve.scalar_tensor_tensor(x[:, cols(b)], ps[:, bank, :], bias, x[:, cols(b)], ALU.add, ALU.add)\
                .then_inc(*x_new.mark((key, b)))
            read(dve, bank, x_new, (key, b))

        def b_pe(pe):
            for b in range(B):
                norm_pe(pe, "B1", b, b, x[:, cols(b)], wait=(x_new.at(("A", b)),))
            for b in range(B):
                qkv_pe(pe, "B", b, Bw)
                pe.wait_ge(*q_ready.at(("B", b)))
                pe.wait_ge(*k_ready.at(("B", b)))
                for t in range(NT + 1):
                    if t < NT:
                        k = 4 + t % 2
                        take(pe, k)
                        pe.matmul(ps[:, k, 0:S], qt[:, 128 * t:128 * t + 128], kt, start=True, stop=True)\
                            .then_inc(*full[k].mark(("B", b, t)))
                    if t > 0:
                        u = t - 1
                        k = 6 + u % 2
                        pe.wait_ge(*b_prob.at((b, u)))
                        take(pe, k)
                        for hf in range(2):
                            last = pe.transpose(ps[0:SH, k, 128 * hf:128 * hf + 128], pe_[:, u % 2, SH * hf:SH * hf + SH], ident[:, :])
                        last.then_inc(*full[k].mark(("B", b, u)))
                        pe.wait_ge(*b_turn.at((b, u)))
                        if u == 0:
                            pe.wait_ge(*vv_ready.at(("B", b)))
                            take(pe, 2)
                        for hf in range(2):
                            last = pe.matmul(ps[:, 2, 128 * u:128 * u + 128], vt[0:SH, hf, :], pt2[0:SH, u % 2, 128 * hf:128 * hf + 128],
                                             start=hf == 0, stop=hf == 1)
                last.then_inc(*full[2].mark(("B", b, "o")))
                out_pe(pe, "B", b, Bw[:, 3, :], ctxo, b_ctx.at(("B", b)))

        def b_act(act):
            for b in range(B):
                norm_act(act, "B1", b, b, None, 0)
            for b in range(B):
                qkv_act(act, "B", b, Bb)
                for t in range(NT + 1):
                    if t < NT:
                        act.wait_ge(*picked.at((b, t)))
                        act.activation(pe_[:, t % 2, :], sc_[:, t % 2, :], ACT.Exp, bias=m8[:, t % 2, 32:33], scale=C ** -0.5)\
                            .then_inc(*b_exp.mark((b, t)))
                    if t > 0:
                        u = t - 1
                        k = 6 + u % 2
                        act.wait_ge(*full[k].at(("B", b, u)))
                        act.activation(pt2[0:SH, u % 2, 0:256], ps[0:SH, k, 0:256], ACT.Copy).then_inc(*b_turn.mark((b, u)))
                        read(act, k, b_turn, (b, u))
                act.wait_ge(*full[2].at(("B", b, "o")))
                act.activation(ctxo, ps[:, 2, :], ACT.Identity, bias=Bb[:, 2:3]).then_inc(*b_ctx.mark(("B", b)))
                read(act, 2, b_ctx, ("B", b))

        def b_dve(dve):
            for b in range(B):
                norm_dve(dve, "B1", b, b, x[:, cols(b)])
            for b in range(B):
                for t in range(NT + 1):
                    if t < NT:
                        i, k = t % 2, 4 + t % 2
                        dve.wait_ge(*full[k].at(("B", b, t)))
                        if t >= 2:
                            dve.wait_ge(*full[6 + i].at(("B", b, t - 2)))
                        step(dve, dve_step, dve.tensor_copy(sc_[:, i, :], ps[:, k, 0:S]))
                        dve.sem_inc(free[k].mark()[0], 1)
                        for r in range(TOPK // 8):
                            src = sc_[:, i, :] if r == 0 else rem[:, i, :]
                            step(dve, dve_step, dve.max(m8[:, i, 8 * r:8 * r + 8], src))
                            step(dve, dve_step, dve.match_replace(rem[:, i, :], m8[:, i, 8 * r:8 * r + 8], src, -3e38))
                        dve.tensor_scalar(m8[:, i, 32:33], m8[:, i, 0:1], -C ** -0.5, None, ALU.mult).then_inc(*picked.mark((b, t)))
                    if t > 0:
                        u, i = t - 1, (t - 1) % 2
                        step(dve, dve_step, dve.tensor_tensor(msk, rem[:, i, :], sc_[:, i, :], ALU.not_equal))
                        dve.wait_ge(*b_exp.at((b, u)))
                        step(dve, dve_step, dve.tensor_tensor(pe_[:, i, :], pe_[:, i, :], msk, ALU.mult))
                        step(dve, dve_step, dve.tensor_reduce(m8[:, i, 33:34], pe_[:, i, :], AX, ALU.add))
                        step(dve, dve_step, dve.reciprocal(m8[:, i, 34:35], m8[:, i, 33:34]))
                        dve.tensor_scalar(pe_[:, i, :], pe_[:, i, :], m8[:, i, 34:35], None, ALU.mult).then_inc(*b_prob.mark((b, u)))
                out_dve(dve, "B", b, Bb[:, 3:4])

        def fp4(dve, key, src, nb, dst):
            n = nb * FB
            s3 = lambda v: v[:, 0:n].rearrange("p (a b) -> p a b", b=FB)
            wide = lambda v: v.unsqueeze(2).to_broadcast([128, nb, FB])
            big_, sca, inv = qb[:, 0, 0:nb], qb[:, 1, 0:nb], qb[:, 2, 0:nb]
            step(dve, dve_step, dve.tensor_reduce(big_, src, AX, ALU.max, apply_absolute_value=True))
            step(dve, dve_step, dve.tensor_scalar(sca, big_, 1 / 6, 1e-12, ALU.mult, ALU.max))
            step(dve, dve_step, dve.reciprocal(inv, sca))
            step(dve, dve_step, dve.tensor_tensor(s3(qa), src, wide(inv), ALU.mult))
            step(dve, dve_step, dve.scalar_tensor_tensor(qa[:, 0:n], qa[:, 0:n], -1.0, qa[:, 0:n], ALU.mult, ALU.max))
            a_, u_ = qa[:, 0:n], qu[:, 0:n]
            step(dve, dve_step, dve.tensor_scalar(u_, a_, 5.0, 2.0, ALU.is_gt, ALU.mult))
            for m in (3.5, 2.5):
                step(dve, dve_step, dve.scalar_tensor_tensor(u_, a_, m, u_, ALU.is_gt, ALU.add))
            step(dve, dve_step, dve.tensor_scalar(u_, u_, 2.0, None, ALU.mult))
            for m in (1.75, 1.25, 0.75, 0.25):
                step(dve, dve_step, dve.scalar_tensor_tensor(u_, a_, m, u_, ALU.is_gt, ALU.add))
            dve.wait_ge(*signed.at(key))
            step(dve, dve_step, dve.scalar_tensor_tensor(u_, u_, 0.5, qs[:, 0:n], ALU.mult, ALU.mult))
            dve.tensor_tensor(dst, s3(qu), wide(sca), ALU.mult).then_inc(*q4.mark(key))
            dve.wait_ge(*q4.at(key))

        def sign_act(act, key, src, n):
            act.activation(qs[:, 0:n], src, ACT.Sign).then_inc(*signed.mark(key))

        def c_pe(pe):
            pe.wait_ge(*q4.at("w"))
            for j, off in enumerate((0, 24, 48)):
                take(pe, j)
                for ch in range(3):
                    m = min(128, I0 - 128 * ch)
                    if j < 2:
                        last = pe.transpose(ps[:, j, 128 * ch:128 * ch + m],
                                            Cw[0:m, off + 8 * ch:off + 8 * ch + 8, :].rearrange("p a b -> p (a b)"), ident[0:m, 0:m])
                    else:
                        last = pe.transpose(ps[0:m, j, 128 * ch:128 * ch + 128],
                                            Cw[:, off + 8 * ch:off + 8 * ch + m // FB, :].rearrange("p a b -> p (a b)"), ident[:, :])
                last.then_inc(*full[j].mark(("C", "w", j)))
            for b in range(B):
                norm_pe(pe, "C1", b, 6 + b, x[:, cols(b)], wait=(x_new.at(("B", b)),))
            for b in range(B):
                pe.wait_ge(*normed.at(("C1", b)))
                take(pe, b)
                for t in range(NT):
                    last = pe.transpose(ps[:, b, 128 * t:128 * t + 128], xn[:, b, 128 * t:128 * t + 128], ident[:, :])
                last.then_inc(*full[b].mark(("C", b, "x")))
            for b in range(B):
                pe.wait_ge(*q4.at(("x", b)))
                take(pe, 2)
                for t in range(NT):
                    last = pe.transpose(ps[:, 2, 128 * t:128 * t + 128], xq[:, b, 128 * t:128 * t + 128], ident[:, :])
                last.then_inc(*full[2].mark(("C", b, "xt")))
                pe.wait_ge(*turned4.at(("x", b)))
                if b == 0:
                    pe.wait_ge(*turned4.at(("w", 2)))
                for t in range(NT):
                    for j, w in enumerate((gT, uT)):
                        k = 4 + 2 * (t % 2) + j
                        take(pe, k)
                        pe.matmul(ps[:, k, 0:I0], xqT[:, b, 128 * t:128 * t + 128], w, start=True, stop=True)\
                            .then_inc(*full[k].mark(("C", b, t, j)))
            for b in range(B):
                pe.wait_ge(*q4.at(("h", b)))
                for t in range(NT):
                    k = t % 2
                    take(pe, k)
                    for ch in range(3):
                        m = min(128, I0 - 128 * ch)
                        last = pe.transpose(ps[0:m, k, 128 * ch:128 * ch + 128], hq[:, b, I0 * t + 128 * ch:I0 * t + 128 * ch + m], ident[:, :])
                    last.then_inc(*full[k].mark(("C", b, "h", t)))
                pe.wait_ge(*turned4.at(("h", b, NT - 1)))
                take(pe, 3)
                for ch in range(3):
                    m = min(128, I0 - 128 * ch)
                    last = pe.matmul(ps[:, 3, :], dT[0:m, ch, :], hT[0:m, ch, :], start=ch == 0, stop=ch == 2)
                last.then_inc(*full[3].mark(("C", b, "y")))

        def c_act(act):
            sign_act(act, "w", Cw.rearrange("p a b -> p (a b)"), 1120)
            for j, dst in enumerate((gT, uT)):
                act.wait_ge(*full[j].at(("C", "w", j)))
                act.activation(dst, ps[:, j, 0:I0], ACT.Copy).then_inc(*turned4.mark(("w", j)))
                read(act, j, turned4, ("w", j))
            act.wait_ge(*full[2].at(("C", "w", 2)))
            step(act, act_step, act.activation(dT[:, 0:2, :], ps[:, 2, 0:256].rearrange("p (a b) -> p a b", a=2), ACT.Copy))
            act.activation(dT[0:96, 2, :], ps[0:96, 2, 256:384], ACT.Copy).then_inc(*turned4.mark(("w", 2)))
            read(act, 2, turned4, ("w", 2))
            for b in range(B):
                norm_act(act, "C1", b, 6 + b, None, 0)
            for b in range(B):
                act.wait_ge(*q4.at("w" if b == 0 else ("x", b - 1)))
                act.wait_ge(*centred.at(("xc", b)))
                sign_act(act, ("x", b), xq[:, b, :], T)
                act.wait_ge(*full[2].at(("C", b, "xt")))
                act.activation(xqT[:, b, :], ps[:, 2, :], ACT.Copy).then_inc(*turned4.mark(("x", b)))
                read(act, 2, turned4, ("x", b))
                for t in range(NT):
                    k = 4 + 2 * (t % 2)
                    act.wait_ge(*full[k].at(("C", b, t, 0)))
                    if t >= 2:
                        act.wait_ge(*hgate.at((b, t - 2)))
                    act.activation(eg[:, t % 2, :], ps[:, k, 0:I0], ACT.Exp, scale=-1.0).then_inc(*expg.mark((b, t)))
            for b in range(B):
                act.wait_ge(*hgate.at((b, NT - 1)))
                act.wait_ge(*q4.at(("x", 1) if b == 0 else ("h", b - 1)))
                sign_act(act, ("h", b), hq[:, b, :], NT * I0)
                for t in range(NT):
                    k = t % 2
                    act.wait_ge(*full[k].at(("C", b, "h", t)))
                    step(act, act_step, act.activation(hT[:, 0:2, 128 * t:128 * t + 128],
                                                       ps[:, k, 0:256].rearrange("p (a b) -> p a b", a=2), ACT.Copy))
                    act.activation(hT[0:96, 2, 128 * t:128 * t + 128], ps[0:96, k, 256:384], ACT.Copy).then_inc(*turned4.mark(("h", b, t)))
                    read(act, k, turned4, ("h", b, t))

        def c_dve(dve):
            fp4(dve, "w", Cw, 70, Cw)
            for b in range(B):
                norm_dve(dve, "C1", b, 6 + b, x[:, cols(b)])
            b3 = lambda v: v.rearrange("p (a b) -> p a b", b=FB)
            for b in range(B):
                dve.wait_ge(*full[b].at(("C", b, "x")))
                dve.tensor_copy(xq[:, b, :], ps[:, b, :]).then_inc(*centred.mark(("xc", b)))
                read(dve, b, centred, ("xc", b))
            for b in range(B):
                fp4(dve, ("x", b), b3(xq[:, b, :]), 32, b3(xq[:, b, :]))
                for t in range(NT):
                    k, i = 4 + 2 * (t % 2), t % 2
                    h_ = hq[:, b, I0 * t:I0 * t + I0]
                    dve.wait_ge(*expg.at((b, t)))
                    step(dve, dve_step, dve.tensor_scalar(eg[:, i, :], eg[:, i, :], 1.0, None, ALU.add))
                    step(dve, dve_step, dve.reciprocal(eg[:, i, :], eg[:, i, :]))
                    step(dve, dve_step, dve.tensor_tensor(h_, eg[:, i, :], ps[:, k, 0:I0], ALU.mult))
                    dve.sem_inc(free[k].mark()[0], 1)
                    dve.wait_ge(*full[k + 1].at(("C", b, t, 1)))
                    dve.tensor_tensor(h_, h_, ps[:, k + 1, 0:I0], ALU.mult).then_inc(*hgate.mark((b, t)))
                    read(dve, k + 1, hgate, (b, t))
            for b in range(B):
                fp4(dve, ("h", b), b3(hq[:, b, :]), NT * I0 // FB, b3(hq[:, b, :]))
                dve.wait_ge(*full[3].at(("C", b, "y")))
                dve.tensor_tensor(x[:, cols(b)], x[:, cols(b)], ps[:, 3, :], ALU.add).then_inc(*x_new.mark(("C", b)))
                read(dve, 3, x_new, ("C", b))

        def e_pe(pe, before):
            for b in range(B):
                norm_pe(pe, "E1", b, b, x[:, cols(b)], wait=(x_new.at((before, b)),))
            for b in range(B):
                qkv_pe(pe, "E", b, Ew)
                pe.wait_ge(*q_ready.at(("E", b)))
                pe.wait_ge(*kb_ready.at(b))
                pe.wait_ge(*vv_ready.at(("E", b)))
                for t in range(NT):
                    for g in range(6):
                        n = min(3, HS - 3 * g)
                        k = (6 * t + g) % 5
                        take(pe, k)
                        pe.matmul(ps[:, k, 0:n * S], qt[:, 128 * t:128 * t + 128],
                                  KB[:, 3 * g:3 * g + n, :].rearrange("p a b -> p (a b)"), start=True, stop=True)\
                            .then_inc(*full[k].mark(("E", b, t, g)))
                    pe.wait_ge(*e_exp.at((b, t)))
                    take(pe, 5)
                    for m in range(9):
                        if m < 8:
                            k = 6 + m % 2
                            take(pe, k)
                            for q_ in range(4):
                                last = pe.transpose(ps[0:SH, k, 128 * q_:128 * q_ + 128],
                                                    PE_[:, 2 * m + q_ // 2, SH * (q_ % 2):SH * (q_ % 2) + SH], ident[:, :])
                            last.then_inc(*full[k].mark(("E", b, t, m)))
                        if m > 0:
                            w = m - 1
                            pe.wait_ge(*(e_turn_a if w % 2 == 0 else e_turn_d).at((b, t, w)))
                            for q_ in range(4):
                                h = 2 * w + q_ // 2
                                last = pe.matmul(ps[:, 5, 9 * h:9 * h + 9], pt2[0:SH, w % 2, 128 * q_:128 * q_ + 128],
                                                 vt1[0:SH, q_ % 2, 9 * h:9 * h + 9], start=q_ % 2 == 0, stop=q_ % 2 == 1)
                    last.then_inc(*full[5].mark(("E", b, t, "o")))
                    pe.wait_ge(*e_norm.at((b, t)))
                    take(pe, 5)
                    pe.transpose(ps[:, 5, 0:128], atok, ident[:, :]).then_inc(*full[5].mark(("E", b, t, "a")))
                out_pe(pe, "E", b, Ew[:, 3, :], aT, b_ctx.at(("E", b, NT - 1)))

        def e_act(act):
            for b in range(B):
                norm_act(act, "E1", b, b, None, 0)
            for b in range(B):
                qkv_act(act, "E", b, Eb)
                for t in range(NT):
                    for h in range(HS):
                        g, j = h // 3, h % 3
                        k = (6 * t + g) % 5
                        if j == 0:
                            act.wait_ge(*e_max.at((b, t, g)))
                        ins = act.activation(PE_[:, h, :], ps[:, k, S * j:S * j + S], ACT.Exp, bias=mx[:, 1, h:h + 1], scale=DS ** -0.5)
                        if j == 2:
                            ins.then_inc(*free[k].mark())
                        elif h == HS - 1:
                            ins.then_inc(*e_exp.mark((b, t)))
                            read(act, k, e_exp, (b, t))
                    for m in range(0, 8, 2):
                        act.wait_ge(*full[6].at(("E", b, t, m)))
                        act.activation(pt2[0:SH, 0, :], ps[0:SH, 6, :], ACT.Copy).then_inc(*e_turn_a.mark((b, t, m)))
                        read(act, 6, e_turn_a, (b, t, m))
                    act.wait_ge(*full[5].at(("E", b, t, "a")))
                    act.activation(aT[:, 128 * t:128 * t + 128], ps[:, 5, 0:128], ACT.Identity, bias=Eb[:, 2:3])\
                        .then_inc(*b_ctx.mark(("E", b, t)))
                    read(act, 5, b_ctx, ("E", b, t))

        def e_dve(dve):
            dve.wait_ge(*x_new.at(("D", 1)))
            dve.memset(vt1, 1.0).then_inc(*vv_one.mark("ones"))
            for b in range(B):
                norm_dve(dve, "E1", b, b, x[:, cols(b)])
            for b in range(B):
                dve.wait_ge(*k_ready.at(("E", b)))
                dve.tensor_tensor(KB, kt.unsqueeze(1).to_broadcast([128, HS, S]), hmask.unsqueeze(2).to_broadcast([128, HS, S]), ALU.mult)\
                    .then_inc(*kb_ready.mark(b))
                for t in range(NT):
                    if (b, t) != (0, 0):
                        dve.wait_ge(*e_exp.at((b, t - 1) if t else (b - 1, NT - 1)))
                    for g in range(6):
                        n = min(3, HS - 3 * g)
                        k = (6 * t + g) % 5
                        dve.wait_ge(*full[k].at(("E", b, t, g)))
                        hs = slice(3 * g, 3 * g + n)
                        step(dve, dve_step, dve.tensor_reduce(mx[:, 0, hs], ps[:, k, 0:n * S].rearrange("p (a b) -> p a b", a=n), AX, ALU.max))
                        dve.tensor_scalar(mx[:, 1, hs], mx[:, 0, hs], -DS ** -0.5, None, ALU.mult).then_inc(*e_max.mark((b, t, g)))
                    for m in range(1, 8, 2):
                        dve.wait_ge(*full[7].at(("E", b, t, m)))
                        dve.tensor_copy(pt2[0:SH, 1, :], ps[0:SH, 7, :]).then_inc(*e_turn_d.mark((b, t, m)))
                        read(dve, 7, e_turn_d, (b, t, m))
                    dve.wait_ge(*full[5].at(("E", b, t, "o")))
                    o = ps[:, 5, 0:144].rearrange("p (h d) -> p h d", d=9)
                    step(dve, dve_step, dve.reciprocal(rd, o[:, :, 8]))
                    dve.tensor_tensor(atok.rearrange("p (h d) -> p h d", d=DS), o[:, :, 0:DS], rd.unsqueeze(2).to_broadcast([128, HS, DS]),
                                      ALU.mult).then_inc(*e_norm.mark((b, t)))
                    read(dve, 5, e_norm, (b, t))
                out_dve(dve, "E", b, Eb[:, 3:4])
        vv_one = sg("vv_one")

        a4 = Area()
        o = a4(N)
        Dw = a4(4, C)
        Dqk = a4(4)
        bv = a4(C)
        omr = a4(DS)
        Db = a4(10)
        OmS = a4(HS * FS)
        Bn = a4(HS * FS)
        Om = a4(HS * FS)
        own = a4(2, C)
        DW1 = a4(DFF)
        DW2 = a4(4, C)
        dq = a4(B, 2, T)
        dsq = a4(B, 2, T)
        Qf = a4(B, 2, T)
        Kz = a4(B, 4, T)
        Kt = a4(B * 3, HS * FS)
        VP = HS * (C + DS)
        Vz = a4(B * NT, VP)
        st = a4(B * 3, 2 * C)
        sT = a4(2, 4, 512)
        recd, num_a = rs, xn
        h0 = dq[:, :, 0, :]
        h1 = dq[:, :, 1, :]
        rel = Kz
        om_ready, d_q, d_k, d_v, d_sq = sg("om_ready"), sg("d_q"), sg("d_k"), sg("d_v"), sg("d_sq")
        phi, ktok, state, masked, d_norm = sg("phi"), sg("ktok"), sg("state"), sg("masked"), sg("d_norm")
        summed, den_copied = sg("summed"), sg("den_copied")
        res1, affine, relued, res2 = sg("res1"), sg("affine"), sg("relued"), sg("res2")
        qkv_used, ff_used = sg("qkv_used"), sg("ff_used")
        o_ready = raw("o_ready")
        d_const, qkv_in, ff_in = raw("d_const"), raw("qkv_in"), raw("ff_in")
        QKV_DMA, FF_DMA = 4 * 16, 3 * 16
        phi_bank = ((6, 7, 0, 1), (4, 5, 6, 7))
        kt_bank = ((2, 3), (0, 1))
        st_bank = ((2, 3), (4, 5))

        def chunk(ch):
            return slice(128 * ch, 128 * ch + 128)

        def d_state_pe(pe, b):
            for ch in range(3):
                k = st_bank[b][ch // 2]
                if ch != 1:
                    pe.wait_ge(*ktok.at((b, ch // 2)))
                    take(pe, k)
                vch = Vz[:, NT * b + ch, :].rearrange("p (h w) -> p h w", h=HS)[:, :, 0:DS]
                for g in range(2):
                    n = 256 * (ch % 2) + 128 * g
                    last = pe.matmul(ps[:, k, n:n + 128], Kt[:, 3 * b + ch, 128 * g:128 * g + 128], vch, start=True, stop=True)
                if ch > 0:
                    last.then_inc(*full[k].mark(("D", b, "st", ch)))

        def d_den_pe(pe, b):
            pe.wait_ge(*summed.at(b))
            take(pe, 6 + b)
            for g in range(2):
                last = pe.matmul(ps[:, 6 + b, :], own[:, g, :], dsq[:, b, g, :], start=g == 0, stop=g == 1)
            last.then_inc(*full[6 + b].mark(("D", b, "den")))

        def d_attn_pe(pe, b, between):
            def scores(ch, r):
                take(pe, r)
                sl = chunk(ch)
                rows = slice(32 * r, 32 * r + 32)
                for gp in range(4):
                    last = pe.matmul(ps[:, r, 128 * gp:128 * gp + 128], Kz[rows, b, gp, sl], Qf[rows, b, gp // 2, sl],
                                     start=True, stop=True, tile_position=(32 * r, 0))
                last.then_inc(*full[r].mark(("D", b, ch, r)))
            pe.wait_ge(*phi.at((b, 1, 1)))
            for r in range(4):
                scores(0, r)
            k = 6 + b
            for ch in range(NT):
                out_ = ps[:, k, chunk(ch)]
                for r in range(4):
                    if ch + 1 < NT:
                        scores(ch + 1, r)
                    if r == 0 and ch == 0:
                        take(pe, k)
                    if r == 0 and ch > 0:
                        pe.wait_ge(*state.at((b, ch - 1)))
                        for g in range(2):
                            pe.matmul(out_, st[:, 3 * b + ch - 1, 128 * g:128 * g + 128], Qf[:, b, g, chunk(ch)], start=g == 0, stop=False)
                    pe.wait_ge(*masked.at((b, ch, r)))
                    for gp in range(4):
                        h = 8 * (gp // 2) + 2 * r + gp % 2
                        last = pe.matmul(out_, Vz[:, NT * b + ch, C * h:C * h + C], sT[:, ch % 2, r, 128 * gp:128 * gp + 128],
                                         start=ch == 0 and (r, gp) == (0, 0), stop=(r, gp) == (3, 3))
                last.then_inc(*full[k].mark(("D", b, "num", ch)))
                if ch in between:
                    between[ch]()

        def d_mean_pe(pe, key, b, bank, wait):
            pe.wait_ge(*wait)
            take(pe, bank)
            pe.matmul(ps[:, bank, :], mean_m[:, :], h0[:, b, :], start=True, stop=True).then_inc(*full[bank].mark((key, b, "mean")))

        def d_var_pe(pe, key, b, bank):
            pe.wait_ge(*squared.at((key, b)))
            take(pe, bank)
            pe.matmul(ps[:, bank, :], mean_m[:, :], sq[:, b, :], start=True, stop=True).then_inc(*full[bank].mark((key, b, "var")))

        def d_out_pe(pe, b):
            pe.wait_ge(*d_norm.at(b))
            take(pe, 4)
            pe.matmul(ps[:, 4, :], Dw[:, 3, :], num_a[:, b, :], start=True, stop=True).then_inc(*full[4].mark(("D", b, "wo")))

        def d_up_pe(pe, b):
            pe.wait_ge(*affine.at(b))
            for f_ in range(4):
                take(pe, f_)
                pe.matmul(ps[:, f_, :], DW1[:, 128 * f_:128 * f_ + 128], h1[:, b, :], start=True, stop=True).then_inc(*full[f_].mark(("D", b, "f", f_)))

        def d_down_pe(pe, b):
            take(pe, 6 + b)
            for f_ in range(4):
                pe.wait_ge(*relued.at((b, f_)))
                last = pe.matmul(ps[:, 6 + b, :], DW2[:, f_, :], rel[:, b, f_, :], start=f_ == 0, stop=f_ == 3)
            last.then_inc(*full[6 + b].mark(("D", b, "f2")))

        def d_pe_layer(pe, L):
            pe.wait_ge(qkv_in, L * QKV_DMA + QKV_DMA)
            for b in range(B):
                pe.wait_ge(o_ready, L * 2 + (b + 1))
                for j in range(2):
                    k = 3 * b + j
                    take(pe, k)
                    pe.matmul(ps[:, k, :], Dw[:, j, :], o[:, cols(b)], start=True, stop=True).then_inc(*full[k].mark(("D", b, j)))
                k = 3 * b + 2
                take(pe, k)
                for t in range(NT):
                    last = pe.matmul(ps[:, k, chunk(t)], o[:, T * b + 128 * t:T * b + 128 * t + 128], Dw[:, 2, :], start=True, stop=True)
                last.then_inc(*full[k].mark(("D", b, 2)))
            pe.wait_ge(*om_ready.at("om"))
            for b in range(B):
                for j, done in enumerate((d_q, d_k)):
                    pe.wait_ge(*done.at(b))
                    pe.wait_ge(*d_sq.at((b, j)))
                    for g in range(2):
                        k = phi_bank[b][2 * j + g]
                        take(pe, k)
                        pe.matmul(ps[:, k, :], Om[:, 128 * g:128 * g + 128], dq[:, b, j, :], start=True, stop=False)
                        pe.matmul(ps[:, k, :], Bn[:, 128 * g:128 * g + 128], dsq[:, b, j, :], start=False, stop=True)\
                            .then_inc(*full[k].mark(("D", b, "phi", j, g)))
                for ch in range(3):
                    k = kt_bank[b][ch // 2]
                    if ch != 1:
                        take(pe, k)
                    n = 256 * (ch % 2)
                    pe.matmul(ps[:, k, n:n + 256], dq[:, b, 1, chunk(ch)], Om, start=True, stop=False)
                    last = pe.matmul(ps[:, k, n:n + 256], dsq[:, b, 1, chunk(ch)], Bn, start=False, stop=True)
                    if ch > 0:
                        last.then_inc(*full[k].mark(("D", b, "kt", ch // 2)))
            pe.wait_ge(*d_v.at(1))
            d_state_pe(pe, 0)
            d_den_pe(pe, 0)
            d_attn_pe(pe, 0, {0: lambda: d_state_pe(pe, 1), 1: lambda: d_den_pe(pe, 1)})
            d_attn_pe(pe, 1, {0: lambda: d_out_pe(pe, 0), 1: lambda: d_mean_pe(pe, "D1", 0, 5, res1.at(0)), 2: lambda: d_var_pe(pe, "D1", 0, 5)})
            pe.wait_ge(ff_in, L * FF_DMA + FF_DMA)
            d_up_pe(pe, 0)
            d_out_pe(pe, 1)
            d_mean_pe(pe, "D1", 1, 5, res1.at(1))
            d_down_pe(pe, 0)
            d_var_pe(pe, "D1", 1, 5)
            d_mean_pe(pe, "D2", 0, 4, res2.at(0))
            d_var_pe(pe, "D2", 0, 4)
            d_up_pe(pe, 1)
            d_down_pe(pe, 1)
            d_mean_pe(pe, "D2", 1, 5, res2.at(1))
            d_var_pe(pe, "D2", 1, 5)

        def d_pe(pe):
            for b in range(B):
                norm_pe(pe, "D0", b, b, x[:, cols(b)], wait=(x_new.at(("C", b)),))
            pe.wait_ge(d_const, 48)
            with layers(pe, "D") as L:
                d_pe_layer(pe, L)

        def d_square_act(act, key, b, bank):
            act.wait_ge(*centred.at((key, b)))
            act.sem_inc(free[bank].mark()[0], 1)
            act.activation(sq[:, b, :], xc[:, b, :], ACT.Square).then_inc(*squared.mark((key, b)))

        def d_root_act(act, key, b, bank):
            act.wait_ge(*full[bank].at((key, b, "var")))
            step(act, act_step, act.activation(rs[:, b, :], ps[:, bank, :], ACT.Ln, bias=eps5[:, 0:1]))
            act.sem_inc(free[bank].mark()[0], 1)
            act.activation(rs[:, b, :], rs[:, b, :], ACT.Exp, scale=-0.5).then_inc(*rooted.mark((key, b)))

        def d_h1_act(act, b):
            act.wait_ge(*normed.at(("D1", b)))
            act.activation(h1[:, b, :], xn[:, b, :], ACT.Identity, bias=Db[:, 2:3], scale=Db[:, 1:2]).then_inc(*affine.mark(b))

        def d_o_act(act, b):
            act.wait_ge(*normed.at(("D2", b)))
            act.activation(o[:, cols(b)], xn[:, b, :], ACT.Identity, bias=Db[:, 4:5], scale=Db[:, 3:4]).then_inc(o_ready, 1)

        def d_relu_act(act, b):
            for f_ in range(4):
                act.wait_ge(*full[f_].at(("D", b, "f", f_)))
                act.activation(rel[:, b, f_, :], ps[:, f_, :], ACT.Relu, bias=Db[:, 6 + f_:7 + f_]).then_inc(*relued.mark((b, f_)))
                read(act, f_, relued, (b, f_))

        def d_act_layer(act, L):
            act.wait_ge(*om_ready.at("om"))
            for b in range(B):
                for j, done in enumerate((d_q, d_k)):
                    k = 3 * b + j
                    act.wait_ge(*full[k].at(("D", b, j)))
                    act.activation(dq[:, b, j, :], ps[:, k, :], ACT.Identity, bias=Dqk[:, 2 + j:3 + j], scale=DS ** -0.25).then_inc(*done.mark(b))
                    read(act, k, done, b)
                    act.activation(dsq[:, b, j, :], dq[:, b, j, :], ACT.Square).then_inc(*d_sq.mark((b, j)))
            for b in range(B):
                for g in range(2):
                    k = phi_bank[b][g]
                    act.wait_ge(*full[k].at(("D", b, "phi", 0, g)))
                    act.activation(Qf[:, b, g, :], ps[:, k, :], ACT.Exp, bias=eps5[:, 2:3]).then_inc(*phi.mark((b, 0, g)))
                    read(act, k, phi, (b, 0, g))
                for g in range(2):
                    k = phi_bank[b][2 + g]
                    act.wait_ge(*full[k].at(("D", b, "phi", 1, g)))
                    act.activation(Kz[:, b, 2 * g, :], ps[:, k, :], ACT.Exp, bias=eps5[:, 4:5])
                    act.activation(Kz[:, b, 2 * g + 1, :], ps[:, k, :], ACT.Exp, bias=eps5[:, 5:6]).then_inc(*phi.mark((b, 1, g)))
                    read(act, k, phi, (b, 1, g))
                for i, (c0, n) in enumerate(((0, 2), (2, 1))):
                    k = kt_bank[b][i]
                    act.wait_ge(*full[k].at(("D", b, "kt", i)))
                    act.activation(Kt[:, 3 * b + c0:3 * b + c0 + n, :], ps[:, k, 0:256 * n].rearrange("p (a c) -> p a c", a=n), ACT.Exp,
                                   bias=eps5[:, 2:3]).then_inc(*ktok.mark((b, i)))
                    read(act, k, ktok, (b, i))
            act.wait_ge(ff_in, L * FF_DMA + FF_DMA)
            d_square_act(act, "D1", 0, 5)
            d_root_act(act, "D1", 0, 5)
            d_h1_act(act, 0)
            d_relu_act(act, 0)
            d_square_act(act, "D1", 1, 5)
            d_root_act(act, "D1", 1, 5)
            d_square_act(act, "D2", 0, 4)
            d_h1_act(act, 1)
            d_root_act(act, "D2", 0, 4)
            d_o_act(act, 0)
            d_relu_act(act, 1)
            d_square_act(act, "D2", 1, 5)
            d_root_act(act, "D2", 1, 5)
            d_o_act(act, 1)
            act.wait_ge(o_ready, L * 2 + 4)
            act.sem_inc(ff_used.mark("layer")[0], 1)

        def d_act(act):
            for b in range(B):
                norm_act(act, "D0", b, b, None, 0)
            with layers(act, "D") as L:
                d_act_layer(act, L)

        def d_v_dve(dve, b):
            k = 3 * b + 2
            dve.wait_ge(*full[k].at(("D", b, 2)))
            dve.tensor_tensor(Vz[:, NT * b:NT * b + NT, :].rearrange("p t (h w) -> p t h w", h=HS)[:, :, :, 0:DS],
                              ps[:, k, :].rearrange("p (t h d) -> p t h d", t=NT, d=DS),
                              bv.rearrange("p (h d) -> p h d", d=DS).unsqueeze(1).to_broadcast([128, NT, HS, DS]),
                              ALU.add).then_inc(*d_v.mark(b))
            read(dve, k, d_v, b)

        def d_sum_dve(dve, b):
            dve.wait_ge(*full[kt_bank[b][1]].at(("D", b, "kt", 1)))
            for g in range(2):
                dve.wait_ge(*phi.at((b, 1, g)))
                step(dve, dve_step, dve.tensor_tensor_scan(dsq[:, b, g, :], Kz[:, b, 2 * g, :], Kz[:, b, 2 * g + 1, :], 0.0, ALU.add, ALU.add))
                last = dve.tensor_tensor(dsq[:, b, g, :], dsq[:, b, g, :], Qf[:, b, g, :], ALU.mult)
            last.then_inc(*summed.mark(b))

        def d_den_dve(dve, b):
            dve.wait_ge(*full[6 + b].at(("D", b, "den")))
            dve.tensor_scalar(recd[:, b, :], ps[:, 6 + b, :], 1e-6, None, ALU.add).then_inc(*den_copied.mark(b))
            read(dve, 6 + b, den_copied, b)

        def d_state_dve(dve, b):
            for ch in range(3):
                k = st_bank[b][ch // 2]
                dve.wait_ge(*full[k].at(("D", b, "st", max(ch, 1))))
                n = 256 * (ch % 2)
                ins = dve.tensor_tensor(st[:, 3 * b + ch, :], ps[:, k, n:n + 256], own.rearrange("p a b -> p (a b)"), ALU.mult)
                if ch > 0:
                    step(dve, dve_step, ins)
                    ins = dve.tensor_tensor(st[:, 3 * b + ch, :], st[:, 3 * b + ch - 1, :], st[:, 3 * b + ch, :], ALU.add)
                ins.then_inc(*state.mark((b, ch)))
                if ch > 0:
                    read(dve, k, state, (b, ch))
                else:
                    dve.wait_ge(*state.at((b, ch)))

        def d_mask_dve(dve, b, ch):
            if ch > 1:
                dve.wait_ge(*full[6 + b].at(("D", b, "num", ch - 2)))
            elif b == 1:
                dve.wait_ge(*full[6].at(("D", 0, "num", ch + 2)))
            for r in range(4):
                dve.wait_ge(*full[r].at(("D", b, ch, r)))
                dve.tensor_tensor(sT[:, ch % 2, r, :].rearrange("p (g i) -> p g i", g=4), ps[:, r, :].rearrange("p (g i) -> p g i", g=4),
                                  tri.unsqueeze(1).to_broadcast([128, 4, 128]), ALU.mult).then_inc(*masked.mark((b, ch, r)))
                read(dve, r, masked, (b, ch, r))

        def d_a_dve(dve, b):
            dve.wait_ge(*full[6 + b].at(("D", b, "num", NT - 1)))
            dve.tensor_tensor(num_a[:, b, :], ps[:, 6 + b, :], recd[:, b, :], ALU.mult).then_inc(*d_norm.mark(b))
            read(dve, 6 + b, d_norm, b)

        def d_res1_dve(dve, b):
            dve.wait_ge(*full[4].at(("D", b, "wo")))
            dve.scalar_tensor_tensor(h0[:, b, :], ps[:, 4, :], Db[:, 0:1], o[:, cols(b)], ALU.add, ALU.add).then_inc(*res1.mark(b))
            read(dve, 4, res1, b)

        def d_res2_dve(dve, b):
            dve.wait_ge(*full[6 + b].at(("D", b, "f2")))
            dve.scalar_tensor_tensor(h0[:, b, :], ps[:, 6 + b, :], Db[:, 5:6], h1[:, b, :], ALU.add, ALU.add).then_inc(*res2.mark(b))
            read(dve, 6 + b, res2, b)

        def d_centre_dve(dve, key, b, bank):
            dve.wait_ge(*full[bank].at((key, b, "mean")))
            dve.tensor_tensor(xc[:, b, :], h0[:, b, :], ps[:, bank, :], ALU.subtract).then_inc(*centred.mark((key, b)))

        def d_scale_dve(dve, key, b):
            dve.wait_ge(*rooted.at((key, b)))
            dve.tensor_tensor(xn[:, b, :], xc[:, b, :], rs[:, b, :], ALU.mult).then_inc(*normed.mark((key, b)))

        def d_recip_dve(dve, b):
            step(dve, dve_step, dve.reciprocal(recd[:, b, :], recd[:, b, :]))

        def d_dve_layer(dve, L):
            dve.wait_ge(qkv_in, L * QKV_DMA + QKV_DMA)
            step(dve, dve_step, dve.tensor_scalar(Dqk[:, 2:4], Dqk[:, 0:2], DS ** -0.25, None, ALU.mult))
            dve.tensor_tensor(Om.rearrange("p (a d) -> p a d", d=DS), OmS.rearrange("p (a d) -> p a d", d=DS),
                              omr.unsqueeze(1).to_broadcast([128, 2 * HS, DS]), ALU.mult).then_inc(*om_ready.mark("om"))
            for b in range(B):
                d_v_dve(dve, b)
            d_sum_dve(dve, 0)
            d_state_dve(dve, 0)
            d_den_dve(dve, 0)
            d_mask_dve(dve, 0, 0)
            d_sum_dve(dve, 1)
            d_mask_dve(dve, 0, 1)
            d_state_dve(dve, 1)
            d_mask_dve(dve, 0, 2)
            d_den_dve(dve, 1)
            d_mask_dve(dve, 0, 3)
            d_recip_dve(dve, 0)
            d_mask_dve(dve, 1, 0)
            d_a_dve(dve, 0)
            d_mask_dve(dve, 1, 1)
            dve.wait_ge(ff_in, L * FF_DMA + FF_DMA)
            d_res1_dve(dve, 0)
            d_mask_dve(dve, 1, 2)
            d_centre_dve(dve, "D1", 0, 5)
            d_mask_dve(dve, 1, 3)
            d_scale_dve(dve, "D1", 0)
            d_recip_dve(dve, 1)
            d_a_dve(dve, 1)
            d_res1_dve(dve, 1)
            dve.sem_inc(qkv_used.mark("layer")[0], 1)
            d_centre_dve(dve, "D1", 1, 5)
            d_res2_dve(dve, 0)
            d_centre_dve(dve, "D2", 0, 4)
            d_scale_dve(dve, "D1", 1)
            d_scale_dve(dve, "D2", 0)
            d_res2_dve(dve, 1)
            d_centre_dve(dve, "D2", 1, 5)
            d_scale_dve(dve, "D2", 1)

        def d_dve(dve):
            step(dve, dve_step, dve.memset(Vz, 0.0))
            for b in range(B):
                norm_dve(dve, "D0", b, b, x[:, cols(b)], out_=o[:, cols(b)])
                dve.wait_ge(*normed.at(("D0", b)))
                dve.sem_inc(o_ready, 1)
            dve.wait_ge(d_const, 48)
            with layers(dve, "D") as L:
                d_dve_layer(dve, L)
            for b in range(B):
                dve.wait_ge(o_ready, 2 * LAYERS + 1 + b)
                dve.tensor_tensor(x[:, cols(b)], x[:, cols(b)], o[:, cols(b)], ALU.add).then_inc(*x_new.mark(("D", b)))

        def qkv_weights(sp, l):
            for dst, name in ((Dw.rearrange("p a b -> p (a b)"), "D_w"), (Dqk[:, 0:2], "D_qk"), (omr, "D_om"), (bv, "D_bv")):
                sp.dma_start(dst, A[name][bass.ds(l * 128, 128), :]).then_inc(qkv_in, 16)

        def ff_weights_d(sp, l):
            for dst, name in ((Db, "D_b"), (DW1, "D_w1"), (DW2.rearrange("p a b -> p (a b)"), "D_w2")):
                sp.dma_start(dst, A[name][bass.ds(l * 128, 128), :]).then_inc(ff_in, 16)

        def d_sp(sp):
            sp.wait_ge(*x_new.at(("C", 1)))
            sp.dma_start(OmS, A["OmS"]).then_inc(d_const, 16)
            sp.dma_start(Bn, A["Bn"]).then_inc(d_const, 16)
            sp.dma_start(own.rearrange("p a b -> p (a b)"), A["own"]).then_inc(d_const, 16)
            qkv_weights(sp, 0)
            ff_weights_d(sp, 0)
            with layers(sp, "D", LAYERS - 1) as L:
                sp.wait_ge(*qkv_used.at("layer"))
                qkv_weights(sp, L + 1)
                sp.wait_ge(*ff_used.at("layer"))
                ff_weights_d(sp, L + 1)

        f_used, gg, f_mul = sg("f_used"), sg("gg"), sg("f_mul")
        f_const, fa_loaded, ff_loaded = raw("f_const"), raw("fa_loaded"), raw("ff_loaded")

        up_bank = (0, 1, 2, 4, 5, 3)

        def f_mean_pe(pe, b, bank):
            pe.wait_ge(*shifted.at(("F2", b)))
            take(pe, bank)
            pe.matmul(ps[:, bank, :], mean_m[:, :], xsh[:, b, :], start=True, stop=True).then_inc(*full[bank].mark(("F1", b, "mean")))

        def f_up_pe(pe, b, i):
            c0, m = DIC[i]
            pe.wait_ge(*affine.at(("F", b)))
            for j in range(2):
                k = up_bank[2 * i + j]
                take(pe, k)
                pe.matmul(ps[0:m, k, :], W1[:, DI * j + c0:DI * j + c0 + m], xn[:, b, :], start=True, stop=True)\
                    .then_inc(*full[k].mark(("F", b, "f", k)))

        def f_down_pe(pe, b):
            take(pe, 6)
            for i, (c0, m) in enumerate(DIC):
                pe.wait_ge(*f_mul.at((b, i)))
                last = pe.matmul(ps[:, 6, :], W2[0:m, i, :], fh[0:m, i, :], start=i == 0, stop=i == 2)
            last.then_inc(*full[6].mark(("F", b, "f2")))

        def f_pe_layer(pe, L):
            pe.wait_ge(fa_loaded, L * 48 + 48)
            attn_pe(pe, "F", lambda b: xsh[:, b, :], True, {4: lambda: f_mean_pe(pe, 0, 3), 7: lambda: d_var_pe(pe, "F1", 0, 3)})
            pe.wait_ge(ff_loaded, L * 80 + 80)
            f_up_pe(pe, 0, 0)
            f_mean_pe(pe, 1, 7)
            f_up_pe(pe, 0, 1)
            f_up_pe(pe, 0, 2)
            d_var_pe(pe, "F1", 1, 7)
            f_down_pe(pe, 0)
            for i in range(3):
                f_up_pe(pe, 1, i)
            f_down_pe(pe, 1)

        def f_pe(pe):
            for b in range(B):
                norm_pe(pe, "F0", b, b, x[:, cols(b)], wait=(x_new.at(("E", b)),))
            pe.wait_ge(f_const, 48)
            with layers(pe, "F") as L:
                f_pe_layer(pe, L)

        def f_xn_act(act, b):
            act.wait_ge(*normed.at(("F1", b)))
            act.activation(xn[:, b, :], xn[:, b, :], ACT.Identity, bias=lng[:, 1:2], scale=lng[:, 0:1]).then_inc(*affine.mark(("F", b)))

        def f_gelu_act(act, b, i):
            m, k = DIC[i][1], up_bank[2 * i + 1]
            act.wait_ge(*full[k].at(("F", b, "f", k)))
            if b == 1:
                act.wait_ge(*f_mul.at((0, i)))
            act.activation(fg[0:m, i, :], ps[0:m, k, :], ACT.Gelu, bias=b1[0:m, 3 + i:4 + i]).then_inc(*gg.mark((b, i)))
            read(act, k, gg, (b, i))

        def f_act_layer(act, L):
            def norm_done():
                act.wait_ge(ff_loaded, L * 80 + 80)
                f_xn_act(act, 0)
            attn_act(act, "F", True, {6: lambda: d_square_act(act, "F1", 0, 3), 8: lambda: d_root_act(act, "F1", 0, 3), 10: norm_done})
            f_gelu_act(act, 0, 0)
            f_gelu_act(act, 0, 1)
            d_square_act(act, "F1", 1, 7)
            f_gelu_act(act, 0, 2)
            act.preload_act_table_set("natural_log_exp_and_others")
            d_root_act(act, "F1", 1, 7)
            f_xn_act(act, 1)
            for i in range(3):
                f_gelu_act(act, 1, i)
            act.preload_act_table_set("natural_log_exp_and_others")

        def f_act(act):
            for b in range(B):
                norm_act(act, "F0", b, b, None, 0)
            act.preload_act_table_set("natural_log_exp_and_others")
            with layers(act, "F") as L:
                f_act_layer(act, L)

        xsh = sb("xsh", [128, B, T])
        aside = sb("aside", [128, B, T])

        def shift_dve(dve, b, done):
            step(dve, dve_step, dve.tensor_copy(xsh[0:64, b, :], x[0:64, cols(b)]))
            dve.tensor_copy(xsh[64:128, b, 1:T], x[64:128, T * b:T * b + T - 1]).then_inc(*done)

        def f_shift_dve(dve, b):
            dve.wait_ge(*x_new.at(("F", b)))
            shift_dve(dve, b, shifted.mark(("F2", b)))
            dve.wait_ge(*shifted.at(("F2", b)))

        def f_centre_dve(dve, b, bank):
            dve.wait_ge(*full[bank].at(("F1", b, "mean")))
            dve.wait_ge(*k_raised.at(("F", 1, NP - 1)))
            dve.tensor_tensor(xc[:, b, :], xsh[:, b, :], ps[:, bank, :], ALU.subtract).then_inc(*centred.mark(("F1", b)))
            dve.wait_ge(*centred.at(("F1", b)))

        def f_dve_layer(dve, L):
            dve.wait_ge(fa_loaded, L * 48 + 48)
            for j in range(4):
                ins = dve.tensor_scalar(tab[:, j, :], tab0[:, j, :], scl[:, j:j + 1], None, ALU.mult)
            step(dve, dve_step, ins)
            attn_dve(dve, "F", True, {2: lambda: f_shift_dve(dve, 0), 5: lambda: f_centre_dve(dve, 0, 3), 9: lambda: d_scale_dve(dve, "F1", 0)})
            f_shift_dve(dve, 1)
            f_centre_dve(dve, 1, 7)
            dve.wait_ge(ff_loaded, L * 80 + 80)
            for b in range(B):
                for i, (c0, m) in enumerate(DIC):
                    k = up_bank[2 * i]
                    dve.wait_ge(*full[k].at(("F", b, "f", k)))
                    dve.wait_ge(*gg.at((b, i)))
                    if b == 1:
                        dve.wait_ge(*full[6].at(("F", 0, "f2")))
                    dve.scalar_tensor_tensor(fh[0:m, i, :], ps[0:m, k, :], b1[0:m, i:i + 1], fg[0:m, i, :], ALU.add, ALU.mult)\
                        .then_inc(*f_mul.mark((b, i)))
                    read(dve, k, f_mul, (b, i))
                if b == 0:
                    d_scale_dve(dve, "F1", 1)
                dve.wait_ge(*full[6].at(("F", b, "f2")))
                dve.scalar_tensor_tensor(x[:, cols(b)], ps[:, 6, :], lng[:, 2:3], x[:, cols(b)], ALU.add, ALU.add).then_inc(*x_new.mark(("Ff", b)))
                read(dve, 6, x_new, ("Ff", b))
                shift_dve(dve, b, (moved, 1))
            dve.sem_inc(f_used.mark("layer")[0], 1)

        def f_dve(dve):
            step(dve, dve_step, dve.memset(xsh[:, :, :], 0.0))
            step(dve, dve_step, dve.memset(P, 0.0))
            step(dve, dve_step, dve.memset(V2[0:WIN, 0, :], 0.0))
            for b in range(B):
                norm_dve(dve, "F0", b, b, x[:, cols(b)])
                dve.tensor_copy(aside[:, b, :], x[:, cols(b)]).then_inc(*x_new.mark(("aside", b)))
                dve.wait_ge(*x_new.at(("aside", b)))
                dve.wait_ge(*normed.at(("F0", b)))
                dve.tensor_copy(x[:, cols(b)], xn[:, b, :]).then_inc(*x_new.mark(("F0", b)))
                dve.wait_ge(*x_new.at(("F0", b)))
            for b in range(B):
                shift_dve(dve, b, (moved, 1))
            dve.wait_ge(f_const, 48)
            with layers(dve, "F") as L:
                f_dve_layer(dve, L)
            dve.wait_ge(moved, 2 * LAYERS + 2)
            for b in range(B):
                dve.wait_ge(*x_new.at(("Ff", b)))
                dve.tensor_tensor(x[:, cols(b)], x[:, cols(b)], aside[:, b, :], ALU.add).then_inc(*x_new.mark(("F_end", b)))

        def f_pool(pool):
            pool.wait_ge(*x_new.at(("D", 1)))
            step(pool, zeroed, pool.memset(QZ, 0.0))
            with layers(pool, "F") as L:
                attn_pool(pool, "F", True)

        def fa_weights(sp, l):
            for dst, name in ((Wqkv.rearrange("p a b -> p (a b)"), "F_w"), (scl, "F_scl"), (Wo.rearrange("p a b -> p (a b)"), "F_wo")):
                sp.dma_start(dst, A[name][bass.ds(l * 128, 128), :]).then_inc(fa_loaded, 16)

        def ff_weights(sp, l):
            for dst, name in ((W1, "F_w1"), (W2.rearrange("p a b -> p (a b)"), "F_w2"), (b1, "F_b1"), (lng[:, 0:2], "F_ln"), (lng[:, 2:3], "F_b2")):
                sp.dma_start(dst, A[name][bass.ds(l * 128, 128), :]).then_inc(ff_loaded, 16)

        def f_sp(sp):
            sp.wait_ge(*x_new.at(("E", 1)))
            for dst, name in ((tab0, "tabF"), (seg, "seg"), (spread, "spread")):
                sp.dma_start(dst, A[name]).then_inc(f_const, 16)
            fa_weights(sp, 0)
            ff_weights(sp, 0)
            with layers(sp, "F", LAYERS - 1) as L:
                v2_sp(sp, "F")
                sp.wait_ge(*x_new.at(("F", 1)))
                fa_weights(sp, L + 1)
                sp.wait_ge(*f_used.at("layer"))
                ff_weights(sp, L + 1)
            v2_sp(sp, "F")
        block = c.enter_context(nc.Block())

        first = ((x[:, :], "x"), (mean_m[:, :], "mean_m"), (eps5[:, :], "eps5"))
        second = ((ident[:, :], "ident"), (identb[:, :], "identb"), (band[:, :], "band"), (tab0, "tab0"), (Wqkv, "A_w"), (Wo, "A_wo"))
        third = ((ctxT, "ctx"), (Bw, "B_w"), (Bb, "B_b"), (Ew, "E_w"), (Eb, "E_b"), (hmask, "hmask"), (Cw, "C_w"), (tri, "tri"))

        @block.sync
        def _(sp):
            for parts, sem in ((first, first_in), (second, second_in), (third, third_in)):
                for dst, name in parts:
                    sp.dma_start(dst, A[name]).then_inc(sem, 16)
            v2_sp(sp, "A")
            d_sp(sp)
            f_sp(sp)
            sp.wait_ge(*x_new.at(("F_end", 1)))
            sp.dma_start(out, x[:, :]).then_inc(stored, 16)
            sp.wait_ge(stored, 16)

        @block.tensor
        def _(pe):
            pe.wait_ge(first_in, 16 * len(first))
            for b in range(B):
                norm_pe(pe, "A1", b, b, x[:, cols(b)])
            for b in range(B):
                norm_pe(pe, "A2", b, b, None, center=False)
            pe.wait_ge(second_in, 16 * len(second))
            attn_pe(pe, "A", lambda b: xn[:, b, :], False)
            pe.wait_ge(third_in, 16 * len(third))
            b_pe(pe)
            c_pe(pe)
            d_pe(pe)
            e_pe(pe, "D")
            f_pe(pe)

        @block.scalar
        def _(act):
            act.preload_act_table_set("natural_log_exp_and_others")
            act.wait_ge(first_in, 16 * len(first))
            for b in range(B):
                norm_act(act, "A1", b, b, None, 0)
            for b in range(B):
                norm_act(act, "A2", b, b, xn[:, b, :], 1, center=False, wait=(normed.at(("A1", b)),))
            attn_act(act, "A", False)
            act.wait_ge(third_in, 16 * len(third))
            b_act(act)
            c_act(act)
            d_act(act)
            act.wait_ge(*vv_one.at("ones"))
            e_act(act)
            f_act(act)

        @block.vector
        def _(dve):
            step(dve, dve_step, dve.memset(P, 0.0))
            step(dve, dve_step, dve.memset(V2[0:WIN, 0, :], 0.0))
            dve.wait_ge(first_in, 16 * len(first))
            for b in range(B):
                norm_dve(dve, "A1", b, b, x[:, cols(b)])
            for b in range(B):
                norm_dve(dve, "A2", b, b, xn[:, b, :], center=False)
            dve.wait_ge(second_in, 16 * len(second))
            attn_dve(dve, "A", False)
            dve.wait_ge(third_in, 16 * len(third))
            b_dve(dve)
            c_dve(dve)
            d_dve(dve)
            e_dve(dve)
            f_dve(dve)

        @block.gpsimd
        def _(pool):
            step(pool, zeroed, pool.memset(QZ, 0.0))
            attn_pool(pool, "A", False)
            f_pool(pool)
        assert all(taken[k].n == free[k].n for k in range(8))


def swapped(w):
    w = w.reshape(*w.shape[:-1], H, 2, D // 2)
    return w[..., ::-1, :].reshape(*w.shape[:-3], INNER)

def five(w):
    q, k, v = (w[..., i * INNER:(i + 1) * INNER] for i in range(3))
    import numpy as np
    return np.stack([q, k, v, swapped(q), swapped(k)], -2)


def more(a, f, np):
    w = lambda p: np.stack([f(p + n).T for n in ("Wq", "Wk", "Wv", "Wo")], 1)
    bb = lambda p: np.stack([f(p + n) for n in ("bq", "bk", "bv", "bo")], 1)
    a["ctx"] = f("ctx_1024").transpose(2, 0, 1)
    a["B_w"], a["B_b"] = w("L0_xattn_"), bb("L0_xattn_")
    a["E_w"], a["E_b"] = w("L1_xattn_"), bb("L1_xattn_")
    a["hmask"] = (np.arange(128)[:, None] // DS == np.arange(HS)[None, :]).astype(np.float32)
    cw = np.zeros((128, 70 * FB), np.float32)
    for j, n in enumerate(("gate", "up")):
        for ch in range(3):
            part = f("L0_ffn_w_" + n)[128 * ch:128 * ch + 128]
            cw[:len(part), 384 * j + 128 * ch:384 * j + 128 * ch + 128] = part
    cw[:, 768:] = f("L0_ffn_w_down")
    a["C_w"] = cw.reshape(128, 70, FB)
    i = np.arange(128)
    a["tri"] = (i[:, None] <= i[None, :]).astype(np.float32)
    lay = lambda name: f("L1_attn_" + name)
    rows = lambda v: v.reshape(-1, v.shape[-1])
    L = LAYERS
    a["D_w"] = rows(np.stack([lay(n) for n in ("Wq", "Wk", "Wv", "Wo")], 2).reshape(L, 128, 512))
    a["D_qk"] = rows(np.stack([lay(n) for n in ("bq", "bk")], 2))
    a["D_b"] = rows(np.concatenate([np.stack([lay(n) for n in ("bo", "g1", "be1", "g2", "be2", "bf2")], 2),
                                    lay("bf1").reshape(L, 4, 128).transpose(0, 2, 1)], 2))
    a["D_bv"] = np.repeat(lay("bv"), 128, 0)
    a["D_om"] = rows(np.tile(lay("omega"), (1, HS, 1)))
    a["D_w1"] = rows(lay("W1"))
    a["D_w2"] = rows(lay("W2").reshape(L, 4, 128, 128).transpose(0, 2, 1, 3).reshape(L, 128, 512))
    slot = np.arange(HS * FS)[None, :]
    same = np.arange(128)[:, None] // DS == slot // FS
    a["OmS"] = (same * np.where(slot % FS < DS, 1.0, -1.0)).astype(np.float32)
    a["Bn"] = (same * -0.5).astype(np.float32)
    a["own"] = np.ascontiguousarray((np.arange(2 * 128).reshape(2, 128)[:, :, None] // FS == np.arange(C) // DS)
                                    .transpose(1, 0, 2).reshape(128, 2 * C)).astype(np.float32)
    g = lambda name: f("L1_ffn_" + name)
    a["F_w"] = rows(five(g("Wqkv")).reshape(L, 128, 5 * INNER))
    a["F_wo"] = rows(g("Wo").reshape(L, NP, 128, C).transpose(0, 2, 1, 3).reshape(L, 128, NP * C))
    sw = lambda v: np.concatenate([v[:, D // 2:], v[:, :D // 2]], 1)
    qs_, ks_ = g("q_scale"), g("k_scale")
    a["F_scl"] = rows(np.stack([np.tile(v, (1, 2)) for v in (qs_, sw(qs_), ks_, sw(ks_))], 2))
    a["F_w1"] = rows(g("W1"))

    def parts(v):
        z = np.zeros((L, 3 * 128, v.shape[2]), np.float32)
        z[:, :DI] = v
        return z.reshape(L, 3, 128, -1).transpose(0, 2, 1, 3)
    a["F_w2"] = rows(parts(g("W2")).reshape(L, 128, 3 * C))
    a["F_b1"] = rows(np.concatenate([parts(g("b1")[:, :DI, None])[..., 0], parts(g("b1")[:, DI:, None])[..., 0]], 2))
    a["F_ln"] = rows(np.stack([g("ln_g"), g("ln_b")], 2))
    a["F_b2"] = rows(g("b2")[:, :, None])
    seg = (i[:, None] // D == np.arange(2)[None, :]).astype(np.float32)
    spread = (i[:, None] // D == i[None, :] // D).astype(np.float32)
    a["seg"], a["spread"] = seg, spread



def kernel(**inp):
    import numpy as np
    import concourse.bacc as bacc
    from concourse.bass_utils import run_bass_kernel_spmd as run

    f = lambda name: np.asarray(inp[name])
    a = {}
    a["x"] = f("x").reshape(N, C).T
    a["mean_m"] = np.full((128, 128), 1 / 128, np.float32)
    a["ident"] = np.eye(128, dtype=np.float32)
    import ml_dtypes
    a["identb"] = np.eye(128).astype(ml_dtypes.bfloat16)
    q, k = np.arange(128)[:, None] % 64, np.arange(64 + WIN)[None, :]
    see = (k >= q) & (k <= q + WIN)
    see = np.concatenate([see & (k >= WIN)] + [see] * 4, 1)
    a["band"] = np.where(see, 0.0, NEG).astype(ml_dtypes.bfloat16)
    e = np.zeros((128, 6), np.float32)
    e[:, 0:4] = [1e-5, 1e-6, math.log(0.25), 10 * math.log(2)]
    odd = np.arange(128) // FS % 2
    for p_ in range(2):
        e[:, 4 + p_] = np.where(odd == p_, math.log(0.25), NEG)
    a["eps5"] = e
    half = np.arange(0, D, 2, dtype=np.float32)
    freqs = np.arange(T, dtype=np.float32)[:, None] * (1.0 / 10000.0 ** (half / D)).astype(np.float32)[None, :]
    cos, sin = np.cos(freqs).T, np.sin(freqs).T
    cos2 = np.concatenate([cos] * 4, 0)
    sin2 = np.concatenate([-sin, sin] * 2, 0)
    a["tab0"] = np.stack([cos2, sin2, cos2, sin2], 1).astype(np.float32)
    base = (half + 0.4 * D) / (1.4 * D)
    power = (np.arange(T, dtype=np.float32) - T // 2) / (WIN // 2)
    sc = (base[:, None] ** power[None, :]).astype(np.float32)
    sc = np.concatenate([sc] * 4, 0)
    a["tabF"] = np.stack([cos2 * sc, sin2 * sc, cos2 / sc, sin2 / sc], 1).astype(np.float32)

    a["A_w"] = five(f("L0_attn_w_qkv").T)
    a["A_wo"] = f("L0_attn_w_out").T.reshape(NP, 128, C).transpose(1, 0, 2)
    more(a, f, np)
    a = {k: np.ascontiguousarray(v) for k, v in a.items()}
    book = {}
    for turn in range(2):
        nc = bacc.Bacc("TRN2", target_bir_lowering=False, num_devices=1)
        A = {k: nc.dram_tensor(f"in_{k}", v.shape, mybir.dt.from_np(v.dtype), kind="ExternalInput").ap() for k, v in a.items()}
        out = nc.dram_tensor("out_x", (128, N), F32, kind="ExternalOutput").ap()
        build(nc, A, out, book)
    r = run(nc, [{f"in_{k}": v for k, v in a.items()}], core_ids=[0])
    return np.ascontiguousarray(r.results[0]["out_x"].T).reshape(B, T, C)
```
